# Optimizing a Trainium2 kernel written in Bass

```python
import numpy as np
import jax
import jax.numpy as jnp

def _softmax(x, axis=-1):
    return jax.nn.softmax(x, axis=axis)

def _gelu(x):
    return jax.nn.gelu(x, approximate=True)

def _silu(x):
    return jax.nn.silu(x)

def _sigmoid(x):
    return jax.nn.sigmoid(x)

def _layernorm(x, axis=-1, eps=1e-05):
    m = jnp.mean(x, axis=axis, keepdims=True)
    v = jnp.var(x, axis=axis, keepdims=True)
    return (x - m) / jnp.sqrt(v + eps)

def _scatter_add(tgt, idx, src, axis=0):
    return tgt.at[idx].add(src)

def _segment_sum(src, seg, n):
    return jax.ops.segment_sum(src, seg, n)
kernel_name = 'mk_decoder_preln_d1_seqx_r8_bdc320'

def setup_inputs(seed: int=0):
    np.random.seed(seed)
    _w = jnp.asarray

    def _rec_inputs():
        import jax
        import jax.numpy as jnp
        _rk = jax.random.key(seed)
        x = -0.0002928 + 1 * jax.random.normal(jax.random.fold_in(_rk, 1), (16, 256, 128), jnp.float32)
        _lenS = 256 - jax.random.randint(jax.random.fold_in(_rk, 7), (16,), 0, max(1, 256 // 4) + 1, jnp.int32)
        _lenS2 = 64 - jax.random.randint(jax.random.fold_in(_rk, 8), (16,), 0, max(1, 64 // 4) + 1, jnp.int32)
        _ctx_1024P = jax.random.normal(jax.random.fold_in(_rk, 11), (16, 16, 128), jnp.float32)
        _ctx_1024c = jax.random.dirichlet(jax.random.fold_in(_rk, 511), 0.3 * jnp.ones((16,), jnp.float32), (16, 64))
        _ctx_1024t = jnp.einsum('bsk,bkd->bsd', _ctx_1024c, _ctx_1024P)
        _ctx_1024t = _ctx_1024t * jax.lax.rsqrt(jnp.mean(jnp.square(_ctx_1024t)) + 1e-12) * 0.953939
        ctx_1024 = 0.000227908 + 0.99994 * (_ctx_1024t + 0.3 * jax.random.normal(jax.random.fold_in(_rk, 611), (16, 64, 128), jnp.float32))
        return (x, ctx_1024)
    x, ctx_1024 = _rec_inputs()

    def _L0_attn_setup():
        import jax, jax.numpy as jnp
        import numpy as np
        H, D, CR, SEL_K = (8, 64, 32, 16)
        ROPE_DIM, THETA, WINDOW, GROUPS = (32, 10000.0, 64, 2)
        INTER, HID, QC = (64, 128, 32)
        NEG = -1e+30

        def _rope_cache(t):
            half = ROPE_DIM // 2
            inv = 1.0 / THETA ** (jnp.arange(half, dtype=jnp.float32) * 2.0 / ROPE_DIM)
            ang = jnp.arange(t, dtype=jnp.float32)[:, None] * inv[None, :]
            return (jnp.cos(ang), jnp.sin(ang))

        def _apply_partial_rope(x, cos, sin):
            half = ROPE_DIM // 2
            x1, x2, rest = (x[..., :half], x[..., half:ROPE_DIM], x[..., ROPE_DIM:])
            return jnp.concatenate([x1 * cos - x2 * sin, x1 * sin + x2 * cos, rest], -1)

        def _rmsnorm(x, g, eps=1e-06):
            return x * jax.lax.rsqrt(jnp.mean(x * x, -1, keepdims=True) + eps) * g
        key = jax.random.key(seed)
        ks = jax.random.split(key, 9)
        f = lambda k, shp, s: jax.random.normal(k, shp, jnp.float32) * s
        return {'h': f(ks[0], (1, 256, HID), 1.0), 'w_qc': f(ks[1], (HID, QC), QC ** (-0.5)), 'w_qup': f(ks[2], (QC, H * D), (H * D) ** (-0.5)), 'w_k': f(ks[3], (HID, D), HID ** (-0.5)), 'w_v': f(ks[4], (HID, D), HID ** (-0.5)), 'g_qnorm': jnp.ones((D,), jnp.float32), 'g_knorm': jnp.ones((D,), jnp.float32), 'w_gate': f(ks[5], (D, 3), 0.05), 'b_gate': jnp.zeros((3,), jnp.float32), 'sink_logit': f(ks[6], (H,), 0.1), 'w_out_group': f(ks[7], (GROUPS, H // GROUPS * D, INTER), 0.05), 'w_out': f(ks[8], (GROUPS * INTER, HID), 0.03)}
    _L0_attn_all = _L0_attn_setup()
    _L0_attn_in = {k: v for k, v in _L0_attn_all.items() if k in ('w_qc', 'w_qup', 'w_k', 'w_v', 'g_qnorm', 'g_knorm', 'w_gate', 'b_gate', 'sink_logit', 'w_out_group', 'w_out')}
    del _L0_attn_all

    def _L0_xattn_setup():
        import jax, jax.numpy as jnp
        import numpy as np
        HEADS = 16
        key = jax.random.key(seed)
        ks = jax.random.split(key, 6)
        b, n, m, dim = (2, 256, 64, 128)
        s = dim ** (-0.5)
        return {'x': jax.random.normal(ks[0], (b, n, dim), jnp.float32), 'mem': jax.random.normal(ks[1], (b, m, dim), jnp.float32), 'Wq': jax.random.normal(ks[2], (dim, dim), jnp.float32) * s, 'Wkv': jax.random.normal(ks[3], (dim, 2 * dim), jnp.float32) * s, 'Wout': jax.random.normal(ks[4], (dim, dim), jnp.float32) * s, 'bout': jnp.zeros((dim,), jnp.float32)}
    _L0_xattn_all = _L0_xattn_setup()
    _L0_xattn_in = {k: v for k, v in _L0_xattn_all.items() if k in ('Wq', 'Wkv', 'Wout', 'bout')}
    del _L0_xattn_all

    def _L0_ffn_setup():
        import jax, jax.numpy as jnp
        import numpy as np
        B, S, F, E, K = (4, 128, 128, 8, 2)
        H = 4 * F
        key = jax.random.key(seed)
        ks = jax.random.split(key, 7)

        def xavier(k, shape):
            fan_in, fan_out = (shape[-2], shape[-1])
            scale = jnp.sqrt(6.0 / (fan_in + fan_out))
            return jax.random.uniform(k, shape, jnp.float32, -scale, scale)
        return {'x': jax.random.normal(ks[0], (B, S, F), jnp.float32), 'Wg': xavier(ks[1], (F, E)), 'bg': jnp.zeros((E,), jnp.float32), 'W1': xavier(ks[2], (E, F, H)), 'b1': jnp.zeros((E, H), jnp.float32), 'W2': xavier(ks[3], (E, H, F)), 'b2': jnp.zeros((E, F), jnp.float32)}
    _L0_ffn_all = _L0_ffn_setup()
    _L0_ffn_in = {k: v for k, v in _L0_ffn_all.items() if k in ('Wg', 'bg', 'W1', 'b1', 'W2', 'b2')}
    del _L0_ffn_all
    return {'x': x, 'ctx_1024': ctx_1024, 'L0_attn_w_qc': _L0_attn_in['w_qc'], 'L0_attn_w_qup': _L0_attn_in['w_qup'], 'L0_attn_w_k': _L0_attn_in['w_k'], 'L0_attn_w_v': _L0_attn_in['w_v'], 'L0_attn_g_qnorm': _L0_attn_in['g_qnorm'], 'L0_attn_g_knorm': _L0_attn_in['g_knorm'], 'L0_attn_w_gate': _L0_attn_in['w_gate'], 'L0_attn_b_gate': _L0_attn_in['b_gate'], 'L0_attn_sink_logit': _L0_attn_in['sink_logit'], 'L0_attn_w_out_group': _L0_attn_in['w_out_group'], 'L0_attn_w_out': _L0_attn_in['w_out'], 'L0_xattn_Wq': _L0_xattn_in['Wq'], 'L0_xattn_Wkv': _L0_xattn_in['Wkv'], 'L0_xattn_Wout': _L0_xattn_in['Wout'], 'L0_xattn_bout': _L0_xattn_in['bout'], 'L0_ffn_Wg': _L0_ffn_in['Wg'], 'L0_ffn_bg': _L0_ffn_in['bg'], 'L0_ffn_W1': _L0_ffn_in['W1'], 'L0_ffn_b1': _L0_ffn_in['b1'], 'L0_ffn_W2': _L0_ffn_in['W2'], 'L0_ffn_b2': _L0_ffn_in['b2']}

def reference(x, ctx_1024, L0_attn_w_qc, L0_attn_w_qup, L0_attn_w_k, L0_attn_w_v, L0_attn_g_qnorm, L0_attn_g_knorm, L0_attn_w_gate, L0_attn_b_gate, L0_attn_sink_logit, L0_attn_w_out_group, L0_attn_w_out, L0_xattn_Wq, L0_xattn_Wkv, L0_xattn_Wout, L0_xattn_bout, L0_ffn_Wg, L0_ffn_bg, L0_ffn_W1, L0_ffn_b1, L0_ffn_W2, L0_ffn_b2):
    import jax
    import jax.numpy as jnp

    def _L0_attn_ref(h, w_qc, w_qup, w_k, w_v, g_qnorm, g_knorm, w_gate, b_gate, sink_logit, w_out_group, w_out):
        import jax, jax.numpy as jnp
        import numpy as np
        H, D, CR, SEL_K = (8, 64, 32, 16)
        ROPE_DIM, THETA, WINDOW, GROUPS = (32, 10000.0, 64, 2)
        INTER, HID, QC = (64, 128, 32)
        NEG = -1e+30

        def _rope_cache(t):
            half = ROPE_DIM // 2
            inv = 1.0 / THETA ** (jnp.arange(half, dtype=jnp.float32) * 2.0 / ROPE_DIM)
            ang = jnp.arange(t, dtype=jnp.float32)[:, None] * inv[None, :]
            return (jnp.cos(ang), jnp.sin(ang))

        def _apply_partial_rope(x, cos, sin):
            half = ROPE_DIM // 2
            x1, x2, rest = (x[..., :half], x[..., half:ROPE_DIM], x[..., ROPE_DIM:])
            return jnp.concatenate([x1 * cos - x2 * sin, x1 * sin + x2 * cos, rest], -1)

        def _rmsnorm(x, g, eps=1e-06):
            return x * jax.lax.rsqrt(jnp.mean(x * x, -1, keepdims=True) + eps) * g
        b, t, _ = h.shape
        cos, sin = _rope_cache(t)
        q = (h @ w_qc @ w_qup).reshape(b, t, H, D).transpose(0, 2, 1, 3)
        q = _rmsnorm(_apply_partial_rope(q, cos, sin), g_qnorm)
        k = _rmsnorm(_apply_partial_rope(h @ w_k, cos, sin), g_knorm)
        v = h @ w_v
        scale = 1.0 / np.sqrt(D).astype(np.float32)
        qpos = jnp.arange(t)
        sink = jnp.broadcast_to(sink_logit[None, :, None, None], (b, H, t, 1))
        nb = t // CR
        kc = k[:, :nb * CR].reshape(b, nb, CR, D).mean(2)
        vc = v[:, :nb * CR].reshape(b, nb, CR, D).mean(2)
        comp_valid = ((jnp.arange(nb) + 1) * CR - 1)[None, :] <= qpos[:, None]
        any_blk = comp_valid.any(-1, keepdims=True)
        safe = jnp.where(any_blk, comp_valid, True)
        sc_raw = jnp.einsum('bhqd,bnd->bhqn', q, kc) * scale
        pc = jax.nn.softmax(jnp.concatenate([jnp.where(safe, sc_raw, NEG), sink], -1), -1)
        comp_out = jnp.einsum('bhqn,bnd->bhqd', pc[..., :nb], vc)
        comp_out = jnp.where(any_blk[None, None], comp_out, 0.0)
        sel_sc = jnp.where(comp_valid, sc_raw, -jnp.inf)
        top_idx = jax.lax.top_k(sel_sc, min(SEL_K, nb))[1]
        sel_blocks = (top_idx[..., :, None] == jnp.arange(nb)).any(-2)
        block_of = jnp.minimum(qpos // CR, nb - 1)
        causal = qpos[:, None] >= qpos[None, :]
        in_range = qpos < nb * CR
        tok_sel = sel_blocks[..., block_of] & (causal & in_range[None, :])[None, None]
        scores_full = jnp.einsum('bhqd,bkd->bhqk', q, k) * scale
        ps = jax.nn.softmax(jnp.where(tok_sel, scores_full, NEG), -1)
        sel_out = jnp.einsum('bhqk,bkd->bhqd', ps, v)
        sw = causal & (qpos[:, None] - qpos[None, :] < WINDOW)
        pw = jax.nn.softmax(jnp.concatenate([jnp.where(sw[None, None], scores_full, NEG), sink], -1), -1)
        sw_out = jnp.einsum('bhqk,bkd->bhqd', pw[..., :t], v)
        g = jax.nn.sigmoid(q @ w_gate + b_gate)
        g = g / jnp.clip(g.sum(-1, keepdims=True), 1e-06)
        mixed = g[..., 0:1] * comp_out + g[..., 1:2] * sel_out + g[..., 2:3] * sw_out
        x = mixed.transpose(0, 2, 1, 3).reshape(b, t, GROUPS, H // GROUPS * D)
        y = jnp.einsum('btgf,gfi->btgi', x, w_out_group).reshape(b, t, GROUPS * INTER)
        return y @ w_out

    def _L0_xattn_ref(x, mem, Wq, Wkv, Wout, bout):
        import jax, jax.numpy as jnp
        import numpy as np
        HEADS = 16
        b, n, dim = x.shape
        h = HEADS
        d = dim // h
        scale = d ** (-0.5)
        mem_len = mem.shape[1]
        q = x @ Wq
        xc = jnp.concatenate((mem, x), axis=1)
        kv = xc @ Wkv
        k, v = jnp.split(kv, 2, axis=-1)

        def to_heads(t):
            bb, nn, _ = t.shape
            return t.reshape(bb, nn, h, d).transpose(0, 2, 1, 3)
        q, k, v = (to_heads(q), to_heads(k), to_heads(v))
        dots = jnp.einsum('bhid,bhjd->bhij', q, k) * scale
        j = dots.shape[-1]
        i_idx = jnp.arange(n)[:, None]
        j_idx = jnp.arange(j)[None, :]
        mask = j_idx > i_idx + mem_len
        dots = jnp.where(mask[None, None], -jnp.inf, dots)
        attn = jax.nn.softmax(dots, axis=-1)
        out = jnp.einsum('bhij,bhjd->bhid', attn, v)
        out = out.transpose(0, 2, 1, 3).reshape(b, n, dim)
        return out @ Wout + bout

    def _L0_ffn_ref(x, Wg, bg, W1, b1, W2, b2):
        import jax, jax.numpy as jnp
        import numpy as np
        B, S, F, E, K = (4, 128, 128, 8, 2)
        H = 4 * F
        gate_probs = jax.nn.softmax(x @ Wg + bg, axis=-1)
        k = K
        _, top_idx = jax.lax.top_k(gate_probs, k)
        expert_mask = jax.nn.one_hot(top_idx, gate_probs.shape[-1], dtype=gate_probs.dtype).sum(-2)
        selected = gate_probs * expert_mask
        selected = selected / (selected.sum(-1, keepdims=True) + 1e-08)
        h = jax.nn.gelu(jnp.einsum('bsf,efh->bseh', x, W1) + b1)
        expert_out = jnp.einsum('bseh,ehf->bsef', h, W2) + b2[None, None]
        return jnp.einsum('bsef,bse->bsf', expert_out, selected)
    x = x + _L0_attn_ref(_layernorm(x, axis=-1), L0_attn_w_qc, L0_attn_w_qup, L0_attn_w_k, L0_attn_w_v, L0_attn_g_qnorm, L0_attn_g_knorm, L0_attn_w_gate, L0_attn_b_gate, L0_attn_sink_logit, L0_attn_w_out_group, L0_attn_w_out)
    x = x + _L0_xattn_ref(_layernorm(x, axis=-1), ctx_1024, L0_xattn_Wq, L0_xattn_Wkv, L0_xattn_Wout, L0_xattn_bout)
    x = x + _L0_ffn_ref(_layernorm(x, axis=-1), L0_ffn_Wg, L0_ffn_bg, L0_ffn_W1, L0_ffn_b1, L0_ffn_W2, L0_ffn_b2)
    return x

_drawn_inputs = setup_inputs


def setup_inputs(seed=0):
    import zlib

    import numpy as np

    out = dict(_drawn_inputs(seed))
    spreads = {'L0_attn_g_qnorm': (1.0, 0.6),
     'L0_attn_g_knorm': (1.0, 0.6),
     'L0_attn_b_gate': (0.0, 2.0),
     'L0_xattn_bout': (0.0, 0.1),
     'L0_ffn_bg': (0.0, 0.1),
     'L0_ffn_b1': (0.0, 0.1),
     'L0_ffn_b2': (0.0, 0.1)}
    factors = {'L0_attn_w_gate': 4.808, 'L0_attn_sink_logit': 44.474}
    for name, (base, spread) in spreads.items():
        noise = np.random.default_rng([zlib.crc32(name.encode()), seed]).standard_normal(out[name].shape)
        drawn = base * np.exp(spread * noise) if base else spread * noise
        out[name] = jnp.asarray(drawn.astype(out[name].dtype))
    for name, factor in factors.items():
        out[name] = (out[name] * factor).astype(out[name].dtype)
    return out
```

```python
from contextlib import ExitStack

import concourse.bass as bass
from concourse import mybir

F32 = mybir.dt.float32
F16 = mybir.dt.float16
BF16 = mybir.dt.bfloat16
U32 = mybir.dt.uint32
ALU = mybir.AluOpType
ACT = mybir.ActivationFunctionType
AX = mybir.AxisListType

P = 128
NEG = -1e30
WS = 64.0
CLAMP = 60000.0


class Count:

    def __init__(self, sem, per, credit=0):
        self.sem, self.per, self.credit = sem, per, credit

    def value(self, rounds, k):
        return rounds * self.per + (k + self.credit)


class Steps:

    def __init__(self, eng, count):
        self.eng, self.count, self.rounds, self.k = eng, count, 0, 0

    def start(self, rounds):
        self.rounds, self.k = rounds, 0

    def done(self, ins):
        self.k += 1
        ins.then_inc(self.count.sem, 1)
        self.eng.wait_ge(self.count.sem, self.count.value(self.rounds, self.k))

    def carry(self, spare):
        self.eng.tensor_copy(spare[:, 1:2], spare[:, 0:1])

    def finish(self):
        assert self.k == self.count.per, f"{self.k} steps in a round, not {self.count.per}"


def bc(ap, axis, n):
    ap = ap.unsqueeze(axis)
    shape = list(ap.shape)
    shape[axis] = n
    return ap.broadcast_to(shape)


class Experts:

    TOK = 512
    T = TOK // P
    LEAD = 2
    HB = 4
    DVE_STEPS = 20

    def __init__(self, k):
        self.k = k
        sb, sem = k.sb, k.sem
        self.E, self.F, self.H = k.E, P, k.W1.shape[2]
        self.C = self.H // P
        self.J = self.E * self.C
        self.G = k.tiles // self.T
        self.xn = sb("f_xn", [P, self.T, P], F32)
        self.x32 = sb("f_x32", [P, self.TOK], F32)
        self.xhi = sb("f_xhi", [P, 2, self.TOK], F16)
        self.xlo = sb("f_xlo", [P, 2, self.TOK], F16)
        self.stats = sb("f_stats", [P, self.T, 6], F32)
        self.mv = sb("f_mv", [P, self.T, 2], F32)
        self.ve = sb("f_ve", [P, self.T], F32)
        self.rstd = sb("f_rstd", [P, self.T], F32)
        E, T = self.E, self.T
        self.lg = sb("f_lg", [P, T, E], F32)
        self.mx = sb("f_mx", [P, T], F32)
        self.ex = sb("f_ex", [P, T, E], F32)
        self.z = sb("f_z", [P, T], F32)
        self.zr = sb("f_zr", [P, T], F32)
        self.pr = sb("f_pr", [P, T, E], F32)
        self.top = sb("f_top", [P, T, 8], F32)
        self.topi = sb("f_topi", [P, T, 8], U32)
        self.topf = sb("f_topf", [P, T, 8], F32)
        self.m1 = sb("f_m1", [P, T, E], F32)
        self.m2 = sb("f_m2", [P, T, E], F32)
        self.gs = sb("f_gs", [P, T, E], F32)
        self.gp = k.gp
        self.gT = sb("f_gT", [32, 2, self.TOK], BF16)
        self.Gb = sb("f_Gb", [P, 2, E, self.TOK], F32)
        self.h32 = sb("f_h32", [P, 2, self.TOK], F32)
        self.hhi = sb("f_hhi", [P, self.HB, self.TOK], F16)
        self.hlo = sb("f_hlo", [P, self.HB, self.TOK], F16)
        self.acc = sb("f_acc", [P, self.TOK], F32)
        self.tmp = sb("f_tmp", [P, self.TOK], F32)
        self.ost = sb("f_ost", [P, 2, T, P], F32)
        S = lambda name, per, credit=0: Count(sem("f_" + name), per, credit)
        self.h_ready = S("h_ready", self.J)
        self.gelu_done = S("gelu_done", self.J, self.HB)
        self.lo_done = S("lo_done", self.J, 2)
        self.h_used = S("h_used", self.J, self.HB)
        self.o_used = S("o_used", E, 2)
        self.acc_ready = S("acc_ready", 1)
        self.out_ready = S("out_ready", 1)
        self.out_sum = S("out_sum", 1, 1)
        self.stored = [S(f"stored{i}", 16, 16) for i in range(2)]
        self.ve_ready = S("ve_ready", 1)
        self.rstd_ready = S("rstd_ready", 1)
        self.xn_ready = S("xn_ready", 1)
        self.xT_ready = S("xT_ready", 1)
        self.xhi_ready = S("xhi_ready", 1)
        self.xlo_ready = S("xlo_ready", 1)
        self.lg_ready = S("lg_ready", 1)
        self.shift_ready = S("shift_ready", 1)
        self.ex_ready = S("ex_ready", 1)
        self.gp_ready = S("gp_ready", 1)
        self.gpT_ready = S("gpT_ready", 1)
        self.gT_ready = S("gT_ready", 1)
        self.Gps_ready = S("Gps_ready", E)
        self.Gb_ready = S("Gb_ready", E, 1)
        self.steps = S("dve_steps", self.DVE_STEPS)
        self.M0, self.M1 = k.ps[:, 6, :], k.ps[:, 7, :]

    def h_bank(self, j):
        return self.k.ps[:, j % self.HB, :]

    def o_bank(self, e):
        return self.k.ps[:, 4 + e % 2, :]

    def credits(self, eng):
        for s in (self.gelu_done, self.lo_done, self.h_used, self.o_used, self.out_sum, self.Gb_ready,
                  *self.stored):
            eng.sem_inc(s.sem, s.credit)

    def pe_prep(self, pe, n, par, j):
        k = self.k
        if j == 4:
            pe.wait_ge(self.xn_ready.sem, self.xn_ready.value(n, 1))
            pe.wait_ge(self.Gb_ready.sem, self.Gb_ready.value(n, 0))
            for i in range(self.T):
                last = pe.transpose(self.M0[:, i * P:(i + 1) * P], self.xn[:, i, :], k.identF[:, :])
            last.then_inc(self.xT_ready.sem, 1)
        if j == 7:
            pe.wait_ge(self.xlo_ready.sem, self.xlo_ready.value(n, 1))
            for i in range(self.T):
                last = pe.matmul(self.M0[:, i * self.E:(i + 1) * self.E], self.x32[:, i * P:(i + 1) * P],
                                 k.Wg_sb[:, :], start=True, stop=True)
            last.then_inc(self.lg_ready.sem, 1)
        if j == 18:
            pe.wait_ge(self.gp_ready.sem, self.gp_ready.value(n, 1))
            for i in range(self.T):
                last = pe.transpose(self.M0[0:32, :].bitcast(BF16)[:, i * P:(i + 1) * P], self.gp[:, i, :],
                                    k.identB[:, :])
            last.then_inc(self.gpT_ready.sem, 1)
        if 20 <= j < 20 + self.E:
            e = j - 20
            if e == 0:
                pe.wait_ge(self.gT_ready.sem, self.gT_ready.value(n, 1))
            else:
                pe.wait_ge(self.Gb_ready.sem, self.Gb_ready.value(n, e))
            pe.matmul(self.M0, k.pick[:, e, :], self.gT[:, par, :], start=True,
                      stop=True).then_inc(self.Gps_ready.sem, 1)

    def pe_first(self, pe, g, par, j):
        k, e, c = self.k, j // self.C, j % self.C
        w = slice(c * P, (c + 1) * P)
        if j == 0:
            pe.wait_ge(self.xlo_ready.sem, self.xlo_ready.value(g, 1))
        pe.wait_ge(self.gelu_done.sem, self.gelu_done.value(g, j - self.HB + 1))
        H = self.h_bank(j)
        pe.matmul(H, k.W1hi[:, e, w], self.xhi[:, par, :], start=True, stop=False)
        pe.matmul(H, k.W1hi[:, e, w], self.xlo[:, par, :], start=False, stop=False)
        pe.matmul(H, k.W1lo[:, e, w], self.xhi[:, par, :], start=False, stop=True)\
            .then_inc(self.h_ready.sem, 1)

    def pe_second(self, pe, g, j):
        k, e, c = self.k, j // self.C, j % self.C
        if c == 0:
            pe.wait_ge(self.o_used.sem, self.o_used.value(g, e - 1))
        pe.wait_ge(self.gelu_done.sem, self.gelu_done.value(g, j + 1))
        O, b = self.o_bank(e), j % self.HB
        pe.matmul(O, k.W2hi[:, e, c, :], self.hhi[:, b, :], start=(c == 0), stop=False)
        pe.matmul(O, k.W2lo[:, e, c, :], self.hhi[:, b, :], start=False, stop=False)
        pe.wait_ge(self.lo_done.sem, self.lo_done.value(g, j + 1))
        last = pe.matmul(O, k.W2hi[:, e, c, :], self.hlo[:, b, :], start=False, stop=(c == self.C - 1))
        last.then_inc(self.h_used.sem, 1)

    def tensor(self, pe):
        k = self.k
        for j in range(self.J):
            self.pe_prep(pe, 0, 0, j)
        for j in range(self.LEAD):
            self.pe_first(pe, 0, 0, j)
        with pe.Fori(0, self.G // 2) as i:
            for par in range(2):
                g = i * 2 + par
                for j in range(self.J):
                    self.pe_prep(pe, g + 1, 1 - par, j)
                    if j + self.LEAD < self.J:
                        self.pe_first(pe, g, par, j + self.LEAD)
                    else:
                        self.pe_first(pe, g + 1, 1 - par, j + self.LEAD - self.J)
                    self.pe_second(pe, g, j)
                pe.wait_ge(self.out_sum.sem, self.out_sum.value(g, 0))
                for t in range(self.T):
                    for m in range(3):
                        pe.matmul(self.M1[:, t * P:(t + 1) * P], self.gT[:, par, t * P:(t + 1) * P],
                                  k.b2parts[:, m, :], start=(t == 0 and m == 0), stop=False,
                                  skip_group_check=True)
                pe.wait_ge(self.acc_ready.sem, self.acc_ready.value(g, 1))
                for t in range(self.T):
                    last = pe.matmul(self.M1[:, t * P:(t + 1) * P], self.acc[:, t * P:(t + 1) * P],
                                     k.identF[:, :], start=False, stop=True, skip_group_check=True)
                last.then_inc(self.out_ready.sem, 1)

    def act_prep(self, act, n, par, j):
        if j == 5:
            act.wait_ge(self.xT_ready.sem, self.xT_ready.value(n, 1))
            act.copy(self.xhi[:, par, :], self.M0)
            act.copy(self.x32[:, :], self.M0).then_inc(self.xhi_ready.sem, 1)
        if j == 19:
            act.wait_ge(self.gpT_ready.sem, self.gpT_ready.value(n, 1))
            act.copy(self.gT[:, par, :], self.M0[0:32, :].bitcast(BF16)[:, 0:self.TOK])\
                .then_inc(self.gT_ready.sem, 1)
        if 20 <= j < 20 + self.E:
            e = j - 20
            act.wait_ge(self.Gps_ready.sem, self.Gps_ready.value(n, e + 1))
            act.copy(self.Gb[:, par, e, :], self.M0).then_inc(self.Gb_ready.sem, 1)

    def scalar(self, act):
        k = self.k
        for j in range(self.J):
            self.act_prep(act, 0, 0, j)
        with act.Fori(0, self.G // 2) as i:
            for par in range(2):
                g = i * 2 + par
                for j in range(self.J):
                    act.wait_ge(self.h_ready.sem, self.h_ready.value(g, j + 1))
                    act.wait_ge(self.lo_done.sem, self.lo_done.value(g, j - 1))
                    act.activation(self.h32[:, j % 2, :], self.h_bank(j), ACT.Gelu_apprx_tanh,
                                   bias=k.b1_sb[:, j:j + 1], scale=1.0 / WS)
                    act.wait_ge(self.h_used.sem, self.h_used.value(g, j - self.HB + 1))
                    act.activation(self.hhi[:, j % self.HB, :], self.h_bank(j), ACT.Gelu_apprx_tanh,
                                   bias=k.b1_sb[:, j:j + 1], scale=1.0 / WS)\
                        .then_inc(self.gelu_done.sem, 1)
                    self.act_prep(act, g + 1, 1 - par, j)

    def gpsimd(self, pool):
        k = self.k
        with pool.Fori(0, self.G + 1) as n:
            pool.wait_ge(self.ve_ready.sem, self.ve_ready.value(n, 1))
            pool.tensor_tensor(self.rstd[:, :], self.ve[:, :], k.minus_half[:, 0:self.T], ALU.pow)\
                .then_inc(self.rstd_ready.sem, 1)
            pool.wait_ge(self.shift_ready.sem, self.shift_ready.value(n, 1))
            pool.tensor_tensor(self.ex[:, :, :].rearrange("p t e -> p (t e)"), k.euler[:, 0:self.T * self.E],
                               self.lg[:, :, :].rearrange("p t e -> p (t e)"), ALU.pow)\
                .then_inc(self.ex_ready.sem, 1)

    def dve_prep(self, dve, st, n, par, j):
        k, T = self.k, self.T
        if j == 0:
            st.start(n)
            for i in range(T):
                last = dve.bn_stats(self.stats[:, i, :], k.x_all[:, k.tile0 + n * T + i, :])
            st.done(last)
            st.carry(k.spare)
            for i in range(T):
                last = dve.bn_aggr(self.mv[:, i, :], self.stats[:, i, :])
            st.done(last)
            dve.tensor_scalar(self.ve[:, :], self.mv[:, :, 1], k.EPS, None, ALU.add)\
                .then_inc(self.ve_ready.sem, 1)
        if j == 3:
            dve.wait_ge(self.rstd_ready.sem, self.rstd_ready.value(n, 1))
            for i in range(T):
                last = dve.tensor_scalar(self.xn[:, i, :], k.x_all[:, k.tile0 + n * T + i, :],
                                         self.mv[:, i, 0:1], self.rstd[:, i:i + 1], ALU.subtract, ALU.mult)
            last.then_inc(self.xn_ready.sem, 1)
        if j == 6:
            dve.wait_ge(self.xhi_ready.sem, self.xhi_ready.value(n, 1))
            dve.tensor_tensor(self.xlo[:, par, :], self.M0, self.xhi[:, par, :], ALU.subtract)\
                .then_inc(self.xlo_ready.sem, 1)
        if j == 8:
            dve.wait_ge(self.lg_ready.sem, self.lg_ready.value(n, 1))
            st.done(dve.tensor_tensor(self.lg[:, :, :], self.M0[:, 0:T * self.E].rearrange("p (t e) -> p t e", t=T),
                                      bc(k.bg_sb[:, :], 1, T), ALU.add))
            st.done(dve.tensor_reduce(self.mx[:, :], self.lg[:, :, :], AX.X, ALU.max))
            dve.tensor_tensor(self.lg[:, :, :], self.lg[:, :, :], bc(self.mx[:, :], 2, self.E), ALU.subtract)\
                .then_inc(self.shift_ready.sem, 1)
        if j == 11:
            dve.wait_ge(self.ex_ready.sem, self.ex_ready.value(n, 1))
            st.done(dve.tensor_reduce(self.z[:, :], self.ex[:, :, :], AX.X, ALU.add))
            st.done(dve.reciprocal(self.zr[:, :], self.z[:, :]))
            st.done(dve.tensor_tensor(self.pr[:, :, :], self.ex[:, :, :], bc(self.zr[:, :], 2, self.E), ALU.mult))
        if j == 12:
            for i in range(T):
                last = dve.max(self.top[:, i, :], self.pr[:, i, :])
            st.done(last)
            st.carry(k.spare)
            for i in range(T):
                last = dve.max_index(self.topi[:, i, :], self.top[:, i, :], self.pr[:, i, :])
            st.done(last)
        if j == 14:
            st.done(dve.tensor_copy(self.topf[:, :, :], self.topi[:, :, :]))
            for i in range(T):
                dve.tensor_scalar(self.m1[:, i, :], k.iota8[:, :], self.topf[:, i, 0:1], None, ALU.is_equal)
                last = dve.tensor_scalar(self.m2[:, i, :], k.iota8[:, :], self.topf[:, i, 1:2], None, ALU.is_equal)
            st.done(last)
            st.done(dve.tensor_tensor(self.m1[:, :, :], self.m1[:, :, :], self.m2[:, :, :], ALU.add))
            st.done(dve.tensor_tensor(self.pr[:, :, :], self.pr[:, :, :], self.m1[:, :, :], ALU.mult))
        if j == 15:
            st.done(dve.tensor_reduce(self.z[:, :], self.pr[:, :, :], AX.X, ALU.add))
            st.done(dve.tensor_scalar(self.z[:, :], self.z[:, :], 1e-8, None, ALU.add))
            st.done(dve.reciprocal(self.zr[:, :], self.z[:, :]))
            st.done(dve.tensor_tensor(self.gs[:, :, :], self.pr[:, :, :], bc(self.zr[:, :], 2, self.E), ALU.mult))
        if j == 16:
            E = self.E
            g1, g2, g3 = (self.gp[:, :, m * E:(m + 1) * E] for m in range(3))
            st.done(dve.tensor_copy(g1, self.gs[:, :, :]))
            st.done(dve.tensor_tensor(self.m1[:, :, :], self.gs[:, :, :], g1, ALU.subtract))
            st.done(dve.tensor_copy(g2, self.m1[:, :, :]))
            dve.tensor_tensor(g3, self.m1[:, :, :], g2, ALU.subtract).then_inc(self.gp_ready.sem, 1)
            st.finish()

    def dve_weigh(self, dve, g, par, e):
        dve.wait_ge(self.h_used.sem, self.h_used.value(g, (e + 1) * self.C))
        if e == 0:
            dve.wait_ge(self.Gb_ready.sem, self.Gb_ready.value(g, self.E))
        out = self.acc if e == 0 else self.tmp
        dve.tensor_tensor(out[:, :], self.o_bank(e), self.Gb[:, par, e, :], ALU.mult)\
            .then_inc(self.o_used.sem, 1)
        if e > 0:
            dve.wait_ge(self.o_used.sem, self.o_used.value(g, e + 1))
            last = dve.tensor_tensor(self.acc[:, :], self.acc[:, :], self.tmp[:, :], ALU.add)
            if e == self.E - 1:
                last.then_inc(self.acc_ready.sem, 1)

    def vector(self, dve):
        k = self.k
        st = Steps(dve, self.steps)
        for j in range(self.J):
            self.dve_prep(dve, st, 0, 0, j)
        with dve.Fori(0, self.G // 2) as i:
            for par in range(2):
                g = i * 2 + par
                for j in range(self.J + 1):
                    if j < self.J:
                        dve.wait_ge(self.gelu_done.sem, self.gelu_done.value(g, j + 1))
                        dve.tensor_tensor(self.hlo[:, j % self.HB, :], self.h32[:, j % 2, :],
                                          self.hhi[:, j % self.HB, :], ALU.subtract)\
                            .then_inc(self.lo_done.sem, 1)
                    if j and j % self.C == 0:
                        self.dve_weigh(dve, g, par, j // self.C - 1)
                    if j < self.J:
                        self.dve_prep(dve, st, g + 1, 1 - par, j)
                dve.wait_ge(self.out_ready.sem, self.out_ready.value(g, 1))
                dve.wait_ge(self.stored[par].sem, self.stored[par].value(i, 0))
                dve.tensor_tensor(self.ost[:, par, :, :], k.x_all[:, bass.ds(k.tile0 + g * self.T, self.T), :],
                                  self.M1.rearrange("p (t d) -> p t d", t=self.T), ALU.add)\
                    .then_inc(self.out_sum.sem, 1)

    def sync(self, sp):
        k = self.k
        with sp.Fori(0, self.G // 2) as i:
            for par in range(2):
                g = i * 2 + par
                sp.wait_ge(self.out_sum.sem, self.out_sum.value(g, 1))
                sp.dma_start(k.out_v[:, bass.ds(g * self.T, self.T), :], self.ost[:, par, :, :])\
                    .then_inc(self.stored[par].sem, 16)
        for s in self.stored:
            sp.wait_ge(s.sem, s.value(self.G // 2, 0))


class Cross:

    HEADS, D, ROWS = 16, 8, 24
    UNITS = 4
    DVE_STEPS = 2

    def __init__(self, k):
        self.k = k
        sb, sem = k.sb, k.sem
        H = self.HEADS
        self.MEM = k.ap["ctx_1024"].shape[1]
        self.KEYS = self.MEM + k.S
        self.QS = sb("x_QS", [P, 2, 2, H, 32], F16)
        self.KS = sb("x_KS", [P, 3, H, 32], F16)
        self.VS = sb("x_VS", [P, 2, 3, H, 18], F16)
        self.O = sb("x_O", [P, 2, H * 18], F32)
        self.Os = sb("x_Os", [P, 2, H, 9], F32)
        S = lambda name, per, credit=0: Count(sem("x_" + name), per, credit)
        self.ve_ready = S("ve_ready", 1)
        self.rstd_ready = S("rstd_ready", 1)
        self.h2_ready = S("h2_ready", 1)
        self.XT_ready = S("XT_ready", 1)
        self.XThi_ready = S("XThi_ready", 1)
        self.XTlo_ready = S("XTlo_ready", 1)
        self.kv01_ready = S("kv01_ready", 1)
        self.kvq_ready = S("kvq_ready", 1)
        self.hi_ready = S("hi_ready", 2)
        self.lo_ready = S("lo_ready", 2)
        self.KT_ps = S("KT_ps", 2)
        self.KT_ready = S("KT_ready", 2)
        self.QT_ps = S("QT_ps", 1)
        self.QT_ready = S("QT_ready", 1)
        self.s_ready = S("s_ready", H)
        self.max_done = S("max_done", H, 2)
        self.m_ready = S("m_ready", 4)
        self.QM_ps = S("QM_ps", 4)
        self.QM_ready = S("QM_ready", 4)
        self.t_ready = S("t_ready", H)
        self.exp_done = S("exp_done", H, 2)
        self.elo_done = [S(f"elo_done{i}", H // 2, 1) for i in range(2)]
        self.pv_done = S("pv_done", H, 2)
        self.O_ready = S("O_ready", 1, 1)
        self.at_ready = S("at_ready", 1)
        self.atT_ready = S("atT_ready", 1)
        self.aT_ready = S("aT_ready", 1)
        self.y_ready = S("y_ready", 1)
        self.x_done = S("x_done", 1, 1)
        self.shift_step = S("shift_steps", 2)
        self.tail_step = S("tail_steps", 2)
        self.steps = S("dve_steps", self.DVE_STEPS)
        self.X, self.Y = k.ps[:, 6, :], k.ps[:, 7, :]

    def alloc(self):
        k, sb, H = self.k, self.k.sb, self.HEADS
        self.mem = sb("x_mem", [self.MEM, P], F32)
        self.h2 = sb("x_h2", [P, 2, P], F32)
        self.stats = sb("x_stats", [P, 2, 6], F32)
        self.mv = sb("x_mv", [P, 2, 2], F32)
        self.ve = sb("x_ve", [P, 2], F32)
        self.rstd = sb("x_rstd", [P, 2], F32)
        self.XThi = sb("x_XThi", [P, self.KEYS], F16)
        self.XTlo = sb("x_XTlo", [P, self.KEYS], F16)
        self.QT = sb("x_QT", [P, 2, 4, k.S], F16)
        self.KT = sb("x_KT", [P, 2, 4, 3 * P], F16)
        self.QM = sb("x_QM", [P, 2, k.S], F16)
        self.mneg = sb("x_mneg", [P, 2, 4, 2], F32)
        self.mcl = sb("x_mcl", [P, 2, 4, 2], F32)
        self.E32 = sb("x_E32", [P, 2, 512], F32)
        self.Ehi = sb("x_Ehi", [P, 2, 512], F16)
        self.Elo = sb("x_Elo", [P, 2, 512], F16)
        self.r = sb("x_r", [P, 2, H], F32)
        self.at = sb("x_at", [P, 2, P], F32)
        self.aT = sb("x_aT", [P, k.S], F32)

    def s_bank(self, h):
        return self.k.ps[:, h % 2, :]

    def t_bank(self, h):
        return self.k.ps[:, 2 + h % 2, :]

    def o_bank(self, s):
        return self.k.ps[:, 4 + s, :]

    def credits(self, eng):
        for s in (self.max_done, self.exp_done, *self.elo_done, self.pv_done, self.O_ready, self.x_done):
            eng.sem_inc(s.sem, s.credit)

    def clear(self, pool):
        H = self.HEADS
        pool.memset(self.QS[:, :, :, :, :], 0.0)
        pool.memset(self.VS[:, :, :, :, :], 0.0)
        pool.memset(self.O[:, :, :], 1.0)
        pool.memset(self.Os[:, :, :, :], 1.0)
        return pool.memset(self.KS[:, :, :, :], 0.0)

    def ones(self, pool):
        pool.memset(self.KS[:, :, :, 24:26], 1.0)
        return pool.memset(self.VS[:, :, :, :, 8:9], 1.0)

    def dve_front(self, dve, st, b, par, j):
        k = self.k
        tile = lambda s: k.x_all[:, k.tile0 + b * 2 + s, :]
        if j == 0:
            st.start(b)
            for s in range(2):
                last = dve.bn_stats(self.stats[:, s, :], tile(s))
            st.done(last)
            st.carry(k.spare)
            for s in range(2):
                last = dve.bn_aggr(self.mv[:, s, :], self.stats[:, s, :])
            st.done(last)
            dve.tensor_scalar(self.ve[:, :], self.mv[:, :, 1], k.EPS, None, ALU.add)\
                .then_inc(self.ve_ready.sem, 1)
        if j == 2:
            dve.tensor_copy(self.mem[:, :], k.ctx_all[:, b, :])
            dve.wait_ge(self.rstd_ready.sem, self.rstd_ready.value(b, 1))
            for s in range(2):
                last = dve.tensor_scalar(self.h2[:, s, :], tile(s), self.mv[:, s, 0:1],
                                         self.rstd[:, s:s + 1], ALU.subtract, ALU.mult)
            last.then_inc(self.h2_ready.sem, 1)
        if j == 4:
            dve.wait_ge(self.XThi_ready.sem, self.XThi_ready.value(b, 1))
            dve.tensor_tensor(self.XTlo[:, :], self.X[:, 0:self.KEYS], self.XThi[:, :], ALU.subtract)\
                .then_inc(self.XTlo_ready.sem, 1)
        if j in (6, 7):
            dve.wait_ge(self.hi_ready.sem, self.hi_ready.value(b, j - 5))
            for c in (0, 1) if j == 6 else (2,):
                n = P if c < 2 else self.KEYS - 2 * P
                kv = (self.Y[:, c * 256:(c + 1) * 256] if c < 2 else self.X[:, 0:256])[0:n]
                kh = lambda lo: kv[:, lo:lo + P].rearrange("p (h d) -> p h d", h=self.HEADS)
                dve.scalar_tensor_tensor(self.KS[0:n, c, :, 16:24], kh(0), 1 / WS, self.KS[0:n, c, :, 0:8],
                                         ALU.mult, ALU.subtract)
                last = dve.scalar_tensor_tensor(self.VS[0:n, par, c, :, 9:17], kh(P), 1 / WS,
                                                self.VS[0:n, par, c, :, 0:8], ALU.mult, ALU.subtract)
            if j == 7:
                for s in range(2):
                    q = self.X[:, 256 + s * P:256 + (s + 1) * P].rearrange("p (h d) -> p h d", h=self.HEADS)
                    last = dve.scalar_tensor_tensor(self.QS[:, par, s, :, 8:16], q, self.D ** -0.5 / WS,
                                                    self.QS[:, par, s, :, 0:8], ALU.mult, ALU.subtract)
            last.then_inc(self.lo_ready.sem, 1)
        if j == 10:
            dve.wait_ge(self.QT_ps.sem, self.QT_ps.value(b, 1))
            dve.tensor_copy(self.QT[:, par, :, :].rearrange("p g q -> p (g q)"), self.X.bitcast(F16))\
                .then_inc(self.QT_ready.sem, 1)

    def pe_front(self, pe, b, par, j):
        k = self.k
        if j == 3:
            pe.wait_ge(self.h2_ready.sem, self.h2_ready.value(b, 1))
            for s in range(2):
                pe.transpose(self.X[:, self.MEM + s * P:self.MEM + (s + 1) * P], self.h2[:, s, :], k.identF[:, :])
            last = pe.transpose(self.X[:, 0:self.MEM], self.mem[:, :], k.identF[0:self.MEM, 0:self.MEM])
            last.then_inc(self.XT_ready.sem, 1)
        if j == 5:
            pe.wait_ge(self.XTlo_ready.sem, self.XTlo_ready.value(b, 1))
            pe.wait_ge(self.x_done.sem, self.x_done.value(b, 0))

            def project(out, cols, whi, wlo, first):
                n = cols.stop - cols.start
                for i, (a, w) in enumerate(((self.XThi, whi), (self.XTlo, whi), (self.XThi, wlo))):
                    last = pe.matmul(out[0:n], a[:, cols], w, start=(first and i == 0), stop=(i == 2),
                                     skip_group_check=True)
                return last

            for c in range(2):
                last = project(self.Y[:, c * 256:(c + 1) * 256], slice(c * P, (c + 1) * P),
                               k.Wkv_hi[:, :], k.Wkv_lo[:, :], c == 0)
            last.then_inc(self.kv01_ready.sem, 1)
            for s in range(2):
                project(self.X[:, 256 + s * P:256 + (s + 1) * P],
                        slice(self.MEM + s * P, self.MEM + (s + 1) * P), k.Wq_hi[:, :], k.Wq_lo[:, :], s == 0)
            project(self.X[:, 0:256], slice(2 * P, self.KEYS), k.Wkv_hi[:, :], k.Wkv_lo[:, :], False)\
                .then_inc(self.kvq_ready.sem, 1)
        if j == 8:
            pe.wait_ge(self.lo_ready.sem, self.lo_ready.value(b, 2))
            for half, bank in enumerate((self.Y, self.X)):
                for u in (2 * half, 2 * half + 1):
                    for c in range(3):
                        at = ((u % 2) * 3 + c) * P
                        last = pe.transpose(bank.bitcast(F16)[:, at:at + P],
                                            self.KS[:, c, 4 * u:4 * u + 4, :].rearrange("p h r -> p (h r)"),
                                            k.ident16[:, :])
                last.then_inc(self.KT_ps.sem, 1)
        if j == 10:
            pe.wait_ge(self.KT_ready.sem, self.KT_ready.value(b, 2))
            for u in range(4):
                for s in range(2):
                    last = pe.transpose(self.X.bitcast(F16)[:, (2 * u + s) * P:(2 * u + s + 1) * P],
                                        self.QS[:, par, s, 4 * u:4 * u + 4, :].rearrange("p h r -> p (h r)"),
                                        k.ident16[:, :])
            last.then_inc(self.QT_ps.sem, 1)

    def act_front(self, act, b, par, j):
        k = self.k
        if j == 3:
            act.wait_ge(self.XT_ready.sem, self.XT_ready.value(b, 1))
            act.copy(self.XThi[:, :], self.X[:, 0:self.KEYS]).then_inc(self.XThi_ready.sem, 1)
        if j in (5, 6):
            ready = self.kv01_ready if j == 5 else self.kvq_ready
            act.wait_ge(ready.sem, ready.value(b, 1))
            for c in (0, 1) if j == 5 else (2,):
                n = P if c < 2 else self.KEYS - 2 * P
                kv = (self.Y[:, c * 256:(c + 1) * 256] if c < 2 else self.X[:, 0:256])[0:n]
                kh = lambda lo: kv[:, lo:lo + P].rearrange("p (h d) -> p h d", h=self.HEADS)
                act.activation(self.KS[0:n, c, :, 0:16].rearrange("p h (t d) -> p h t d", t=2), bc(kh(0), 2, 2),
                               ACT.Copy, scale=1 / WS)
                last = act.activation(self.VS[0:n, par, c, :, 0:8], kh(P), ACT.Copy, scale=1 / WS)
            if j == 6:
                for s in range(2):
                    q = self.X[:, 256 + s * P:256 + (s + 1) * P].rearrange("p (h d) -> p h d", h=self.HEADS)
                    act.activation(self.QS[:, par, s, :, 0:8], q, ACT.Copy, scale=self.D ** -0.5 / WS)
                    last = act.activation(self.QS[:, par, s, :, 16:24], q, ACT.Copy, scale=self.D ** -0.5 / WS)
            last.then_inc(self.hi_ready.sem, 1)
        if j in (8, 9):
            half = j - 8
            act.wait_ge(self.KT_ps.sem, self.KT_ps.value(b, half + 1))
            act.copy(self.KT[:, par, 2 * half:2 * half + 2, :].rearrange("p g q -> p (g q)"),
                     (self.Y, self.X)[half].bitcast(F16)[:, 0:6 * P]).then_inc(self.KT_ready.sem, 1)

    def pe_scores(self, pe, b, par, h):
        k, u, r = self.k, h // 4, slice(32 * (h % 4), 32 * (h % 4) + self.ROWS)
        if h == 0:
            pe.wait_ge(self.QT_ready.sem, self.QT_ready.value(b, 1))
        pe.wait_ge(self.max_done.sem, self.max_done.value(b, h - 1))
        S = self.s_bank(h)
        pe.matmul(S, k.identB[:, :], k.maskq_x[:, :], start=True, stop=False)
        pe.matmul(S[:, 0:192], self.QT[r, par, u, 0:P], self.KT[r, par, u, 0:192], start=False, stop=False)
        pe.matmul(S[:, 192:512], self.QT[r, par, u, P:2 * P], self.KT[r, par, u, 0:320], start=False,
                  stop=True).then_inc(self.s_ready.sem, 1)

    def dve_max(self, dve, b, h):
        dve.wait_ge(self.s_ready.sem, self.s_ready.value(b, h + 1))
        S, m = self.s_bank(h), self.mneg[:, (h // 4) % 2, h % 4, :]
        dve.tensor_reduce(m[:, 0:1], S[:, 0:192], AX.X, ALU.max, negate=True)
        dve.tensor_reduce(m[:, 1:2], S[:, 192:512], AX.X, ALU.max, negate=True)\
            .then_inc(self.max_done.sem, 1)

    def dve_shift(self, dve, st, b, par, u):
        dve.wait_ge(self.max_done.sem, self.max_done.value(b, 4 * u + 4))
        w = u % 2
        st.start(b * 4 + u)
        st.done(dve.tensor_scalar(self.mcl[:, w], self.mneg[:, w], CLAMP, -CLAMP, ALU.min, ALU.max))
        rows = self.QS[:, par, :, 4 * u:4 * u + 4, :].rearrange("p s h r -> p h s r")
        st.done(dve.tensor_copy(rows[:, :, :, 24], self.mcl[:, w]))
        dve.tensor_tensor(rows[:, :, :, 25], self.mcl[:, w], rows[:, :, :, 24], ALU.subtract)\
            .then_inc(self.m_ready.sem, 1)

    def pe_shift(self, pe, b, par, u):
        k = self.k
        pe.wait_ge(self.m_ready.sem, self.m_ready.value(b, u + 1))
        for s in range(2):
            last = pe.transpose(self.s_bank(1).bitcast(F16)[:, s * P:(s + 1) * P],
                                self.QS[:, par, s, 4 * u:4 * u + 4, :].rearrange("p h r -> p (h r)"),
                                k.ident16[:, :])
        last.then_inc(self.QM_ps.sem, 1)

    def dve_shifted(self, dve, b, u):
        dve.wait_ge(self.QM_ps.sem, self.QM_ps.value(b, u + 1))
        dve.tensor_copy(self.QM[:, u % 2, :], self.s_bank(1).bitcast(F16)[:, 0:2 * P])\
            .then_inc(self.QM_ready.sem, 1)

    def pe_keys(self, pe, b, par, h):
        k, u, r = self.k, h // 4, slice(32 * (h % 4), 32 * (h % 4) + 32)
        if h % 4 == 0:
            pe.wait_ge(self.QM_ready.sem, self.QM_ready.value(b, u + 1))
        pe.wait_ge(self.exp_done.sem, self.exp_done.value(b, h - 1))
        T = self.t_bank(h)
        pe.matmul(T, k.identB[:, :], k.maskk_x[:, :], start=True, stop=False)
        for c, q0, at in ((0, 0, 0), (1, 64, 256), (2, 192, 448)):
            n = 256 - q0
            last = pe.matmul(T[:, at:at + n], self.KT[r, par, u, c * P:(c + 1) * P], self.QM[r, u % 2, q0:256],
                             start=False, stop=(c == 2))
        last.then_inc(self.t_ready.sem, 1)

    def act_exp(self, act, b, h):
        act.wait_ge(self.t_ready.sem, self.t_ready.value(b, h + 1))
        lo = self.elo_done[h % 2]
        act.wait_ge(lo.sem, lo.value(b, h // 2))
        act.activation(self.E32[:, h % 2, :], self.t_bank(h), ACT.Exp)
        act.wait_ge(self.pv_done.sem, self.pv_done.value(b, h - 1))
        act.activation(self.Ehi[:, h % 2, :], self.t_bank(h), ACT.Exp).then_inc(self.exp_done.sem, 1)

    def split(self, eng, b, h):
        eng.wait_ge(self.exp_done.sem, self.exp_done.value(b, h + 1))
        eng.tensor_tensor(self.Elo[:, h % 2, :], self.E32[:, h % 2, :], self.Ehi[:, h % 2, :], ALU.subtract)\
            .then_inc(self.elo_done[h % 2].sem, 1)

    def pe_values(self, pe, b, par, h):
        if h == 0:
            pe.wait_ge(self.O_ready.sem, self.O_ready.value(b, 0))
        lo = self.elo_done[h % 2]
        pe.wait_ge(lo.sem, lo.value(b, h // 2 + 1))
        w = h % 2
        blocks = ((0, 0, 0, 0), (0, 1, 256, 64), (1, 0, 128, 0), (1, 1, 320, 0), (1, 2, 448, 64))
        for s, c, at, p0 in blocks:
            n = P - p0
            for part, (E, cols) in enumerate(((self.Ehi, 18), (self.Elo, 9))):
                last = pe.matmul(self.o_bank(s)[p0:P, h * 18:h * 18 + cols], E[:, w, at:at + n],
                                 self.VS[:, par, c, h, 0:cols], start=(h == 0 and c == 0 and part == 0),
                                 stop=True, skip_group_check=True)
        last.then_inc(self.pv_done.sem, 1)

    def act_output(self, act, b):
        act.wait_ge(self.pv_done.sem, self.pv_done.value(b, self.HEADS))
        act.wait_ge(self.at_ready.sem, self.at_ready.value(b, 1))
        act.copy(self.O[:, :, :], self.k.ps[:, 4:6, 0:self.HEADS * 18]).then_inc(self.O_ready.sem, 1)

    def tail(self, b1, dve=None, pe=None, act=None, j=0, st=None):
        k, H = self.k, self.HEADS
        O = self.O[:, :, :].rearrange("p s (h v) -> p (s h) v", h=H)
        Os = self.Os[:, :, :, :].rearrange("p s h v -> p (s h) v")
        if dve is not None and j == 0:
            dve.wait_ge(self.O_ready.sem, self.O_ready.value(b1, 0))
            st.done(dve.tensor_tensor(Os[:, :, 0:8], O[:, :, 0:8], O[:, :, 9:17], ALU.add))
            st.done(dve.reciprocal(self.r[:, :, :].rearrange("p s h -> p (s h)"), O[:, :, 8]))
            dve.tensor_tensor(self.at[:, :, :].rearrange("p s (h d) -> p (s h) d", h=H), Os[:, :, 0:8],
                              bc(self.r[:, :, :].rearrange("p s h -> p (s h)"), 2, self.D), ALU.mult)\
                .then_inc(self.at_ready.sem, 1)
        if pe is not None and j == 0:
            pe.wait_ge(self.at_ready.sem, self.at_ready.value(b1, 1))
            for s in range(2):
                last = pe.transpose(self.Y[:, s * P:(s + 1) * P], self.at[:, s, :], k.identF[:, :])
            last.then_inc(self.atT_ready.sem, 1)
        if act is not None and j == 0:
            act.wait_ge(self.atT_ready.sem, self.atT_ready.value(b1, 1))
            act.copy(self.aT[:, :], self.Y[:, 0:2 * P]).then_inc(self.aT_ready.sem, 1)
        if pe is not None and j == 1:
            pe.wait_ge(self.aT_ready.sem, self.aT_ready.value(b1, 1))
            for s in range(2):
                out = self.Y[:, s * P:(s + 1) * P]
                pe.matmul(out, k.one_row[:, :], k.bout_sb[:, :], start=(s == 0), stop=False, skip_group_check=True)
                last = pe.matmul(out, self.aT[:, s * P:(s + 1) * P], k.Wout_sb[:, :], start=False, stop=True,
                                 skip_group_check=True)
            last.then_inc(self.y_ready.sem, 1)
        if dve is not None and j == 1:
            dve.wait_ge(self.y_ready.sem, self.y_ready.value(b1, 1))
            x = k.x_all[:, bass.ds(b1 * 2, 2), :]
            dve.tensor_tensor(x, x, self.Y[:, 0:2 * P].rearrange("p (s d) -> p s d", s=2), ALU.add)\
                .then_inc(self.x_done.sem, 1)

    def tensor(self, pe):
        for j in range(self.HEADS):
            self.pe_front(pe, 0, 0, j)
        for h in range(4):
            self.pe_scores(pe, 0, 0, h)
        self.pe_shift(pe, 0, 0, 0)
        self.pe_keys(pe, 0, 0, 0)
        with pe.Fori(0, self.k.B // 2) as i:
            for par in range(2):
                b = i * 2 + par
                for h in range(self.HEADS):
                    u, j = h // 4, h % 4
                    if h == 1:
                        self.tail(b, pe=pe, j=0)
                    if h == 3:
                        self.tail(b, pe=pe, j=1)
                    self.pe_front(pe, b + 1, 1 - par, h)
                    nb, npar, nu = (b, par, u + 1) if u < 3 else (b + 1, 1 - par, 0)
                    for x in ((0, 1), (2,), (3,), ())[j]:
                        self.pe_scores(pe, nb, npar, 4 * nu + x)
                    if j == 3:
                        self.pe_shift(pe, nb, npar, nu)
                        self.pe_values(pe, b, par, h)
                    if h + 1 < self.HEADS:
                        self.pe_keys(pe, b, par, h + 1)
                    else:
                        self.pe_keys(pe, b + 1, 1 - par, 0)
                    if j != 3:
                        self.pe_values(pe, b, par, h)
        self.tail(self.k.B, pe=pe, j=0)
        self.tail(self.k.B, pe=pe, j=1)

    def vector(self, dve):
        st, shift_st = Steps(dve, self.steps), Steps(dve, self.shift_step)
        for j in range(self.HEADS):
            self.dve_front(dve, st, 0, 0, j)
        for h in range(4):
            self.dve_max(dve, 0, h)
        self.dve_shift(dve, shift_st, 0, 0, 0)
        self.dve_shifted(dve, 0, 0)
        with dve.Fori(0, self.k.B // 2) as i:
            for par in range(2):
                b = i * 2 + par
                for h in range(self.HEADS):
                    u, j = h // 4, h % 4
                    nb, npar, nu = (b, par, u + 1) if u < 3 else (b + 1, 1 - par, 0)
                    for x in ((0, 1), (2,), (3,), ())[j]:
                        self.dve_max(dve, nb, 4 * nu + x)
                    if j == 2:
                        self.dve_shift(dve, shift_st, nb, npar, nu)
                    if h % 2 == 0:
                        self.split(dve, b, h)
                    if h == 0:
                        self.tail(b, dve=dve, j=0, st=self.tail_steps(dve, b))
                    if h == 4:
                        self.tail(b, dve=dve, j=1)
                    self.dve_front(dve, st, b + 1, 1 - par, h)
                    if j == 3:
                        self.dve_shifted(dve, nb, nu)
        self.tail(self.k.B, dve=dve, j=0, st=self.tail_steps(dve, self.k.B))
        self.tail(self.k.B, dve=dve, j=1)

    def tail_steps(self, dve, b1):
        st = Steps(dve, self.tail_step)
        st.start(b1)
        return st

    def scalar(self, act):
        for j in range(self.HEADS):
            self.act_front(act, 0, 0, j)
        with act.Fori(0, self.k.B // 2) as i:
            for par in range(2):
                b = i * 2 + par
                for h in range(self.HEADS):
                    self.act_exp(act, b, h)
                    if h == 2:
                        self.tail(b, act=act, j=0)
                    self.act_front(act, b + 1, 1 - par, h)
                self.act_output(act, b)
        self.tail(self.k.B, act=act, j=0)

    def gpsimd(self, pool):
        k = self.k

        def rstd(b):
            pool.wait_ge(self.ve_ready.sem, self.ve_ready.value(b, 1))
            pool.tensor_tensor(self.rstd[:, :], self.ve[:, :], k.minus_half[:, 0:2], ALU.pow)\
                .then_inc(self.rstd_ready.sem, 1)

        rstd(0)
        with pool.Fori(0, k.B) as b:
            for h in range(1, self.HEADS, 2):
                self.split(pool, b, h)
                if h == 1:
                    rstd(b + 1)


class SelfAttention:

    H, D, CR = 8, 64, 32
    OLD, WIN, SINK = range(3)
    KBLOCKS = ((0, 128, 0, 0, 0), (128, 64, 128, 64, 1), (192, 64, 192, 128, 2),
               (256, 192, 64, 0, 0), (448, 64, 192, 128, 2))
    VBLOCKS = ((0, 1, 0, 128, 0, 0), (1, 1, 128, 64, 0, 1), (1, 1, 192, 64, 64, 2),
               (0, 0, 256, 64, 64, 0), (1, 0, 320, 128, 0, 0), (1, 0, 448, 64, 64, 2))

    def __init__(self, k):
        self.k = k
        sb, sem = k.sb, k.sem
        H, D = self.H, self.D
        self.NB = k.S // self.CR
        NB = self.NB
        self.stats = sb("a_stats", [P, 2, 6], F32)
        self.mv = sb("a_mv", [P, 2, 2], F32)
        self.ve = sb("a_ve", [P, 2], F32)
        self.rstd = sb("a_rstd", [P, 2], F32)
        self.hn = sb("a_hn", [P, 2, P], F32)
        self.hThi = sb("a_hThi", [P, k.S], F16)
        self.hTlo = sb("a_hTlo", [P, k.S], F16)
        self.qraw = sb("a_qraw", [P, 2, H + 1, D], F32)
        self.sq = sb("a_sq", [P, 2, H + 1, D], F32)
        self.ms = sb("a_ms", [P, 2 * (H + 1)], F32)
        self.rq = sb("a_rq", [P, 2 * (H + 1)], F32)
        self.rope1 = sb("a_rope1", [P, 2, H + 1, 32], F32)
        self.rope2 = sb("a_rope2", [P, 2, H + 1, 32], F32)
        self.qn = sb("a_qn", [P, 2, H + 1, D], F32)
        self.QS = sb("a_QS", [P, 2, H, 2, D], F16)
        self.KS = sb("a_KS", [P, 2, 4, D], F16)
        self.QT = sb("a_QT", [P, 2, H, k.S], F16)
        self.KT = sb("a_KT", [P, 2, 2, k.S], F16)
        self.VS = sb("a_VS", [P, 2, 3, 2 * D + 1], F16)
        self.ks = sb("a_ks", [P, 2, NB], F32)
        self.kc = sb("a_kc", [P, NB], F32)
        self.kcg = sb("a_kcg", [P, 2, NB + 3], F16)
        self.vcT = sb("a_vcT", [P, 4, H, NB], F32)
        self.VW = sb("a_VW", [H * NB, 2, P], F32)
        self.EX = sb("a_EX", [P, 2 * H * (NB + 1) + 2 * H * 3], F32)
        self.cz = self.EX[:, 0:2 * H * (NB + 1)].rearrange("p (g n) -> p g n", n=NB + 1)
        self.gz = self.EX[:, 2 * H * (NB + 1):].rearrange("p (g n) -> p g n", n=3)
        self.czr = sb("a_czr", [P, 2 * H, NB], F32)
        self.cm = sb("a_cm", [P, 2 * H], F32)
        self.cl = sb("a_cl", [P, 2 * H], F32)
        self.gsum = sb("a_gsum", [P, 2 * H], F32)
        self.gcl = sb("a_gcl", [P, 2 * H], F32)
        self.gate = sb("a_gate", [P, 2, 3, 2 * H], F32)
        self.pcs = sb("a_pcs", [P, 2, 2 * H, NB], F32)
        self.pcT = sb("a_pcT", [H * NB, k.S], F32)
        self.mneg = sb("a_mneg", [P, 2, 4, 2, 2], F32)
        self.mcl = sb("a_mcl", [P, 2, 4, 2, 2], F32)
        self.mst = sb("a_mst", [P, 2, H, 2, 2], F16)
        self.mT = sb("a_mT", [4 * H, 2, k.S], F16)
        self.nm = sb("a_nm", [P, 2, 3, 2, H], F32)
        self.E32 = sb("a_E32", [P, 2, 512], F32)
        self.Ehi = sb("a_Ehi", [P, 2, 512], F16)
        self.Elo = sb("a_Elo", [P, 2, 512], F16)
        self.O = sb("a_O", [P, 2, 2, 2, H, D + 1], F32)
        self.n12 = sb("a_n12", [P, 2, 2 * H], F32)
        self.dx = sb("a_dx", [P, 4, 2 * H], F32)
        self.ea = sb("a_ea", [P, 4, 2 * H], F32)
        self.pl = sb("a_pl", [P, 3, 2 * H], F32)
        self.LL = sb("a_LL", [P, 2, 2 * H], F32)
        self.rr = sb("a_rr", [P, 2, 2 * H], F32)
        self.co = sb("a_co", [P, 3, 2 * H], F32)
        self.mixw = sb("a_mixw", [P, 2, H, D], F32)
        self.mixo = sb("a_mixo", [P, 2, H, D], F32)
        self.mixT = sb("a_mixT", [P, 2, 4, P], F32)
        S = lambda name, per, credit=0: Count(sem("a_" + name), per, credit)
        self.ve_ready = S("ve_ready", 1)
        self.rstd_ready = S("rstd_ready", 1)
        self.hn_ready = S("hn_ready", 1)
        self.hT_ps = S("hT_ps", 1)
        self.hThi_ready = S("hThi_ready", 1)
        self.hTlo_ready = S("hTlo_ready", 1)
        self.kv_ps = S("kv_ps", 1)
        self.kvhi_ready = S("kvhi_ready", 1)
        self.kvlo_ready = S("kvlo_ready", 1)
        self.ms_ready = S("ms_ready", 1)
        self.rq_ready = S("rq_ready", 1)
        self.rope_ready = S("rope_ready", 1)
        self.qn_ready = S("qn_ready", 1)
        self.QShi_ready = S("QShi_ready", 1)
        self.QSlo_ready = S("QSlo_ready", 1)
        self.cg_ps = S("cg_ps", 1)
        self.vc_ps = S("vc_ps", 1)
        self.vcT_ready = S("vcT_ready", 1)
        self.VW_ps = S("VW_ps", 1)
        self.VW_ready = S("VW_ready", 1)
        self.ex_ready = S("ex_ready", 1)
        self.exp_ready = S("exp_ready", 1)
        self.pcT_ps = S("pcT_ps", 1)
        self.pcT_ready = S("pcT_ready", 1)
        self.dx_ready = S("dx_ready", 1)
        self.ea_ready = S("ea_ready", 1)
        self.co_ready = S("co_ready", 1)
        self.mixo_ready = S("mixo_ready", 1)
        self.mix_ready = S("mix_ready", 1)
        self.mix_ps = S("mix_ps", 1)
        self.y_ps = S("y_ps", 1)
        self.kcg_ready = S("kcg_ready", 1)
        self.K_ps = S("K_ps", 1)
        self.K_ready = S("K_ready", 1)
        self.qs_done = S("qs_done", 1)
        self.q_ps = S("q_ps", 2)
        self.q_read = S("q_read", 2)
        self.Q_ps = S("Q_ps", 2)
        self.Q_ready = [S(f"Q_ready{s}", 1) for s in range(2)]
        self.mixT_ready = [S(f"mixT_ready{s}", 1) for s in range(2)]
        self.x_done = S("x_done", 1, 1)
        self.s_ready = S("s_ready", H)
        self.max_done = S("max_done", H, 2)
        self.m_ready = S("m_ready", 2)
        self.m_ps = S("m_ps", 2)
        self.mT_ready = S("mT_ready", 2)
        self.t_ready = S("t_ready", H)
        self.exp_done = S("exp_done", H, 2)
        self.elo_done = S("elo_done", H, 2)
        self.pv_done = S("pv_done", H, 2)
        self.o_done = S("o_done", H, 2)
        self.early_step = S("early_steps", 2)
        self.late_step = S("late_steps", 2)
        self.kc_step = S("kc_steps", 3)
        self.cg_step = S("cg_steps", 11)
        self.shift_step = S("shift_steps", 3)
        self.tail_step = S("tail_steps", 7)
        self.rope_step = S("rope_steps", 1)
        self.X, self.Y = k.ps[:, 6, :], k.ps[:, 7, :]

    def s_bank(self, h):
        return self.k.ps[:, h % 2, :]

    def t_bank(self, h):
        return self.k.ps[:, 2 + h % 2, :]

    def o_bank(self, h):
        return self.k.ps[:, 4 + h % 2, :]

    def credits(self, eng):
        for s in (self.max_done, self.exp_done, self.elo_done, self.pv_done, self.o_done, self.x_done):
            eng.sem_inc(s.sem, s.credit)

    def clear(self, pool):
        for t in (self.gate, self.nm, self.pcs, self.mst):
            pool.memset(t[:, :], 0.0)
        pool.memset(self.VW[:, :, :], 0.0)
        pool.memset(self.O[:, :], 1.0)
        pool.memset(self.VS[:, :, :, :], 1.0)
        return pool.memset(self.kcg[:, :, :], 0.0)

    def dve_front(self, dve, st, n, par, j, early):
        k, H, D = self.k, self.H, self.D
        tile = lambda s: k.x_all[:, k.tile0 + n * 2 + s, :]
        if early and j == 5:
            st.start(n)
            for s in range(2):
                last = dve.bn_stats(self.stats[:, s, :], tile(s))
            st.done(last)
            st.carry(k.spare)
            for s in range(2):
                last = dve.bn_aggr(self.mv[:, s, :], self.stats[:, s, :])
            st.done(last)
            dve.tensor_scalar(self.ve[:, :], self.mv[:, :, 1], k.EPS, None, ALU.add)\
                .then_inc(self.ve_ready.sem, 1)
        if early and j == 6:
            dve.wait_ge(self.rstd_ready.sem, self.rstd_ready.value(n, 1))
            for s in range(2):
                last = dve.tensor_scalar(self.hn[:, s, :], tile(s), self.mv[:, s, 0:1],
                                         self.rstd[:, s:s + 1], ALU.subtract, ALU.mult)
            last.then_inc(self.hn_ready.sem, 1)
        if early and j == 7:
            dve.wait_ge(self.hThi_ready.sem, self.hThi_ready.value(n, 1))
            dve.tensor_tensor(self.hTlo[:, :], self.Y[:, 0:k.S], self.hThi[:, :], ALU.subtract)\
                .then_inc(self.hTlo_ready.sem, 1)
        if early:
            return
        if j == 0:
            dve.wait_ge(self.kvhi_ready.sem, self.kvhi_ready.value(n, 1))
            for o, at in enumerate((D, 4 * D, 3 * D)):
                last = dve.scalar_tensor_tensor(self.VS[:, par, o, D + 1:], self.X[:, at:at + D], 1 / WS,
                                                self.VS[:, par, o, 0:D], ALU.mult, ALU.subtract)
            last.then_inc(self.kvlo_ready.sem, 1)
            st.start(n)
            dve.wait_ge(self.qs_done.sem, self.qs_done.value(n, 1))
            st.done(dve.tensor_reduce(self.ms[:, :], self.sq[:, :, :, :].rearrange("p s h d -> p (s h) d"),
                                      AX.X, ALU.add))
            dve.tensor_scalar(self.ms[:, :], self.ms[:, :], 1 / D, WS * WS * 1e-6, ALU.mult, ALU.add)\
                .then_inc(self.ms_ready.sem, 1)
        if j == 2:
            dve.wait_ge(self.rq_ready.sem, self.rq_ready.value(n, 1))
            flat = lambda t: t.rearrange("p s h d -> p (s h) d")
            dve.tensor_tensor(flat(self.qn[:, :, :, 32:D]), flat(self.qraw[:, :, :, 32:D]),
                              bc(self.rq[:, :], 2, D - 32), ALU.mult)
            dve.wait_ge(self.rope_ready.sem, self.rope_ready.value(n, 1))
            st.done(dve.tensor_tensor(flat(self.qn[:, :, :, 0:32]), flat(self.rope1[:, :, :, :]),
                                      bc(self.rq[:, :], 2, 32), ALU.mult))
            dve.tensor_tensor(self.qn[:, :, H, :], self.qn[:, :, H, :], bc(k.gqk_sb[:, :], 1, 2), ALU.mult)\
                .then_inc(self.qn_ready.sem, 1)
        if j == 3:
            dve.wait_ge(self.QShi_ready.sem, self.QShi_ready.value(n, 1))
            dve.tensor_tensor(self.KS[:, :, 2:4, :], bc(self.qn[:, :, H, :], 2, 2), self.KS[:, :, 0:2, :],
                              ALU.subtract)
            for s in range(2):
                last = dve.tensor_tensor(self.QS[:, s, :, 1, :], self.qn[:, s, 0:H, :], self.QS[:, s, :, 0, :],
                                         ALU.subtract)
            last.then_inc(self.QSlo_ready.sem, 1)
        if j == 4:
            dve.wait_ge(self.Q_ps.sem, self.Q_ps.value(n, 2))
            dve.tensor_copy(self.QT[:, par, :, P:2 * P], self.Y.bitcast(F16).rearrange("p (h q) -> p h q", h=H))\
                .then_inc(self.Q_ready[1].sem, 1)
        if j == 5:
            dve.wait_ge(self.K_ready.sem, self.K_ready.value(n, 1))
            st_ = self.kc_steps
            st_.start(n)
            st_.done(dve.tensor_reduce(self.ks[:, :, :], self.KT[:, par, :, :].rearrange(
                "p a (n c) -> p a n c", c=self.CR), AX.X, ALU.add))
            st_.done(dve.tensor_tensor(self.kc[:, :], self.ks[:, 0, :], self.ks[:, 1, :], ALU.add))
            st_.done(dve.tensor_scalar(self.kcg[:, 0, 0:self.NB], self.kc[:, :], 1 / self.CR, None, ALU.mult))
            dve.scalar_tensor_tensor(self.kcg[:, 1, 0:self.NB], self.kc[:, :], 1 / self.CR,
                                     self.kcg[:, 0, 0:self.NB], ALU.mult, ALU.subtract)\
                .then_inc(self.kcg_ready.sem, 1)
        if j == 6:
            dve.wait_ge(self.vc_ps.sem, self.vc_ps.value(n, 1))
            dve.tensor_tensor(self.vcT[:, :, :, :].rearrange("p c h n -> p (c h) n"),
                              bc(self.X[:, 0:self.NB], 1, 4 * H),
                              k.headmask[:, :, :, :].rearrange("p c h n -> p (c h) n"), ALU.mult)\
                .then_inc(self.vcT_ready.sem, 1)
            dve.wait_ge(self.cg_ps.sem, self.cg_ps.value(n, 1))
            cg = self.Y[:, 0:2 * H * (self.NB + 3)].rearrange("p (g n) -> p g n", n=self.NB + 3)
            cs = self.cg_steps
            cs.start(n)
            for s in range(2):
                g = slice(s * H, (s + 1) * H)
                dve.tensor_tensor(self.czr[:, g, :], cg[:, g, 0:self.NB], bc(k.maskc[:, s, :], 1, H), ALU.add)
            cs.done(dve.scalar_tensor_tensor(self.gz, cg[:, :, self.NB:], -1.0, bc(k.bgate_sb[:, :], 1, 2 * H),
                                             ALU.mult, ALU.subtract))
            cs.done(dve.tensor_reduce(self.cm[:, :], self.czr[:, :, :], AX.X, ALU.max))
            cs.done(dve.tensor_tensor(self.cm[:, :], self.cm[:, :], k.sink2[:, :], ALU.max))
            dve.tensor_tensor(self.cz[:, :, 0:self.NB], self.czr[:, :, :], bc(self.cm[:, :], 2, self.NB),
                              ALU.subtract)
            dve.tensor_tensor(self.cz[:, :, self.NB], k.sink2[:, :], self.cm[:, :], ALU.subtract)\
                .then_inc(self.ex_ready.sem, 1)
        if j == 7:
            cs = self.cg_steps
            g, NB = self.gate[:, par], self.NB
            dve.wait_ge(self.exp_ready.sem, self.exp_ready.value(n, 1))
            dve.tensor_reduce(self.cl[:, :], self.cz, AX.X, ALU.add)
            cs.done(dve.tensor_scalar(self.gz, self.gz, 1.0, None, ALU.add))
            cs.done(dve.reciprocal(self.gz, self.gz))
            cs.done(dve.tensor_reduce(self.gsum[:, :], self.gz, AX.X, ALU.add))
            cs.done(dve.tensor_scalar(self.gsum[:, :], self.gsum[:, :], 1e-6, None, ALU.max))
            dve.reciprocal(self.cl[:, :], self.cl[:, :])
            cs.done(dve.reciprocal(self.gsum[:, :], self.gsum[:, :]))
            cs.done(dve.tensor_tensor(g.rearrange("p n g -> p g n"), self.gz, bc(self.gsum[:, :], 2, 3), ALU.mult))
            cs.done(dve.tensor_tensor(self.gcl[:, :], g[:, 0, :], self.cl[:, :], ALU.mult))
            cs.done(dve.tensor_tensor(self.pcs[:, par, :, :], self.cz[:, :, 0:NB], bc(self.gcl[:, :], 2, NB),
                                      ALU.mult))

    def pe_front(self, pe, n, par, j, early, first=False):
        k, H, D = self.k, self.H, self.D
        parts = lambda whi, wlo: ((self.hThi, whi), (self.hTlo, whi), (self.hThi, wlo))
        if early and j == 6:
            pe.wait_ge(self.hn_ready.sem, self.hn_ready.value(n, 1))
            if not first:
                pe.wait_ge(self.ex_ready.sem, self.ex_ready.value(n - 1, 1))
            for s in range(2):
                last = pe.transpose(self.Y[:, s * P:(s + 1) * P], self.hn[:, s, :], k.identF[:, :])
            last.then_inc(self.hT_ps.sem, 1)
        if early and j == 7:
            pe.wait_ge(self.hTlo_ready.sem, self.hTlo_ready.value(n, 1))
            if not first:
                pe.wait_ge(self.VW_ready.sem, self.VW_ready.value(n - 1, 1))
            for s in range(2):
                for i, (a, w) in enumerate(parts(k.WQ_hi[:, :], k.WQ_lo[:, :])):
                    last = pe.matmul((self.X, self.Y)[s], a[:, s * P:(s + 1) * P], w, start=(i == 0), stop=(i == 2))
                last.then_inc(self.q_ps.sem, 1)
        if early:
            return
        if j == 0:
            pe.wait_ge(self.q_read.sem, self.q_read.value(n, 2))
            for at, w0, t0 in ((0, 0, 0), (P, 0, P), (2 * P, D, D)):
                for i, (a, w) in enumerate(parts(k.aKV_hi[:, w0:], k.aKV_lo[:, w0:])):
                    last = pe.matmul(self.X[:, at:at + P - w0], a[:, t0:t0 + P], w, start=(at == 0 and i == 0),
                                     stop=(i == 2), skip_group_check=True)
            last.then_inc(self.kv_ps.sem, 1)
        if j == 4:
            pe.wait_ge(self.QSlo_ready.sem, self.QSlo_ready.value(n, 1))
            pe.wait_ge(self.x_done.sem, self.x_done.value(n, 0))
            for s in range(2):
                for h in range(H):
                    last = pe.transpose((self.X, self.Y)[s].bitcast(F16)[:, h * P:(h + 1) * P],
                                        self.QS[:, s, h, :, :].rearrange("p a d -> p (a d)"), k.ident16[:, :])
                last.then_inc(self.Q_ps.sem, 1)
            pe.wait_ge(self.Q_ready[0].sem, self.Q_ready[0].value(n, 1))
            for s in range(2):
                for a in range(2):
                    last = pe.transpose(self.X.bitcast(F16)[:, a * k.S + s * P:a * k.S + (s + 1) * P],
                                        self.KS[:, s, 2 * a:2 * a + 2, :].rearrange("p a d -> p (a d)"),
                                        k.ident16[:, :])
            last.then_inc(self.K_ps.sem, 1)
        if j == 5:
            pe.wait_ge(self.kcg_ready.sem, self.kcg_ready.value(n, 1))
            for half in range(2):
                for s, o in ((0, 0), (1, 2)):
                    for a in (slice(0, D), slice(D + 1, 2 * D + 1)):
                        last = pe.matmul(self.X[half * D:(half + 1) * D, 0:self.NB], self.VS[:, par, o, a],
                                         k.blockmean[:, s, :], start=(s == 0 and a.start == 0),
                                         stop=(s == 1 and a.start > 0), skip_group_check=True)
            last.then_inc(self.vc_ps.sem, 1)
            pe.wait_ge(self.Q_ready[1].sem, self.Q_ready[1].value(n, 1))
            w = self.NB + 3
            for s in range(2):
                for h in range(H):
                    at = (s * H + h) * w
                    q = slice(s * P, (s + 1) * P)
                    pe.matmul(self.Y[:, at:at + w], self.QT[:, par, h, q], self.kcg[:, 0, :],
                              start=(s == 0 and h == 0), stop=False, skip_group_check=True)
                    last = pe.matmul(self.Y[:, at:at + w], self.QT[0:D, par, h, q], self.kcg[0:D, 1, :],
                                     start=False, stop=True, skip_group_check=True)
            last.then_inc(self.cg_ps.sem, 1)
        if j == 6:
            pe.wait_ge(self.vcT_ready.sem, self.vcT_ready.value(n, 1))
            for c in range(4):
                last = pe.matmul(self.X[0:H * self.NB, 0:P], self.vcT[:, c, :, :].rearrange("p h n -> p (h n)"),
                                 k.Weff[:, c, :], start=(c == 0), stop=(c == 3))
            last.then_inc(self.VW_ps.sem, 1)

    def act_front(self, act, n, par, j, early):
        k, H, D = self.k, self.H, self.D
        if early and j == 6:
            act.wait_ge(self.hT_ps.sem, self.hT_ps.value(n, 1))
            act.copy(self.hThi[:, :], self.Y[:, 0:k.S]).then_inc(self.hThi_ready.sem, 1)
        if early and j == 7:
            for s in range(2):
                act.wait_ge(self.q_ps.sem, self.q_ps.value(n, s + 1))
                q = (self.X, self.Y)[s].rearrange("p (h d) -> p h d", h=H)
                act.copy(self.qraw[:, s, 0:H, :], q)
                act.activation(self.sq[:, s, 0:H, :], q, ACT.Square).then_inc(self.q_read.sem, 1)
        if early:
            return
        if j == 0:
            act.wait_ge(self.kv_ps.sem, self.kv_ps.value(n, 1))
            kx = self.X[:, 0:2 * P].rearrange("p (s d) -> p s d", s=2)[:, :, 0:D]
            act.copy(self.qraw[:, :, H, :], kx)
            act.activation(self.sq[:, :, H, :], kx, ACT.Square).then_inc(self.qs_done.sem, 1)
            for o, at in enumerate((D, 4 * D, 3 * D)):
                last = act.activation(self.VS[:, par, o, 0:D], self.X[:, at:at + D], ACT.Copy, scale=1 / WS)
            last.then_inc(self.kvhi_ready.sem, 1)
        if j == 2:
            act.wait_ge(self.qn_ready.sem, self.qn_ready.value(n, 1))
            act.copy(self.KS[:, :, 0:2, :], bc(self.qn[:, :, H, :], 2, 2))
            for s in range(2):
                last = act.copy(self.QS[:, s, :, 0, :], self.qn[:, s, 0:H, :])
            last.then_inc(self.QShi_ready.sem, 1)
        if j == 4:
            act.wait_ge(self.Q_ps.sem, self.Q_ps.value(n, 1))
            act.copy(self.QT[:, par, :, 0:P], self.X.bitcast(F16).rearrange("p (h q) -> p h q", h=H))\
                .then_inc(self.Q_ready[0].sem, 1)
            act.wait_ge(self.K_ps.sem, self.K_ps.value(n, 1))
            act.copy(self.KT[:, par, :, :].rearrange("p a q -> p (a q)"), self.X.bitcast(F16)[:, 0:2 * k.S])\
                .then_inc(self.K_ready.sem, 1)
        if j == 6:
            act.wait_ge(self.VW_ps.sem, self.VW_ps.value(n, 1))
            act.copy(self.VW[:, par, :], self.X[0:H * self.NB, 0:P]).then_inc(self.VW_ready.sem, 1)
            act.wait_ge(self.ex_ready.sem, self.ex_ready.value(n, 1))
            act.activation(self.EX[:, :], self.EX[:, :], ACT.Exp).then_inc(self.exp_ready.sem, 1)

    def pool_rstd(self, pool, n):
        pool.wait_ge(self.ve_ready.sem, self.ve_ready.value(n, 1))
        pool.tensor_tensor(self.rstd[:, :], self.ve[:, :], self.k.minus_half[:, 0:2], ALU.pow)\
            .then_inc(self.rstd_ready.sem, 1)

    def pool_rope(self, pool, n):
        k, H = self.k, self.H
        pool.wait_ge(self.qs_done.sem, self.qs_done.value(n, 1))
        x, r1, r2 = self.qraw, self.rope1, self.rope2
        for s in range(2):
            cos, sin = (bc(k.rope_sb[:, s, a * 32:(a + 1) * 32], 1, H + 1) for a in range(2))
            pool.tensor_tensor(r1[:, s, :, :], x[:, s, :, 0:32], cos, ALU.mult)
            pool.tensor_tensor(r2[:, s, :, 0:16], x[:, s, :, 16:32], sin[:, :, 0:16], ALU.mult)
            last = pool.tensor_tensor(r2[:, s, :, 16:32], x[:, s, :, 0:16], sin[:, :, 16:32], ALU.mult)
        self.rope_steps.start(n)
        self.rope_steps.done(last)
        flat = lambda t: t[:, :, :, :].rearrange("p s h d -> p (s h d)")
        pool.tensor_tensor(flat(r1), flat(r1), flat(r2), ALU.add).then_inc(self.rope_ready.sem, 1)
        pool.wait_ge(self.ms_ready.sem, self.ms_ready.value(n, 1))
        pool.tensor_tensor(self.rq[:, :], self.ms[:, :], k.minus_half[:, 0:2 * (H + 1)], ALU.pow)\
            .then_inc(self.rq_ready.sem, 1)

    def pe_scores(self, pe, b, par, h):
        k, D = self.k, self.D
        if h == 0:
            pe.wait_ge(self.K_ready.sem, self.K_ready.value(b, 1))
            pe.wait_ge(self.Q_ready[1].sem, self.Q_ready[1].value(b, 1))
        pe.wait_ge(self.max_done.sem, self.max_done.value(b, h - 1))
        S, Q, K = self.s_bank(h), self.QT[0:D, par, h, :], self.KT[0:D, par, 0, :]
        pe.matmul(S, k.identB[:, :], k.maskq_a[:, :], start=True, stop=False)
        mm = lambda out, q, keys, stop=False: pe.matmul(out, Q[:, q], K[:, keys], start=False, stop=stop)
        mm(S[:, 0:128], slice(0, 128), slice(0, 128))
        mm(S[0:64, 128:256], slice(128, 192), slice(64, 192))
        mm(S[64:128, 128:256], slice(192, 256), slice(128, 256))
        mm(S[:, 256:320], slice(0, 128), slice(0, 64))
        mm(S[:, 320:512], slice(128, 256), slice(0, 192), True).then_inc(self.s_ready.sem, 1)

    def dve_max(self, dve, b, h):
        dve.wait_ge(self.s_ready.sem, self.s_ready.value(b, h + 1))
        S, m = self.s_bank(h), self.mneg[:, h // 4, h % 4]
        dve.tensor_reduce(m[:, self.WIN, :], S[:, 0:256].rearrange("p (s c) -> p s c", s=2), AX.X, ALU.max,
                          negate=True)
        dve.tensor_reduce(m[:, self.OLD, 0:1], S[:, 256:320], AX.X, ALU.max, negate=True)
        dve.tensor_reduce(m[:, self.OLD, 1:2], S[:, 320:512], AX.X, ALU.max, negate=True)\
            .then_inc(self.max_done.sem, 1)

    def dve_shift(self, dve, b, par, u):
        dve.wait_ge(self.max_done.sem, self.max_done.value(b, 4 * u + 4))
        st, hs = self.shift_steps, slice(4 * u, 4 * u + 4)
        st.start(b * 2 + u)
        st.done(dve.tensor_scalar(self.mcl[:, u], self.mneg[:, u], CLAMP, -CLAMP, ALU.min, ALU.max))
        m = lambda a: self.mst[:, :, hs, :, a].rearrange("p s h w -> p h w s")
        st.done(dve.tensor_copy(m(0), self.mcl[:, u]))
        st.done(dve.tensor_tensor(m(1), self.mcl[:, u], m(0), ALU.subtract))
        for w in (self.OLD, self.WIN):
            last = dve.tensor_tensor(self.nm[:, par, w, :, hs], self.mst[:, :, hs, w, 0], self.mst[:, :, hs, w, 1],
                                     ALU.add)
        last.then_inc(self.m_ready.sem, 1)

    def pe_shift(self, pe, b, u):
        k = self.k
        pe.wait_ge(self.m_ready.sem, self.m_ready.value(b, u + 1))
        for s in range(2):
            last = pe.transpose(self.s_bank(1)[0:4 * self.H].bitcast(F16)[:, s * P:(s + 1) * P],
                                self.mst[:, s, :, :, :].rearrange("p h w a -> p (h w a)"), k.ident16[:, :])
        last.then_inc(self.m_ps.sem, 1)

    def dve_shifted(self, dve, b, u):
        dve.wait_ge(self.m_ps.sem, self.m_ps.value(b, u + 1))
        dve.tensor_copy(self.mT[:, u, :], self.s_bank(1)[0:4 * self.H].bitcast(F16)[:, 0:2 * P])\
            .then_inc(self.mT_ready.sem, 1)

    def pe_keys(self, pe, b, par, h):
        k, D = self.k, self.D
        if h % 4 == 0:
            pe.wait_ge(self.mT_ready.sem, self.mT_ready.value(b, h // 4 + 1))
        pe.wait_ge(self.exp_done.sem, self.exp_done.value(b, h - 1))
        T = self.t_bank(h)
        pe.matmul(T, k.identB[:, :], k.maskk_a[:, :], start=True, stop=False)
        mT = self.mT[:, h // 4, :]
        for at, n, q0, wo in ((0, 256, 0, self.WIN), (256, 192, 64, self.OLD), (448, 64, 192, self.OLD)):
            pe.matmul(T[:, at:at + n], k.select[:, 2 * h + wo, :], mT[:, q0:q0 + n], start=False, stop=False)
        for at, n, q0, k0, _ in self.KBLOCKS:
            pe.matmul(T[:, at:at + n], self.KT[0:D, par, 1, k0:k0 + P], self.QT[0:D, par, h, q0:q0 + n],
                      start=False, stop=False)
        for at, n, q0, k0, _ in self.KBLOCKS:
            last = pe.matmul(T[:, at:at + n], self.KT[:, par, 0, k0:k0 + P], self.QT[:, par, h, q0:q0 + n],
                             start=False, stop=(at == 448))
        last.then_inc(self.t_ready.sem, 1)

    def act_exp(self, act, b, h):
        act.wait_ge(self.t_ready.sem, self.t_ready.value(b, h + 1))
        act.wait_ge(self.elo_done.sem, self.elo_done.value(b, h - 1))
        act.activation(self.E32[:, h % 2, :], self.t_bank(h), ACT.Exp)
        act.wait_ge(self.pv_done.sem, self.pv_done.value(b, h - 1))
        act.activation(self.Ehi[:, h % 2, :], self.t_bank(h), ACT.Exp).then_inc(self.exp_done.sem, 1)

    def split(self, eng, b, h):
        eng.wait_ge(self.exp_done.sem, self.exp_done.value(b, h + 1))
        eng.tensor_tensor(self.Elo[:, h % 2, :], self.E32[:, h % 2, :], self.Ehi[:, h % 2, :], ALU.subtract)\
            .then_inc(self.elo_done.sem, 1)

    def pe_values(self, pe, b, par, h):
        k, D = self.k, self.D
        if h == 0:
            pe.wait_ge(self.kvlo_ready.sem, self.kvlo_ready.value(b, 1))
        pe.wait_ge(self.o_done.sem, self.o_done.value(b, h - 1))
        pe.wait_ge(self.elo_done.sem, self.elo_done.value(b, h + 1))
        O = self.o_bank(h)[:, 0:4 * (D + 1)].rearrange("p (s w d) -> p s w d", s=2, w=2)
        pe.matmul(O[:, 0, self.OLD, :], k.zero16[:, :], self.VS[:, par, 0, 0:D + 1], start=True, stop=False,
                  skip_group_check=True)
        for s, wo, at, m, p0, o in self.VBLOCKS:
            for E, v in ((self.Ehi, slice(0, D + 1)), (self.Ehi, slice(D + 1, 2 * D + 1)), (self.Elo, slice(0, D + 1))):
                last = pe.matmul(O[p0:p0 + m, s, wo, 0:v.stop - v.start], E[:, h % 2, at:at + m],
                                 self.VS[:, par, o, v], start=False, stop=True, skip_group_check=True)
        last.then_inc(self.pv_done.sem, 1)

    def act_output(self, act, b, par, h):
        act.wait_ge(self.pv_done.sem, self.pv_done.value(b, h + 1))
        act.copy(self.O[:, par, :, :, h, :].rearrange("p s w d -> p (s w) d"),
                 self.o_bank(h)[:, 0:4 * (self.D + 1)].rearrange("p (g d) -> p g d", g=4))\
            .then_inc(self.o_done.sem, 1)

    def dve_tail(self, dve, b1, par, j):
        k, H, D = self.k, self.H, self.D
        st = self.tail_steps
        nm = self.nm[:, par].rearrange("p w s h -> p w (s h)")
        L = self.O[:, par, :, :, :, D]
        sh = lambda t: t.rearrange("p (s h) -> p s h", s=2)
        if j == 0:
            st.start(b1)
            dve.tensor_tensor(self.n12[:, 0, :], nm[:, self.OLD, :], nm[:, self.WIN, :], ALU.min)
            st.done(dve.tensor_tensor(self.n12[:, 1, :], nm[:, self.WIN, :], nm[:, self.SINK, :], ALU.min))
            for a in range(2):
                last = dve.tensor_tensor(self.dx[:, 2 * a:2 * a + 2, :], bc(self.n12[:, a, :], 1, 2),
                                         nm[:, a:a + 2, :], ALU.subtract)
            last.then_inc(self.dx_ready.sem, 1)
        if j == 1:
            dve.wait_ge(self.ea_ready.sem, self.ea_ready.value(b1, 1))
            dve.wait_ge(self.o_done.sem, self.o_done.value(b1, 0))
            for i, (e, w) in enumerate(((0, self.OLD), (1, self.WIN), (2, self.WIN))):
                last = dve.tensor_tensor(sh(self.pl[:, i, :]), sh(self.ea[:, e, :]), L[:, :, w, :], ALU.mult)
            st.done(last)
            dve.tensor_tensor(self.LL[:, 0, :], self.pl[:, 0, :], self.pl[:, 1, :], ALU.add)
            st.done(dve.tensor_tensor(self.LL[:, 1, :], self.pl[:, 2, :], self.ea[:, 3, :], ALU.add))
            st.done(dve.reciprocal(self.LL[:, :, :], self.LL[:, :, :]))
            st.done(dve.tensor_tensor(self.rr[:, :, :], self.LL[:, :, :], self.gate[:, par, 1:3, :], ALU.mult))
            dve.tensor_tensor(self.co[:, 0:2, :], self.ea[:, 0:2, :], bc(self.rr[:, 0, :], 1, 2), ALU.mult)
            st.done(dve.tensor_tensor(self.co[:, 2, :], self.ea[:, 2, :], self.rr[:, 1, :], ALU.mult))
            dve.tensor_tensor(self.co[:, 1, :], self.co[:, 1, :], self.co[:, 2, :], ALU.add)\
                .then_inc(self.co_ready.sem, 1)
            dve.wait_ge(self.co_ready.sem, self.co_ready.value(b1, 1))
            for s in range(2):
                last = dve.tensor_tensor(self.mixw[:, s, :, :], self.O[:, par, s, self.WIN, :, 0:D],
                                         bc(self.co[:, 1, s * H:(s + 1) * H], 2, D), ALU.mult)
            st.done(last)
            dve.wait_ge(self.mixo_ready.sem, self.mixo_ready.value(b1, 1))
            dve.tensor_tensor(self.mixw[:, :, :, :], self.mixw[:, :, :, :], self.mixo[:, :, :, :], ALU.add)\
                .then_inc(self.mix_ready.sem, 1)
        if j == 2:
            dve.wait_ge(self.mix_ps.sem, self.mix_ps.value(b1, 1))
            dve.tensor_copy(self.mixT[:, 1, :, :].rearrange("p c q -> p (c q)"), self.X)\
                .then_inc(self.mixT_ready[1].sem, 1)
        if j == 3:
            dve.wait_ge(self.y_ps.sem, self.y_ps.value(b1, 1))
            x = k.x_all[:, bass.ds(b1 * 2, 2), :]
            dve.tensor_tensor(x, x, self.Y[:, 0:2 * P].rearrange("p (s d) -> p s d", s=2), ALU.add)\
                .then_inc(self.x_done.sem, 1)

    def act_tail(self, act, b1, par, j):
        if j == 0:
            act.wait_ge(self.dx_ready.sem, self.dx_ready.value(b1, 1))
            act.activation(self.ea[:, :, :], self.dx[:, :, :], ACT.Exp).then_inc(self.ea_ready.sem, 1)
            act.wait_ge(self.pcT_ps.sem, self.pcT_ps.value(b1, 1))
            act.copy(self.pcT[:, :], self.Y[0:self.H * self.NB, 0:2 * P]).then_inc(self.pcT_ready.sem, 1)
        if j == 2:
            act.wait_ge(self.mix_ps.sem, self.mix_ps.value(b1, 1))
            act.copy(self.mixT[:, 0, :, :].rearrange("p c q -> p (c q)"), self.Y)\
                .then_inc(self.mixT_ready[0].sem, 1)

    def pool_tail(self, pool, b1, par):
        pool.wait_ge(self.co_ready.sem, self.co_ready.value(b1, 1))
        for s in range(2):
            last = pool.tensor_tensor(self.mixo[:, s, :, :], self.O[:, par, s, self.OLD, :, 0:self.D],
                                      bc(self.co[:, 0, s * self.H:(s + 1) * self.H], 2, self.D), ALU.mult)
        last.then_inc(self.mixo_ready.sem, 1)

    def pe_tail(self, pe, b1, par, j):
        k, H = self.k, self.H
        if j == 0:
            for s in range(2):
                last = pe.transpose(self.Y[0:H * self.NB, s * P:(s + 1) * P],
                                    self.pcs[:, par, s * H:(s + 1) * H, :].rearrange("p h n -> p (h n)"),
                                    k.identF[:, :])
            last.then_inc(self.pcT_ps.sem, 1)
        if j == 2:
            pe.wait_ge(self.mix_ready.sem, self.mix_ready.value(b1, 1))
            pe.wait_ge(self.pcT_ready.sem, self.pcT_ready.value(b1, 1))
            for s in range(2):
                for c in range(4):
                    last = pe.transpose((self.Y, self.X)[s][:, c * P:(c + 1) * P],
                                        self.mixw[:, s, 2 * c:2 * c + 2, :].rearrange("p h d -> p (h d)"),
                                        k.identF[:, :])
            last.then_inc(self.mix_ps.sem, 1)
        if j == 3:
            for s in range(2):
                pe.wait_ge(self.mixT_ready[s].sem, self.mixT_ready[s].value(b1, 1))
                out = self.Y[:, s * P:(s + 1) * P]
                pe.matmul(out, self.pcT[:, s * P:(s + 1) * P], self.VW[:, par, :], start=(s == 0), stop=False,
                          skip_group_check=True)
                for c in range(4):
                    last = pe.matmul(out, self.mixT[:, s, c, :], k.Weff[:, c, :], start=False, stop=(c == 3),
                                     skip_group_check=True)
            last.then_inc(self.y_ps.sem, 1)

    def tensor(self, pe):
        for n, j, early in self.prologue():
            self.pe_front(pe, n, n % 2, j, early, first=(n == 0))
        for h in range(4):
            self.pe_scores(pe, 0, 0, h)
        self.pe_shift(pe, 0, 0)
        self.pe_keys(pe, 0, 0, 0)
        with pe.Fori(0, self.k.B // 2) as i:
            for par in range(2):
                b = i * 2 + par
                for h in range(self.H):
                    u, j = h // 4, h % 4
                    self.pe_front(pe, b + 1, 1 - par, h, False) if h == 0 else None
                    self.pe_tail(pe, b, 1 - par, h)
                    self.pe_front(pe, b + 1, 1 - par, h, False) if h > 0 else None
                    self.pe_front(pe, b + 2, par, h, True)
                    nb, npar, nu = (b, par, 1) if u == 0 else (b + 1, 1 - par, 0)
                    for x in ((), (0, 1), (2, 3), ())[j]:
                        self.pe_scores(pe, nb, npar, 4 * nu + x)
                    if j == 3:
                        self.pe_shift(pe, nb, nu)
                        self.pe_values(pe, b, par, h)
                    if h + 1 < self.H:
                        self.pe_keys(pe, b, par, h + 1)
                    else:
                        self.pe_keys(pe, b + 1, 1 - par, 0)
                    if j != 3:
                        self.pe_values(pe, b, par, h)
        pe.wait_ge(self.q_read.sem, self.q_read.value(self.k.B + 1, 2))
        for j in range(4):
            self.pe_tail(pe, self.k.B, 1, j)

    def prologue(self):
        return [(0, j, True) for j in (5, 6, 7)] + [(0, j, False) for j in range(8)] + \
            [(1, j, True) for j in (5, 6, 7)]

    def vector(self, dve):
        st, late = Steps(dve, self.early_step), Steps(dve, self.late_step)
        self.kc_steps, self.cg_steps = Steps(dve, self.kc_step), Steps(dve, self.cg_step)
        self.shift_steps, self.tail_steps = Steps(dve, self.shift_step), Steps(dve, self.tail_step)
        for n, j, early in self.prologue():
            self.dve_front(dve, st if early else late, n, n % 2, j, early)
        for h in range(4):
            self.dve_max(dve, 0, h)
        self.dve_shift(dve, 0, 0, 0)
        self.dve_shifted(dve, 0, 0)
        with dve.Fori(0, self.k.B // 2) as i:
            for par in range(2):
                b = i * 2 + par
                for h in range(self.H):
                    u, j = h // 4, h % 4
                    self.dve_tail(dve, b, 1 - par, h)
                    self.dve_front(dve, late, b + 1, 1 - par, h, False)
                    self.dve_front(dve, st, b + 2, par, h, True)
                    nb, npar, nu = (b, par, 1) if u == 0 else (b + 1, 1 - par, 0)
                    for x in ((), (0, 1), (2, 3), ())[j]:
                        self.dve_max(dve, nb, 4 * nu + x)
                    if j == 2:
                        self.dve_shift(dve, nb, npar, nu)
                    if j == 3:
                        self.dve_shifted(dve, nb, nu)
            self.k.split_expert(dve, i)
        for j in range(4):
            self.dve_tail(dve, self.k.B, 1, j)

    def scalar(self, act):
        for n, j, early in self.prologue():
            self.act_front(act, n, n % 2, j, early)
        with act.Fori(0, self.k.B // 2) as i:
            for par in range(2):
                b = i * 2 + par
                for h in range(self.H):
                    self.act_exp(act, b, h)
                    self.act_front(act, b + 1, 1 - par, h, False) if h == 0 else None
                    self.act_tail(act, b, 1 - par, h)
                    self.act_front(act, b + 1, 1 - par, h, False) if h > 0 else None
                    self.act_front(act, b + 2, par, h, True)
                    self.act_output(act, b, par, h)
        for j in range(4):
            self.act_tail(act, self.k.B, 1, j)

    def gpsimd(self, pool):
        self.rope_steps = Steps(pool, self.rope_step)
        self.pool_rstd(pool, 0)
        self.pool_rope(pool, 0)
        self.pool_rstd(pool, 1)
        with pool.Fori(0, self.k.B // 2) as i:
            for par in range(2):
                b = i * 2 + par
                for h in range(self.H):
                    self.split(pool, b, h)
                    if h == 0:
                        self.pool_rope(pool, b + 1)
                        self.pool_tail(pool, b, 1 - par)
                    if h == 5:
                        self.pool_rstd(pool, b + 2)
        self.pool_tail(pool, self.k.B, 1)


class SelfWeights:

    def self_alloc(self):
        sb, sem = self.sb, self.sem
        H, D = SelfAttention.H, SelfAttention.D
        NB = self.S // SelfAttention.CR
        self.wqc_raw = sb("wqc_raw", [P, 32], F32)
        self.wqup_raw = sb("wqup_raw", [32, H * D], F32)
        self.wkv_raw = sb("wkv_raw", [P, 2, D], F32)
        self.wog_raw = sb("wog_raw", [P, 4, D], F32)
        self.wout_raw = sb("wout_raw", [D, 2, P], F32)
        self.wqcT = sb("wqcT", [32, P], F32)
        self.wogT = sb("wogT", [D, 4, P], F32)
        self.wgate_raw = sb("wgate_raw", [P, 3], F32)
        self.gq_col = sb("gq_col", [P, 1], F32)
        self.gq_row = sb("gq_row", [P, D], F32)
        self.gk_row = sb("gk_row", [P, D], F32)
        self.gqk_sb = sb("gqk_sb", [P, D], F32)
        self.wg_sb = sb("wg_sb", [P, 3], F32)
        self.bgate_sb = sb("bgate_sb", [P, 3], F32)
        self.sink2 = sb("sink2", [P, 2 * H], F32)
        self.rope_sb = sb("rope_sb", [P, self.S // P, 64], F32)
        self.WQ_hi = sb("WQ_hi", [P, H * D], F16)
        self.WQ_lo = sb("WQ_lo", [P, H * D], F16)
        self.aKV_hi = sb("aKV_hi", [P, 2 * D], F16)
        self.aKV_lo = sb("aKV_lo", [P, 2 * D], F16)
        self.Weff = sb("Weff", [P, 4, P], F32)
        self.maskq_a = sb("maskq_a", [P, 512], BF16)
        self.maskk_a = sb("maskk_a", [P, 512], BF16)
        self.maskc = sb("maskc", [P, 2, NB], F32)
        self.headmask = sb("headmask", [P, 4, H, NB], F32)
        self.blockmean = sb("blockmean", [P, 2, NB], F16)
        self.select = sb("select", [4 * H, 2 * H, P], F16)
        self.zero16 = sb("zero16", [P, P], F16)
        self.self_loaded = sem("self_loaded")
        self.self_small = sem("self_small_loaded")
        self.self_T_ps = sem("self_T_ps")
        self.self_T = sem("self_T")
        self.self_ps = sem("self_ps")
        self.self_ready = sem("self_ready")

    SELF_LOADS, SELF_SMALL = 6, 10

    def self_sync(self, sp):
        ap, D = self.ap, SelfAttention.D
        load = lambda dst, src, s: sp.dma_start(dst, src).then_inc(s, 16)
        load(self.wqc_raw[:, :], ap["L0_attn_w_qc"], self.self_loaded)
        load(self.wog_raw[:, :, :], ap["L0_attn_w_out_group"].rearrange("g (c p) i -> p (g c) i", p=P),
             self.self_loaded)
        load(self.wqup_raw[:, :], ap["L0_attn_w_qup"], self.self_loaded)
        load(self.wout_raw[:, :, :], ap["L0_attn_w_out"].rearrange("(g i) d -> i g d", i=D), self.self_loaded)
        load(self.wkv_raw[:, 0, :], ap["L0_attn_w_k"], self.self_loaded)
        load(self.wkv_raw[:, 1, :], ap["L0_attn_w_v"], self.self_loaded)

    def self_sync_small(self, sp):
        ap, D = self.ap, SelfAttention.D
        load = lambda dst, src: sp.dma_start(dst, src).then_inc(self.self_small, 16)
        row = lambda name: ap[name].rearrange("(a d) -> a d", a=1)
        for half in range(2):
            rows = slice(half * D, (half + 1) * D)
            load(self.wgate_raw[rows, :], ap["L0_attn_w_gate"])
            load(self.gq_col[rows, :], ap["L0_attn_g_qnorm"].rearrange("(d a) -> d a", a=1))
            h = SelfAttention.H
            load(self.sink2[:, half * h:(half + 1) * h], row("L0_attn_sink_logit").broadcast_to([P, h]))
        load(self.gq_row[:, :], row("L0_attn_g_qnorm").broadcast_to([P, D]))
        load(self.gk_row[:, :], row("L0_attn_g_knorm").broadcast_to([P, D]))
        load(self.bgate_sb[:, :], row("L0_attn_b_gate").broadcast_to([P, 3]))
        load(self.rope_sb[:, :, :], ap["rope"].rearrange("(s p) d -> p s d", p=P))

    def self_pool(self, pool):
        H, D, CR = SelfAttention.H, SelfAttention.D, SelfAttention.CR
        NB = self.S // CR
        pool.memset(self.maskq_a[:, :], 0.0)
        pool.memset(self.maskk_a[:, :], 0.0)
        pool.memset(self.maskc[:, :, :], 0.0)
        pool.memset(self.headmask[:, :, :, :], 1.0)
        pool.memset(self.blockmean[:, :, :], 1.0 / CR)
        pool.memset(self.select[:, :, :], 1.0)
        pool.memset(self.zero16[:, :], 0.0)
        self.self_st.done(self.selfatt.clear(pool))

        def keep(t, base, mult, pattern, fill=NEG):
            return pool.affine_select(out=t, in_=t, compare_op=ALU.is_ge, fill=fill, base=base, pattern=pattern,
                                      channel_multiplier=mult)

        step = self.self_st.done
        q, k, hm = self.maskq_a, self.maskk_a, self.headmask
        halves = [(half, slice(half * 64, (half + 1) * 64)) for half in range(2)]
        keep(q[:, 0:128], 0, 1, [[-1, 128]])
        keep(q[:, 256:320], -64, 1, [[-1, 64]])
        keep(q[:, 320:512], 64, 1, [[-1, 192]])
        keep(k[:, 0:128], 0, -1, [[1, 128]])
        keep(k[:, 128:256], 64, -1, [[0, 2], [1, 64]])
        keep(k[:, 256:448], 0, -1, [[1, 192]])
        keep(k[:, 448:512], 0, -1, [[1, 64]])
        keep(self.maskc[:, :, :], 1 - CR, 1, [[P, 2], [-CR, NB]])
        keep(self.blockmean[:, :, :], 0, 1, [[P, 2], [-CR, NB]], 0.0)
        step(keep(self.select[:, :, :], 0, 1, [[-2, 2 * H], [0, P]], 0.0))
        keep(q[:, 0:128], 63, -1, [[1, 128]])
        keep(k[:, 0:128], 63, 1, [[-1, 128]])
        keep(k[:, 128:256], -1, 1, [[0, 2], [-1, 64]])
        keep(self.blockmean[:, :, :], CR - 1, -1, [[-P, 2], [CR, NB]], 0.0)
        step(keep(self.select[:, :, :], 1, -1, [[2, 2 * H], [0, P]], 0.0))
        for half, rows in halves:
            step(keep(q[rows, 128:256], 64, 1, [[-1, 128]]))
            step(keep(q[rows, 128:256], -1, -1, [[1, 128]]))
            for sign in (-1, 1):
                step(keep(hm[rows, :, :, :].rearrange("p c h n -> p (c h n)"), sign * half, 0,
                          [[2 * sign, 4], [-sign, H], [0, NB]], 0.0))
        pool.memset(self.zero16[:, :], 0.0).then_inc(self.consts_ready, 1)

    def self_tensor(self, pe):
        ps, D = self.ps, SelfAttention.D
        pe.wait_ge(self.self_loaded, 16 * self.SELF_LOADS)
        pe.transpose(ps[0:32, 2, 0:P], self.wqc_raw[:, :], self.identF[:, :])
        for c in range(4):
            last = pe.transpose(ps[0:D, 1, c * P:(c + 1) * P], self.wog_raw[:, c, :], self.identF[:, :])
        last.then_inc(self.self_T_ps, 1)
        pe.wait_ge(self.self_T, 2)
        pe.matmul(ps[:, 0, :], self.wqcT[:, :], self.wqup_raw[:, :], start=True, stop=True)
        for c in range(4):
            last = pe.matmul(ps[:, 3, c * P:(c + 1) * P], self.wogT[:, c, :], self.wout_raw[:, c // 2, :],
                             start=(c == 0), stop=(c == 3), skip_group_check=True)
        last.then_inc(self.self_ps, 1)

    def self_vector(self, dve):
        ps, st = self.ps, self.self_dst
        H, NB = SelfAttention.H, self.S // SelfAttention.CR
        dve.wait_ge(self.self_loaded, 16 * self.SELF_LOADS)
        raw = self.wkv_raw[:, :, :].rearrange("p a d -> p (a d)")
        st.done(dve.tensor_scalar(self.aKV_hi[:, :], raw, WS, None, ALU.mult))
        dve.scalar_tensor_tensor(self.aKV_lo[:, :], raw, WS, self.aKV_hi[:, :], ALU.mult, ALU.subtract)
        dve.wait_ge(self.self_T_ps, 1)
        dve.tensor_copy(self.wqcT[:, :], ps[0:32, 2, 0:P]).then_inc(self.self_T, 1)
        dve.tensor_copy(self.wogT[:, :, :].rearrange("p c d -> p (c d)"), ps[0:64, 1, :]).then_inc(self.self_T, 1)
        dve.wait_ge(self.self_small, 16 * self.SELF_SMALL)
        dve.wait_ge(self.consts_ready, 2)
        dve.scalar_tensor_tensor(self.gqk_sb[:, :], self.gq_row[:, :], 0.125, self.gk_row[:, :], ALU.mult, ALU.mult)
        for par in range(2):
            dve.tensor_scalar(self.selfatt.nm[:, par, SelfAttention.SINK, :, :].rearrange("p s h -> p (s h)"),
                              self.sink2[:, :], -1.0, None, ALU.mult)
        st.done(dve.tensor_scalar(self.wg_sb[:, :], self.wgate_raw[:, :], self.gq_col[:, 0:1], None, ALU.mult))
        kcg = self.selfatt.kcg
        st.done(dve.tensor_copy(kcg[:, 0, NB:], self.wg_sb[:, :]))
        dve.tensor_tensor(kcg[:, 1, NB:], self.wg_sb[:, :], kcg[:, 0, NB:], ALU.subtract)
        dve.wait_ge(self.self_ps, 1)
        st.done(dve.tensor_scalar(self.WQ_hi[:, :], ps[:, 0, :], WS, None, ALU.mult))
        dve.tensor_copy(self.Weff[:, :, :].rearrange("p c d -> p (c d)"), ps[:, 3, :])
        dve.scalar_tensor_tensor(self.WQ_lo[:, :], ps[:, 0, :], WS, self.WQ_hi[:, :], ALU.mult, ALU.subtract)\
            .then_inc(self.self_ready, 1)


class Layer(SelfWeights):

    EPS = 1e-5

    def __init__(self, nc, ctx, ap):
        self.nc, self.ctx, self.ap = nc, ctx, ap
        self.scope = ctx
        self.B, self.S, _ = ap["x"].shape
        self.tiles = self.B * self.S // P
        self.tile0 = self.S // P
        self.after = 4
        self.W1, self.W2 = ap["L0_ffn_W1"], ap["L0_ffn_W2"]
        self.E = self.W1.shape[0]
        C = self.W1.shape[2] // P
        self.C = C
        self.ps = ctx.enter_context(nc.psum_tensor("ps", [P, 8, 512], F32))
        sb = self.sb
        self.x_all = sb("x_all", [P, self.tile0 + self.tiles + self.after, P], F32)
        self.x_v = ap["x"].rearrange("b (s p) d -> p (b s) d", p=P)
        self.out_v = ap["out"].rearrange("b (s p) d -> p (b s) d", p=P)
        self.ffn_raw = sb("ffn_raw", [P, 2, C * P], F32)
        self.W1hi = sb("W1hi", [P, self.E, C * P], F16)
        self.W1lo = sb("W1lo", [P, self.E, C * P], F16)
        self.W2hi = sb("W2hi", [P, self.E, C, P], F16)
        self.W2lo = sb("W2lo", [P, self.E, C, P], F16)
        self.b1_raw = sb("b1_raw", [self.E * C, P], F32)
        self.b1_sb = sb("b1_sb", [P, self.E * C], F32)
        self.Wg_sb = sb("Wg_sb", [P, self.E], F32)
        self.bg_sb = sb("bg_sb", [P, self.E], F32)
        self.b2_raw = sb("b2_raw", [32, P], F32)
        self.b2_rest = sb("b2_rest", [32, P], F32)
        self.b2parts = sb("b2parts", [32, 3, P], BF16)
        self.identF = sb("identF", [P, P], F32)
        self.identB = sb("identB", [P, P], BF16)
        self.ident16 = sb("ident16", [P, P], F16)
        self.pick = sb("pick", [32, self.E, P], BF16)
        self.gp = sb("f_gp", [P, self.C * P // P, 32], BF16)
        self.iota8 = sb("iota8", [P, 8], F32)
        self.minus_half = sb("minus_half", [P, 64], F32)
        self.spare = sb("spare", [P, 2], F32)
        self.euler = sb("euler", [P, 64], F32)
        sem = self.sem
        self.pool_step = Count(sem("pool_setup_steps"), 0)
        self.dve_step = Count(sem("dve_setup_steps"), 0)
        self.consts_ready = sem("consts_ready")
        self.x_loaded = [sem(f"x_loaded{i}") for i in range(2)]
        self.ffn_loaded = sem("ffn_loaded")
        self.small_loaded = sem("small_loaded")
        self.ffn_split = Count(sem("ffn_split"), 1, 1)
        self.split_step = Count(sem("ffn_split_steps"), 1)
        self.b2_split = sem("b2_split")
        self.b2_zero = sem("b2_zero")
        self.b1T_ready = sem("b1T_ready")
        self.b1_ready = sem("b1_ready")
        B, H = self.B, P
        self.ctx_all = sb("ctx_all", [ap["ctx_1024"].shape[1], B + 1, P], F32)
        self.xw_raw = sb("xw_raw", [P, 3, P], F32)
        self.xw_hi = sb("xw_hi", [P, 3, P], F16)
        self.xw_lo = sb("xw_lo", [P, 3, P], F16)
        self.Wq_hi, self.Wq_lo = self.xw_hi[:, 0, :], self.xw_lo[:, 0, :]
        self.Wkv_hi, self.Wkv_lo = (w[:, 1:3, :].rearrange("p a d -> p (a d)") for w in (self.xw_hi, self.xw_lo))
        self.Wout_sb = sb("Wout_sb", [P, P], F32)
        self.bout_sb = sb("bout_sb", [1, P], F32)
        self.one_row = sb("one_row", [1, P], F32)
        self.maskq_x = sb("maskq_x", [P, 512], BF16)
        self.maskk_x = sb("maskk_x", [P, 512], BF16)
        self.x_weights_loaded = sem("x_weights_loaded")
        self.ctx_loaded = sem("ctx_loaded")
        self.x_split = sem("x_split")
        self.x_used = sem("x_phase_done")
        self.cross = Cross(self)
        with ExitStack() as self.scope:
            self.self_alloc()
            self.selfatt = SelfAttention(self)
        with ExitStack() as self.scope:
            self.cross.alloc()
        self.scope = ctx
        self.experts = Experts(self)

    def sb(self, name, shape, dt):
        return self.scope.enter_context(self.nc.sbuf_tensor(name, shape, dt))

    def sem(self, name):
        return self.ctx.enter_context(self.nc.semaphore(name))

    SMALL = 6

    def sync_setup(self, sp):
        ap, first = self.ap, 4
        t0 = self.tile0
        self.self_sync(sp)
        sp.dma_start(self.x_all[:, t0:t0 + first, :], self.x_v[:, 0:first, :]).then_inc(self.x_loaded[0], 16)
        sp.dma_start(self.x_all[:, t0 + first:t0 + self.tiles, :], self.x_v[:, first:self.tiles, :])\
            .then_inc(self.x_loaded[1], 16)
        self.self_sync_small(sp)
        sp.dma_start(self.b1_raw[:, :], ap["L0_ffn_b1"].rearrange("e (c p) -> (e c) p", p=P))\
            .then_inc(self.small_loaded, 16)
        sp.dma_start(self.Wg_sb[:, :], ap["L0_ffn_Wg"]).then_inc(self.small_loaded, 16)
        sp.dma_start(self.bg_sb[:, :], ap["L0_ffn_bg"].rearrange("(a e) -> a e", a=1).broadcast_to([P, self.E]))\
            .then_inc(self.small_loaded, 16)
        sp.dma_start(self.xw_raw[:, 0, :], ap["L0_xattn_Wq"]).then_inc(self.x_weights_loaded, 16)
        sp.dma_start(self.xw_raw[:, 1:3, :].rearrange("p a d -> p (a d)"), ap["L0_xattn_Wkv"])\
            .then_inc(self.x_weights_loaded, 16)
        sp.dma_start(self.Wout_sb[:, :], ap["L0_xattn_Wout"]).then_inc(self.x_weights_loaded, 16)
        sp.dma_start(self.bout_sb[:, :], ap["L0_xattn_bout"].rearrange("(a d) -> a d", a=1))\
            .then_inc(self.x_weights_loaded, 16)
        sp.dma_start(self.ctx_all[:, 0:self.B, :], ap["ctx_1024"].rearrange("b m d -> m b d"))\
            .then_inc(self.ctx_loaded, 16)
        sp.wait_ge(self.b2_zero, 1)
        for m in range(3):
            sp.dma_start(self.b2_raw[m * self.E:(m + 1) * self.E, :], ap["L0_ffn_b2"])\
                .then_inc(self.small_loaded, 16)
        self.sync_experts(sp)

    def sync_experts(self, sp):
        with sp.Fori(0, self.E) as e:
            sp.wait_ge(self.ffn_split.sem, self.ffn_split.value(e, 0))
            sp.dma_start(self.ffn_raw[:, 0, :], self.W1[e]).then_inc(self.ffn_loaded, 16)
            sp.dma_start(self.ffn_raw[:, 1, :].rearrange("p (c d) -> p c d", d=P),
                         self.W2[e].rearrange("(c p) d -> p c d", p=P)).then_inc(self.ffn_loaded, 16)

    def split_expert(self, dve, e):
        dve.wait_ge(self.ffn_loaded, e * 32 + 32)
        st = Steps(dve, self.split_step)
        st.start(e)
        W2hi, W2lo = (w[:, e, :, :].rearrange("p c d -> p (c d)") for w in (self.W2hi, self.W2lo))
        dve.tensor_scalar(self.W1hi[:, e, :], self.ffn_raw[:, 0, :], WS, None, ALU.mult)
        st.done(dve.tensor_scalar(W2hi, self.ffn_raw[:, 1, :], WS, None, ALU.mult))
        dve.scalar_tensor_tensor(self.W1lo[:, e, :], self.ffn_raw[:, 0, :], WS, self.W1hi[:, e, :],
                                 ALU.mult, ALU.subtract)
        dve.scalar_tensor_tensor(W2lo, self.ffn_raw[:, 1, :], WS, W2hi, ALU.mult, ALU.subtract)\
            .then_inc(self.ffn_split.sem, 1)

    def gpsimd_setup(self, pool):
        st = Steps(pool, self.pool_step)
        pool.memset(self.b2_raw[:, :], 0.0).then_inc(self.b2_zero, 1)
        pool.memset(self.x_all[:, 0:self.tile0, :], 0.0)
        pool.memset(self.x_all[:, self.tile0 + self.tiles:, :], 0.0)
        pool.memset(self.minus_half[:, :], -0.5)
        pool.memset(self.spare[:, :], 0.0)
        pool.memset(self.euler[:, :], 2.718281828459045)
        pool.memset(self.gp[:, :, :], 0.0)
        pool.memset(self.ctx_all[:, self.B:, :], 0.0)
        pool.memset(self.one_row[:, :], 1.0)
        pool.memset(self.maskq_x[:, :], 0.0)
        pool.memset(self.maskk_x[:, :], 0.0)
        st.done(self.cross.clear(pool))
        st.done(self.cross.ones(pool))
        pool.memset(self.identF[:, :], 0.0)
        st.done(pool.memset(self.pick[:, :, :], 0.0))
        st.done(pool.affine_select(out=self.identF[:, :], in_=self.identF[:, :], compare_op=ALU.not_equal, fill=1.0,
                                   base=0, pattern=[[-1, P]], channel_multiplier=1))
        pool.tensor_copy(self.ident16[:, :], self.identF[:, :])
        for m in range(3):
            st.done(pool.affine_select(out=self.pick[:, :, :], in_=self.pick[:, :, :], compare_op=ALU.not_equal,
                                       fill=1.0 / WS, base=-m * self.E, pattern=[[-1, self.E], [0, P]],
                                       channel_multiplier=1))
        def masked(mask, at, n, base, step, mult):
            return pool.affine_select(out=mask[:, at:at + n], in_=mask[:, at:at + n], compare_op=ALU.is_ge, fill=NEG,
                                      base=base, pattern=[[step, n]], channel_multiplier=mult)

        for at, n, base in ((0, 192, 64), (192, 320, 192)):
            masked(self.maskq_x, at, n, base, -1, 1)
        for at, n, base in ((0, 256, 64), (256, 192, 0), (448, 64, 0)):
            masked(self.maskk_x, at, n, base, 1, -1)
        pool.iota(self.iota8[:, :], pattern=[[1, 8]], base=0, channel_multiplier=0,
                  allow_small_or_imprecise_dtypes=True)
        pool.tensor_copy(self.identB[:, :], self.identF[:, :]).then_inc(self.consts_ready, 1)
        self.self_st = st
        self.self_pool(pool)
        self.selfatt.credits(pool)
        pool.sem_inc(self.ffn_split.sem, self.ffn_split.credit)
        self.cross.credits(pool)
        self.experts.credits(pool)

    def vector_setup(self, dve):
        st = self.self_dst = Steps(dve, self.dve_step)
        self.self_vector(dve)
        dve.wait_ge(self.x_weights_loaded, 16 * 4)
        st.done(dve.tensor_scalar(self.xw_hi[:, :, :], self.xw_raw[:, :, :], WS, None, ALU.mult))
        dve.scalar_tensor_tensor(self.xw_lo[:, :, :], self.xw_raw[:, :, :], WS, self.xw_hi[:, :, :],
                                 ALU.mult, ALU.subtract).then_inc(self.x_split, 1)
        dve.wait_ge(self.ctx_loaded, 16)
        dve.wait_ge(self.small_loaded, 16 * self.SMALL)
        st.done(dve.tensor_copy(self.b2parts[:, 0, :], self.b2_raw[:, :]))
        st.done(dve.tensor_tensor(self.b2_rest[:, :], self.b2_raw[:, :], self.b2parts[:, 0, :], ALU.subtract))
        st.done(dve.tensor_copy(self.b2parts[:, 1, :], self.b2_rest[:, :]))
        dve.tensor_tensor(self.b2parts[:, 2, :], self.b2_rest[:, :], self.b2parts[:, 1, :], ALU.subtract)\
            .then_inc(self.b2_split, 1)
        dve.wait_ge(self.b1T_ready, 1)
        dve.tensor_copy(self.b1_sb[:, :], self.ps[:, 7, 0:self.E * self.C]).then_inc(self.b1_ready, 1)
        for s in self.x_loaded:
            dve.wait_ge(s, 16)
        dve.wait_ge(self.consts_ready, 1)

    def tensor_setup(self, pe):
        pe.wait_ge(self.consts_ready, 1)
        pe.wait_ge(self.small_loaded, 16 * self.SMALL)
        self.self_tensor(pe)
        pe.wait_ge(self.self_ready, 1)
        pe.wait_ge(self.consts_ready, 2)
        n = self.E * self.C
        pe.transpose(self.ps[:, 7, 0:n], self.b1_raw[:, :], self.identF[0:n, 0:n]).then_inc(self.b1T_ready, 1)
        pe.wait_ge(self.b1_ready, 1)
        pe.wait_ge(self.b2_split, 1)
        pe.wait_ge(self.x_split, 1)
        pe.wait_ge(self.x_weights_loaded, 16 * 4)

    def scalar_setup(self, act):
        act.wait_ge(self.b1_ready, 1)

    def build(self):
        block = self.ctx.enter_context(self.nc.Block())

        @block.sync
        def _(sp):
            self.sync_setup(sp)
            self.experts.sync(sp)

        @block.gpsimd
        def _(pool):
            self.gpsimd_setup(pool)
            self.selfatt.gpsimd(pool)
            self.cross.gpsimd(pool)
            self.experts.gpsimd(pool)

        @block.vector
        def _(dve):
            self.vector_setup(dve)
            self.selfatt.vector(dve)
            dve.wait_ge(self.selfatt.x_done.sem, self.selfatt.x_done.value(self.B, 1))
            self.cross.vector(dve)
            dve.wait_ge(self.cross.x_done.sem, self.cross.x_done.value(self.B, 1))
            self.experts.vector(dve)

        @block.scalar
        def _(act):
            self.scalar_setup(act)
            self.selfatt.scalar(act)
            self.cross.scalar(act)
            self.experts.scalar(act)

        @block.tensor
        def _(pe):
            self.tensor_setup(pe)
            self.selfatt.tensor(pe)
            self.cross.tensor(pe)
            pe.wait_ge(self.ffn_split.sem, self.ffn_split.value(self.E, 0))
            self.experts.tensor(pe)


def decoder_layer(nc, ap):
    with ExitStack() as ctx:
        Layer(nc, ctx, ap).build()


_OUT = ((16, 256, 128), 'float32')


def rope_table(positions, half, theta=10000.0):
    import numpy as np
    inv = np.float32(1.0) / np.float32(theta) ** (np.arange(half, dtype=np.float32) * np.float32(2.0)
                                                  / np.float32(2 * half))
    ang = np.arange(positions, dtype=np.float32)[:, None] * inv[None, :]
    cos, sin = np.cos(ang), np.sin(ang)
    return np.concatenate([cos, cos, -sin, sin], axis=1)


def kernel(**inputs):
    import numpy as _np
    import concourse.bacc as _bacc
    from concourse import mybir as _mybir
    from concourse.bass_utils import run_bass_kernel_spmd as _run

    nc = _bacc.Bacc("TRN2", target_bir_lowering=False, num_devices=1)
    arrays, ap = {}, {}
    inputs["rope"] = rope_table(inputs["x"].shape[1], 16)
    for name, value in inputs.items():
        a = _np.ascontiguousarray(value)
        arrays[f"in_{name}_dram"] = a
        ap[name] = nc.dram_tensor(f"in_{name}_dram", a.shape, _mybir.dt.from_np(a.dtype), kind="ExternalInput").ap()
    ap["out"] = nc.dram_tensor("out_dram", _OUT[0], _mybir.dt.from_np(_np.dtype(_OUT[1])), kind="ExternalOutput").ap()
    decoder_layer(nc, ap)
    r = _run(nc, [arrays], core_ids=[0])
    return r.results[0]["out_dram"]
```

```python
from contextlib import ExitStack

import concourse.bass as bass
from concourse import mybir

F32 = mybir.dt.float32
F16 = mybir.dt.float16
BF16 = mybir.dt.bfloat16
U32 = mybir.dt.uint32
ALU = mybir.AluOpType
ACT = mybir.ActivationFunctionType
AX = mybir.AxisListType

P = 128
NEG = -1e30
WS = 64.0
CLAMP = 60000.0


class Count:

    def __init__(self, sem, per, credit=0):
        self.sem, self.per, self.credit = sem, per, credit

    def value(self, rounds, k):
        return rounds * self.per + (k + self.credit)


class Steps:

    def __init__(self, eng, count):
        self.eng, self.count, self.rounds, self.k = eng, count, 0, 0

    def start(self, rounds):
        self.rounds, self.k = rounds, 0

    def done(self, ins):
        self.k += 1
        ins.then_inc(self.count.sem, 1)
        self.eng.wait_ge(self.count.sem, self.count.value(self.rounds, self.k))

    def carry(self, spare):
        self.eng.tensor_copy(spare[:, 1:2], spare[:, 0:1])

    def finish(self):
        assert self.k == self.count.per, f"{self.k} steps in a round, not {self.count.per}"


def bc(ap, axis, n):
    ap = ap.unsqueeze(axis)
    shape = list(ap.shape)
    shape[axis] = n
    return ap.broadcast_to(shape)


class Experts:

    TOK = 512
    T = TOK // P
    LEAD = 2
    HB = 4
    DVE_STEPS = 20

    def __init__(self, k):
        self.k = k
        sb, sem = k.sb, k.sem
        self.E, self.F, self.H = k.E, P, k.W1.shape[2]
        self.C = self.H // P
        self.J = self.E * self.C
        self.G = k.tiles // self.T
        self.xn = sb("f_xn", [P, self.T, P], F32)
        self.x32 = sb("f_x32", [P, self.TOK], F32)
        self.xhi = sb("f_xhi", [P, 2, self.TOK], F16)
        self.xlo = sb("f_xlo", [P, 2, self.TOK], F16)
        self.stats = sb("f_stats", [P, self.T, 6], F32)
        self.mv = sb("f_mv", [P, self.T, 2], F32)
        self.ve = sb("f_ve", [P, self.T], F32)
        self.rstd = sb("f_rstd", [P, self.T], F32)
        E, T = self.E, self.T
        self.lg = sb("f_lg", [P, T, E], F32)
        self.mx = sb("f_mx", [P, T], F32)
        self.ex = sb("f_ex", [P, T, E], F32)
        self.z = sb("f_z", [P, T], F32)
        self.zr = sb("f_zr", [P, T], F32)
        self.pr = sb("f_pr", [P, T, E], F32)
        self.top = sb("f_top", [P, T, 8], F32)
        self.topi = sb("f_topi", [P, T, 8], U32)
        self.topf = sb("f_topf", [P, T, 8], F32)
        self.m1 = sb("f_m1", [P, T, E], F32)
        self.m2 = sb("f_m2", [P, T, E], F32)
        self.gs = sb("f_gs", [P, T, E], F32)
        self.gp = k.gp
        self.gT = sb("f_gT", [32, 2, self.TOK], BF16)
        self.Gb = sb("f_Gb", [P, 2, E, self.TOK], F32)
        self.h32 = sb("f_h32", [P, 2, self.TOK], F32)
        self.hhi = sb("f_hhi", [P, self.HB, self.TOK], F16)
        self.hlo = sb("f_hlo", [P, self.HB, self.TOK], F16)
        self.acc = sb("f_acc", [P, self.TOK], F32)
        self.tmp = sb("f_tmp", [P, self.TOK], F32)
        self.ost = sb("f_ost", [P, 2, T, P], F32)
        S = lambda name, per, credit=0: Count(sem("f_" + name), per, credit)
        self.h_ready = S("h_ready", self.J)
        self.gelu_done = S("gelu_done", self.J, self.HB)
        self.lo_done = S("lo_done", self.J, 2)
        self.h_used = S("h_used", self.J, self.HB)
        self.o_used = S("o_used", E, 2)
        self.acc_ready = S("acc_ready", 1)
        self.out_ready = S("out_ready", 1)
        self.out_sum = S("out_sum", 1, 1)
        self.stored = [S(f"stored{i}", 16, 16) for i in range(2)]
        self.ve_ready = S("ve_ready", 1)
        self.rstd_ready = S("rstd_ready", 1)
        self.xn_ready = S("xn_ready", 1)
        self.xT_ready = S("xT_ready", 1)
        self.xhi_ready = S("xhi_ready", 1)
        self.xlo_ready = S("xlo_ready", 1)
        self.lg_ready = S("lg_ready", 1)
        self.shift_ready = S("shift_ready", 1)
        self.ex_ready = S("ex_ready", 1)
        self.gp_ready = S("gp_ready", 1)
        self.gpT_ready = S("gpT_ready", 1)
        self.gT_ready = S("gT_ready", 1)
        self.Gps_ready = S("Gps_ready", E)
        self.Gb_ready = S("Gb_ready", E, 1)
        self.steps = S("dve_steps", self.DVE_STEPS)
        self.M0, self.M1 = k.ps[:, 6, :], k.ps[:, 7, :]

    def h_bank(self, j):
        return self.k.ps[:, j % self.HB, :]

    def o_bank(self, e):
        return self.k.ps[:, 4 + e % 2, :]

    def credits(self, eng):
        for s in (self.gelu_done, self.lo_done, self.h_used, self.o_used, self.out_sum, self.Gb_ready,
                  *self.stored):
            eng.sem_inc(s.sem, s.credit)

    def pe_prep(self, pe, n, par, j):
        k = self.k
        if j == 4:
            pe.wait_ge(self.xn_ready.sem, self.xn_ready.value(n, 1))
            pe.wait_ge(self.Gb_ready.sem, self.Gb_ready.value(n, 0))
            for i in range(self.T):
                last = pe.transpose(self.M0[:, i * P:(i + 1) * P], self.xn[:, i, :], k.identF[:, :])
            last.then_inc(self.xT_ready.sem, 1)
        if j == 7:
            pe.wait_ge(self.xlo_ready.sem, self.xlo_ready.value(n, 1))
            for i in range(self.T):
                last = pe.matmul(self.M0[:, i * self.E:(i + 1) * self.E], self.x32[:, i * P:(i + 1) * P],
                                 k.Wg_sb[:, :], start=True, stop=True)
            last.then_inc(self.lg_ready.sem, 1)
        if j == 18:
            pe.wait_ge(self.gp_ready.sem, self.gp_ready.value(n, 1))
            for i in range(self.T):
                last = pe.transpose(self.M0[0:32, :].bitcast(BF16)[:, i * P:(i + 1) * P], self.gp[:, i, :],
                                    k.identB[:, :])
            last.then_inc(self.gpT_ready.sem, 1)
        if 20 <= j < 20 + self.E:
            e = j - 20
            if e == 0:
                pe.wait_ge(self.gT_ready.sem, self.gT_ready.value(n, 1))
            else:
                pe.wait_ge(self.Gb_ready.sem, self.Gb_ready.value(n, e))
            pe.matmul(self.M0, k.pick[:, e, :], self.gT[:, par, :], start=True,
                      stop=True).then_inc(self.Gps_ready.sem, 1)

    def pe_first(self, pe, g, par, j):
        k, e, c = self.k, j // self.C, j % self.C
        w = slice(c * P, (c + 1) * P)
        if j == 0:
            pe.wait_ge(self.xlo_ready.sem, self.xlo_ready.value(g, 1))
        pe.wait_ge(self.gelu_done.sem, self.gelu_done.value(g, j - self.HB + 1))
        H = self.h_bank(j)
        pe.matmul(H, k.W1hi[:, e, w], self.xhi[:, par, :], start=True, stop=False)
        pe.matmul(H, k.W1hi[:, e, w], self.xlo[:, par, :], start=False, stop=False)
        pe.matmul(H, k.W1lo[:, e, w], self.xhi[:, par, :], start=False, stop=True)\
            .then_inc(self.h_ready.sem, 1)

    def pe_second(self, pe, g, j):
        k, e, c = self.k, j // self.C, j % self.C
        if c == 0:
            pe.wait_ge(self.o_used.sem, self.o_used.value(g, e - 1))
        pe.wait_ge(self.gelu_done.sem, self.gelu_done.value(g, j + 1))
        O, b = self.o_bank(e), j % self.HB
        pe.matmul(O, k.W2hi[:, e, c, :], self.hhi[:, b, :], start=(c == 0), stop=False)
        pe.matmul(O, k.W2lo[:, e, c, :], self.hhi[:, b, :], start=False, stop=False)
        pe.wait_ge(self.lo_done.sem, self.lo_done.value(g, j + 1))
        last = pe.matmul(O, k.W2hi[:, e, c, :], self.hlo[:, b, :], start=False, stop=(c == self.C - 1))
        last.then_inc(self.h_used.sem, 1)

    def tensor(self, pe):
        k = self.k
        for j in range(self.J):
            self.pe_prep(pe, 0, 0, j)
        for j in range(self.LEAD):
            self.pe_first(pe, 0, 0, j)
        with pe.Fori(0, self.G // 2) as i:
            for par in range(2):
                g = i * 2 + par
                for j in range(self.J):
                    self.pe_prep(pe, g + 1, 1 - par, j)
                    if j + self.LEAD < self.J:
                        self.pe_first(pe, g, par, j + self.LEAD)
                    else:
                        self.pe_first(pe, g + 1, 1 - par, j + self.LEAD - self.J)
                    self.pe_second(pe, g, j)
                pe.wait_ge(self.out_sum.sem, self.out_sum.value(g, 0))
                for t in range(self.T):
                    for m in range(3):
                        pe.matmul(self.M1[:, t * P:(t + 1) * P], self.gT[:, par, t * P:(t + 1) * P],
                                  k.b2parts[:, m, :], start=(t == 0 and m == 0), stop=False,
                                  skip_group_check=True)
                pe.wait_ge(self.acc_ready.sem, self.acc_ready.value(g, 1))
                for t in range(self.T):
                    last = pe.matmul(self.M1[:, t * P:(t + 1) * P], self.acc[:, t * P:(t + 1) * P],
                                     k.identF[:, :], start=False, stop=True, skip_group_check=True)
                last.then_inc(self.out_ready.sem, 1)

    def act_prep(self, act, n, par, j):
        if j == 5:
            act.wait_ge(self.xT_ready.sem, self.xT_ready.value(n, 1))
            act.copy(self.xhi[:, par, :], self.M0)
            act.copy(self.x32[:, :], self.M0).then_inc(self.xhi_ready.sem, 1)
        if j == 19:
            act.wait_ge(self.gpT_ready.sem, self.gpT_ready.value(n, 1))
            act.copy(self.gT[:, par, :], self.M0[0:32, :].bitcast(BF16)[:, 0:self.TOK])\
                .then_inc(self.gT_ready.sem, 1)
        if 20 <= j < 20 + self.E:
            e = j - 20
            act.wait_ge(self.Gps_ready.sem, self.Gps_ready.value(n, e + 1))
            act.copy(self.Gb[:, par, e, :], self.M0).then_inc(self.Gb_ready.sem, 1)

    def scalar(self, act):
        k = self.k
        for j in range(self.J):
            self.act_prep(act, 0, 0, j)
        with act.Fori(0, self.G // 2) as i:
            for par in range(2):
                g = i * 2 + par
                for j in range(self.J):
                    act.wait_ge(self.h_ready.sem, self.h_ready.value(g, j + 1))
                    act.wait_ge(self.lo_done.sem, self.lo_done.value(g, j - 1))
                    act.activation(self.h32[:, j % 2, :], self.h_bank(j), ACT.Gelu_apprx_tanh,
                                   bias=k.b1_sb[:, j:j + 1], scale=1.0 / WS)
                    act.wait_ge(self.h_used.sem, self.h_used.value(g, j - self.HB + 1))
                    act.activation(self.hhi[:, j % self.HB, :], self.h_bank(j), ACT.Gelu_apprx_tanh,
                                   bias=k.b1_sb[:, j:j + 1], scale=1.0 / WS)\
                        .then_inc(self.gelu_done.sem, 1)
                    self.act_prep(act, g + 1, 1 - par, j)

    def gpsimd(self, pool):
        k = self.k
        with pool.Fori(0, self.G + 1) as n:
            pool.wait_ge(self.ve_ready.sem, self.ve_ready.value(n, 1))
            pool.tensor_tensor(self.rstd[:, :], self.ve[:, :], k.minus_half[:, 0:self.T], ALU.pow)\
                .then_inc(self.rstd_ready.sem, 1)
            pool.wait_ge(self.shift_ready.sem, self.shift_ready.value(n, 1))
            pool.tensor_tensor(self.ex[:, :, :].rearrange("p t e -> p (t e)"), k.euler[:, 0:self.T * self.E],
                               self.lg[:, :, :].rearrange("p t e -> p (t e)"), ALU.pow)\
                .then_inc(self.ex_ready.sem, 1)

    def dve_prep(self, dve, st, n, par, j):
        k, T = self.k, self.T
        if j == 0:
            st.start(n)
            for i in range(T):
                last = dve.bn_stats(self.stats[:, i, :], k.x_all[:, k.tile0 + n * T + i, :])
            st.done(last)
            st.carry(k.spare)
            for i in range(T):
                last = dve.bn_aggr(self.mv[:, i, :], self.stats[:, i, :])
            st.done(last)
            dve.tensor_scalar(self.ve[:, :], self.mv[:, :, 1], k.EPS, None, ALU.add)\
                .then_inc(self.ve_ready.sem, 1)
        if j == 3:
            dve.wait_ge(self.rstd_ready.sem, self.rstd_ready.value(n, 1))
            for i in range(T):
                last = dve.tensor_scalar(self.xn[:, i, :], k.x_all[:, k.tile0 + n * T + i, :],
                                         self.mv[:, i, 0:1], self.rstd[:, i:i + 1], ALU.subtract, ALU.mult)
            last.then_inc(self.xn_ready.sem, 1)
        if j == 6:
            dve.wait_ge(self.xhi_ready.sem, self.xhi_ready.value(n, 1))
            dve.tensor_tensor(self.xlo[:, par, :], self.M0, self.xhi[:, par, :], ALU.subtract)\
                .then_inc(self.xlo_ready.sem, 1)
        if j == 8:
            dve.wait_ge(self.lg_ready.sem, self.lg_ready.value(n, 1))
            st.done(dve.tensor_tensor(self.lg[:, :, :], self.M0[:, 0:T * self.E].rearrange("p (t e) -> p t e", t=T),
                                      bc(k.bg_sb[:, :], 1, T), ALU.add))
            st.done(dve.tensor_reduce(self.mx[:, :], self.lg[:, :, :], AX.X, ALU.max))
            dve.tensor_tensor(self.lg[:, :, :], self.lg[:, :, :], bc(self.mx[:, :], 2, self.E), ALU.subtract)\
                .then_inc(self.shift_ready.sem, 1)
        if j == 11:
            dve.wait_ge(self.ex_ready.sem, self.ex_ready.value(n, 1))
            st.done(dve.tensor_reduce(self.z[:, :], self.ex[:, :, :], AX.X, ALU.add))
            st.done(dve.reciprocal(self.zr[:, :], self.z[:, :]))
            st.done(dve.tensor_tensor(self.pr[:, :, :], self.ex[:, :, :], bc(self.zr[:, :], 2, self.E), ALU.mult))
        if j == 12:
            for i in range(T):
                last = dve.max(self.top[:, i, :], self.pr[:, i, :])
            st.done(last)
            st.carry(k.spare)
            for i in range(T):
                last = dve.max_index(self.topi[:, i, :], self.top[:, i, :], self.pr[:, i, :])
            st.done(last)
        if j == 14:
            st.done(dve.tensor_copy(self.topf[:, :, :], self.topi[:, :, :]))
            for i in range(T):
                dve.tensor_scalar(self.m1[:, i, :], k.iota8[:, :], self.topf[:, i, 0:1], None, ALU.is_equal)
                last = dve.tensor_scalar(self.m2[:, i, :], k.iota8[:, :], self.topf[:, i, 1:2], None, ALU.is_equal)
            st.done(last)
            st.done(dve.tensor_tensor(self.m1[:, :, :], self.m1[:, :, :], self.m2[:, :, :], ALU.add))
            st.done(dve.tensor_tensor(self.pr[:, :, :], self.pr[:, :, :], self.m1[:, :, :], ALU.mult))
        if j == 15:
            st.done(dve.tensor_reduce(self.z[:, :], self.pr[:, :, :], AX.X, ALU.add))
            st.done(dve.tensor_scalar(self.z[:, :], self.z[:, :], 1e-8, None, ALU.add))
            st.done(dve.reciprocal(self.zr[:, :], self.z[:, :]))
            st.done(dve.tensor_tensor(self.gs[:, :, :], self.pr[:, :, :], bc(self.zr[:, :], 2, self.E), ALU.mult))
        if j == 16:
            E = self.E
            g1, g2, g3 = (self.gp[:, :, m * E:(m + 1) * E] for m in range(3))
            st.done(dve.tensor_copy(g1, self.gs[:, :, :]))
            st.done(dve.tensor_tensor(self.m1[:, :, :], self.gs[:, :, :], g1, ALU.subtract))
            st.done(dve.tensor_copy(g2, self.m1[:, :, :]))
            dve.tensor_tensor(g3, self.m1[:, :, :], g2, ALU.subtract).then_inc(self.gp_ready.sem, 1)
            st.finish()

    def dve_weigh(self, dve, g, par, e):
        dve.wait_ge(self.h_used.sem, self.h_used.value(g, (e + 1) * self.C))
        if e == 0:
            dve.wait_ge(self.Gb_ready.sem, self.Gb_ready.value(g, self.E))
        out = self.acc if e == 0 else self.tmp
        dve.tensor_tensor(out[:, :], self.o_bank(e), self.Gb[:, par, e, :], ALU.mult)\
            .then_inc(self.o_used.sem, 1)
        if e > 0:
            dve.wait_ge(self.o_used.sem, self.o_used.value(g, e + 1))
            last = dve.tensor_tensor(self.acc[:, :], self.acc[:, :], self.tmp[:, :], ALU.add)
            if e == self.E - 1:
                last.then_inc(self.acc_ready.sem, 1)

    def vector(self, dve):
        k = self.k
        st = Steps(dve, self.steps)
        for j in range(self.J):
            self.dve_prep(dve, st, 0, 0, j)
        with dve.Fori(0, self.G // 2) as i:
            for par in range(2):
                g = i * 2 + par
                for j in range(self.J + 1):
                    if j < self.J:
                        dve.wait_ge(self.gelu_done.sem, self.gelu_done.value(g, j + 1))
                        dve.tensor_tensor(self.hlo[:, j % self.HB, :], self.h32[:, j % 2, :],
                                          self.hhi[:, j % self.HB, :], ALU.subtract)\
                            .then_inc(self.lo_done.sem, 1)
                    if j and j % self.C == 0:
                        self.dve_weigh(dve, g, par, j // self.C - 1)
                    if j < self.J:
                        self.dve_prep(dve, st, g + 1, 1 - par, j)
                dve.wait_ge(self.out_ready.sem, self.out_ready.value(g, 1))
                dve.wait_ge(self.stored[par].sem, self.stored[par].value(i, 0))
                dve.tensor_tensor(self.ost[:, par, :, :], k.x_all[:, bass.ds(k.tile0 + g * self.T, self.T), :],
                                  self.M1.rearrange("p (t d) -> p t d", t=self.T), ALU.add)\
                    .then_inc(self.out_sum.sem, 1)

    def sync(self, sp):
        k = self.k
        with sp.Fori(0, self.G // 2) as i:
            for par in range(2):
                g = i * 2 + par
                sp.wait_ge(self.out_sum.sem, self.out_sum.value(g, 1))
                sp.dma_start(k.out_v[:, bass.ds(g * self.T, self.T), :], self.ost[:, par, :, :])\
                    .then_inc(self.stored[par].sem, 16)
        for s in self.stored:
            sp.wait_ge(s.sem, s.value(self.G // 2, 0))


class Cross:

    HEADS, D, ROWS = 16, 8, 24
    UNITS = 4
    EB = 4
    DVE_STEPS = 2

    def __init__(self, k):
        self.k = k
        sb, sem = k.sb, k.sem
        H = self.HEADS
        self.MEM = k.ap["ctx_1024"].shape[1]
        self.KEYS = self.MEM + k.S
        self.QS = sb("x_QS", [P, 2, 2, H, 32], F16)
        self.KS = sb("x_KS", [P, 3, H, 32], F16)
        self.VS = sb("x_VS", [P, 2, 3, H, 18], F16)
        self.O = sb("x_O", [P, 2, H * 18], F32)
        self.Os = sb("x_Os", [P, 2, H, 9], F32)
        S = lambda name, per, credit=0: Count(sem("x_" + name), per, credit)
        self.ve_ready = S("ve_ready", 1)
        self.rstd_ready = S("rstd_ready", 1)
        self.h2_ready = S("h2_ready", 1)
        self.XT_ready = S("XT_ready", 1)
        self.XThi_ready = S("XThi_ready", 1)
        self.XTlo_ready = S("XTlo_ready", 1)
        self.kv01_ready = S("kv01_ready", 1)
        self.kvq_ready = S("kvq_ready", 1)
        self.hi_ready = S("hi_ready", 2)
        self.lo_ready = S("lo_ready", 2)
        self.KT_ps = S("KT_ps", 2)
        self.KT_ready = S("KT_ready", 2)
        self.QT_ps = S("QT_ps", 1)
        self.QT_ready = S("QT_ready", 1)
        self.s_ready = S("s_ready", H)
        self.max_done = S("max_done", H, 2)
        self.m_ready = S("m_ready", 4)
        self.QM_ps = S("QM_ps", 4)
        self.QM_ready = S("QM_ready", 4)
        self.t_ready = S("t_ready", H)
        self.exp_done = S("exp_done", H, 2)
        self.elo_done = [S(f"elo_done{i}", H // 2, 2) for i in range(2)]
        self.pv_done = S("pv_done", H, self.EB)
        self.O_ready = S("O_ready", 1)
        self.at_ready = S("at_ready", 1, 1)
        self.atT_ready = S("atT_ready", 1)
        self.aT_ready = S("aT_ready", 1)
        self.y_ready = S("y_ready", 1)
        self.x_done = S("x_done", 1, 2)
        self.shift_step = S("shift_steps", 2)
        self.tail_step = S("tail_steps", 2)
        self.steps = S("dve_steps", self.DVE_STEPS)
        self.X, self.Y = k.ps[:, 6, :], k.ps[:, 7, :]

    def alloc(self):
        k, sb, H = self.k, self.k.sb, self.HEADS
        self.mem = sb("x_mem", [self.MEM, P], F32)
        self.h2 = sb("x_h2", [P, 2, P], F32)
        self.stats = sb("x_stats", [P, 2, 6], F32)
        self.mv = sb("x_mv", [P, 2, 2], F32)
        self.ve = sb("x_ve", [P, 2], F32)
        self.rstd = sb("x_rstd", [P, 2], F32)
        self.XThi = sb("x_XThi", [P, self.KEYS], F16)
        self.XTlo = sb("x_XTlo", [P, self.KEYS], F16)
        self.QT = sb("x_QT", [P, 2, 4, k.S], F16)
        self.KT = sb("x_KT", [P, 2, 4, 3 * P], F16)
        self.QM = sb("x_QM", [P, 2, k.S], F16)
        self.mneg = sb("x_mneg", [P, 2, 4, 2], F32)
        self.mcl = sb("x_mcl", [P, 2, 4, 2], F32)
        self.E32 = sb("x_E32", [P, self.EB, 512], F32)
        self.Ehi = sb("x_Ehi", [P, self.EB, 512], F16)
        self.Elo = sb("x_Elo", [P, self.EB, 512], F16)
        self.r = sb("x_r", [P, 2, H], F32)
        self.at = sb("x_at", [P, 2, P], F32)
        self.aT = sb("x_aT", [P, k.S], F32)

    def s_bank(self, h):
        return self.k.ps[:, h % 2, :]

    def t_bank(self, h):
        return self.k.ps[:, 2 + h % 2, :]

    def o_bank(self, s):
        return self.k.ps[:, 4 + s, :]

    def credits(self, eng):
        for s in (self.max_done, self.exp_done, self.at_ready, self.x_done):
            eng.sem_inc(s.sem, s.credit)

    def clear(self, pool):
        H = self.HEADS
        pool.memset(self.QS[:, :, :, :, :], 0.0)
        pool.memset(self.VS[:, :, :, :, :], 0.0)
        return pool.memset(self.KS[:, :, :, :], 0.0)

    def ones(self, pool):
        pool.memset(self.KS[:, :, :, 24:26], 1.0)
        return pool.memset(self.VS[:, :, :, :, 8:9], 1.0)

    def dve_early(self, dve, st, b, j):
        k = self.k
        tile = lambda s: k.x_all[:, k.tile0 + b * 2 + s, :]
        if j == 11:
            st.start(b)
            for s in range(2):
                last = dve.bn_stats(self.stats[:, s, :], tile(s))
            st.done(last)
            st.carry(k.spare)
            for s in range(2):
                last = dve.bn_aggr(self.mv[:, s, :], self.stats[:, s, :])
            st.done(last)
            dve.tensor_scalar(self.ve[:, :], self.mv[:, :, 1], k.EPS, None, ALU.add)\
                .then_inc(self.ve_ready.sem, 1)
        if j == 13:
            dve.tensor_copy(self.mem[:, :], k.ctx_all[:, b, :])
            dve.wait_ge(self.rstd_ready.sem, self.rstd_ready.value(b, 1))
            for s in range(2):
                last = dve.tensor_scalar(self.h2[:, s, :], tile(s), self.mv[:, s, 0:1],
                                         self.rstd[:, s:s + 1], ALU.subtract, ALU.mult)
            last.then_inc(self.h2_ready.sem, 1)
        if j == 15:
            dve.wait_ge(self.XThi_ready.sem, self.XThi_ready.value(b, 1))
            dve.tensor_tensor(self.XTlo[:, :], self.X[:, 0:self.KEYS], self.XThi[:, :], ALU.subtract)\
                .then_inc(self.XTlo_ready.sem, 1)

    def dve_front(self, dve, b, par, j):
        k = self.k
        if j in (3, 4):
            dve.wait_ge(self.hi_ready.sem, self.hi_ready.value(b, j - 2))
            for c in (0, 1) if j == 3 else (2,):
                n = P if c < 2 else self.KEYS - 2 * P
                kv = (self.Y[:, c * 256:(c + 1) * 256] if c < 2 else self.X[:, 0:256])[0:n]
                kh = lambda lo: kv[:, lo:lo + P].rearrange("p (h d) -> p h d", h=self.HEADS)
                dve.scalar_tensor_tensor(self.KS[0:n, c, :, 16:24], kh(0), 1 / WS, self.KS[0:n, c, :, 0:8],
                                         ALU.mult, ALU.subtract)
                last = dve.scalar_tensor_tensor(self.VS[0:n, par, c, :, 9:17], kh(P), 1 / WS,
                                                self.VS[0:n, par, c, :, 0:8], ALU.mult, ALU.subtract)
            if j == 4:
                for s in range(2):
                    q = self.X[:, 256 + s * P:256 + (s + 1) * P].rearrange("p (h d) -> p h d", h=self.HEADS)
                    last = dve.scalar_tensor_tensor(self.QS[:, par, s, :, 8:16], q, self.D ** -0.5 / WS,
                                                    self.QS[:, par, s, :, 0:8], ALU.mult, ALU.subtract)
            last.then_inc(self.lo_ready.sem, 1)
        if j == 7:
            dve.wait_ge(self.QT_ps.sem, self.QT_ps.value(b, 1))
            dve.tensor_copy(self.QT[:, par, :, :].rearrange("p g q -> p (g q)"), self.X.bitcast(F16))\
                .then_inc(self.QT_ready.sem, 1)

    def pe_early(self, pe, b, j, first=False):
        k = self.k
        if j == 14:
            pe.wait_ge(self.h2_ready.sem, self.h2_ready.value(b, 1))
            if not first:
                pe.wait_ge(self.QT_ready.sem, self.QT_ready.value(b - 1, 1))
            for s in range(2):
                pe.transpose(self.X[:, self.MEM + s * P:self.MEM + (s + 1) * P], self.h2[:, s, :], k.identF[:, :])
            last = pe.transpose(self.X[:, 0:self.MEM], self.mem[:, :], k.identF[0:self.MEM, 0:self.MEM])
            last.then_inc(self.XT_ready.sem, 1)

    def pe_front(self, pe, b, par, j):
        k = self.k
        if j == 0:
            pe.wait_ge(self.XTlo_ready.sem, self.XTlo_ready.value(b, 1))
            pe.wait_ge(self.x_done.sem, self.x_done.value(b, -1))

            def project(out, cols, whi, wlo, first):
                n = cols.stop - cols.start
                for i, (a, w) in enumerate(((self.XThi, whi), (self.XTlo, whi), (self.XThi, wlo))):
                    last = pe.matmul(out[0:n], a[:, cols], w, start=(first and i == 0), stop=(i == 2),
                                     skip_group_check=True)
                return last

            for c in range(2):
                last = project(self.Y[:, c * 256:(c + 1) * 256], slice(c * P, (c + 1) * P),
                               k.Wkv_hi[:, :], k.Wkv_lo[:, :], c == 0)
            last.then_inc(self.kv01_ready.sem, 1)
            for s in range(2):
                project(self.X[:, 256 + s * P:256 + (s + 1) * P],
                        slice(self.MEM + s * P, self.MEM + (s + 1) * P), k.Wq_hi[:, :], k.Wq_lo[:, :], s == 0)
            project(self.X[:, 0:256], slice(2 * P, self.KEYS), k.Wkv_hi[:, :], k.Wkv_lo[:, :], False)\
                .then_inc(self.kvq_ready.sem, 1)
        if j == 5:
            pe.wait_ge(self.lo_ready.sem, self.lo_ready.value(b, 2))
            for half, bank in enumerate((self.Y, self.X)):
                for u in (2 * half, 2 * half + 1):
                    for c in range(3):
                        at = ((u % 2) * 3 + c) * P
                        last = pe.transpose(bank.bitcast(F16)[:, at:at + P],
                                            self.KS[:, c, 4 * u:4 * u + 4, :].rearrange("p h r -> p (h r)"),
                                            k.ident16[:, :])
                last.then_inc(self.KT_ps.sem, 1)
        if j == 7:
            pe.wait_ge(self.KT_ready.sem, self.KT_ready.value(b, 2))
            for u in range(4):
                for s in range(2):
                    last = pe.transpose(self.X.bitcast(F16)[:, (2 * u + s) * P:(2 * u + s + 1) * P],
                                        self.QS[:, par, s, 4 * u:4 * u + 4, :].rearrange("p h r -> p (h r)"),
                                        k.ident16[:, :])
            last.then_inc(self.QT_ps.sem, 1)

    def act_early(self, act, b, j):
        if j == 14:
            act.wait_ge(self.XT_ready.sem, self.XT_ready.value(b, 1))
            act.copy(self.XThi[:, :], self.X[:, 0:self.KEYS]).then_inc(self.XThi_ready.sem, 1)

    def act_front(self, act, b, par, j):
        k = self.k
        if j in (2, 3):
            ready = self.kv01_ready if j == 2 else self.kvq_ready
            act.wait_ge(ready.sem, ready.value(b, 1))
            for c in (0, 1) if j == 2 else (2,):
                n = P if c < 2 else self.KEYS - 2 * P
                kv = (self.Y[:, c * 256:(c + 1) * 256] if c < 2 else self.X[:, 0:256])[0:n]
                kh = lambda lo: kv[:, lo:lo + P].rearrange("p (h d) -> p h d", h=self.HEADS)
                act.activation(self.KS[0:n, c, :, 0:16].rearrange("p h (t d) -> p h t d", t=2), bc(kh(0), 2, 2),
                               ACT.Copy, scale=1 / WS)
                last = act.activation(self.VS[0:n, par, c, :, 0:8], kh(P), ACT.Copy, scale=1 / WS)
            if j == 3:
                for s in range(2):
                    q = self.X[:, 256 + s * P:256 + (s + 1) * P].rearrange("p (h d) -> p h d", h=self.HEADS)
                    act.activation(self.QS[:, par, s, :, 0:8], q, ACT.Copy, scale=self.D ** -0.5 / WS)
                    last = act.activation(self.QS[:, par, s, :, 16:24], q, ACT.Copy, scale=self.D ** -0.5 / WS)
            last.then_inc(self.hi_ready.sem, 1)
        if j in (5, 6):
            half = j - 5
            act.wait_ge(self.KT_ps.sem, self.KT_ps.value(b, half + 1))
            act.copy(self.KT[:, par, 2 * half:2 * half + 2, :].rearrange("p g q -> p (g q)"),
                     (self.Y, self.X)[half].bitcast(F16)[:, 0:6 * P]).then_inc(self.KT_ready.sem, 1)

    def pe_scores(self, pe, b, par, h):
        k, u, r = self.k, h // 4, slice(32 * (h % 4), 32 * (h % 4) + self.ROWS)
        if h == 0:
            pe.wait_ge(self.QT_ready.sem, self.QT_ready.value(b, 1))
        pe.wait_ge(self.max_done.sem, self.max_done.value(b, h - 1))
        S = self.s_bank(h)
        pe.matmul(S[:, 0:192], self.QT[r, par, u, 0:P], self.KT[r, par, u, 0:192], start=True, stop=False,
                  skip_group_check=True)
        pe.matmul(S[:, 192:512], self.QT[r, par, u, P:2 * P], self.KT[r, par, u, 0:320], start=False, stop=False,
                  skip_group_check=True)
        for at in (64, 384):
            last = pe.matmul(S[:, at:at + P], k.identB[:, :], k.maskq_x[:, :], start=False, stop=True,
                             skip_group_check=True)
        last.then_inc(self.s_ready.sem, 1)

    def dve_max(self, dve, b, h):
        dve.wait_ge(self.s_ready.sem, self.s_ready.value(b, h + 1))
        S, m = self.s_bank(h), self.mneg[:, (h // 4) % 2, h % 4, :]
        dve.tensor_reduce(m[:, 0:1], S[:, 0:192], AX.X, ALU.max, negate=True)
        dve.tensor_reduce(m[:, 1:2], S[:, 192:512], AX.X, ALU.max, negate=True)\
            .then_inc(self.max_done.sem, 1)

    def dve_shift(self, dve, st, b, par, u):
        dve.wait_ge(self.max_done.sem, self.max_done.value(b, 4 * u + 4))
        w = u % 2
        st.start(b * 4 + u)
        st.done(dve.tensor_scalar(self.mcl[:, w], self.mneg[:, w], CLAMP, -CLAMP, ALU.min, ALU.max))
        rows = self.QS[:, par, :, 4 * u:4 * u + 4, :].rearrange("p s h r -> p h s r")
        st.done(dve.tensor_copy(rows[:, :, :, 24], self.mcl[:, w]))
        dve.tensor_tensor(rows[:, :, :, 25], self.mcl[:, w], rows[:, :, :, 24], ALU.subtract)\
            .then_inc(self.m_ready.sem, 1)

    def pe_shift(self, pe, b, par, u):
        k = self.k
        pe.wait_ge(self.m_ready.sem, self.m_ready.value(b, u + 1))
        for s in range(2):
            last = pe.transpose(self.s_bank(1).bitcast(F16)[:, s * P:(s + 1) * P],
                                self.QS[:, par, s, 4 * u:4 * u + 4, :].rearrange("p h r -> p (h r)"),
                                k.ident16[:, :])
        last.then_inc(self.QM_ps.sem, 1)

    def dve_shifted(self, dve, b, u):
        dve.wait_ge(self.QM_ps.sem, self.QM_ps.value(b, u + 1))
        dve.tensor_copy(self.QM[:, u % 2, :], self.s_bank(1).bitcast(F16)[:, 0:2 * P])\
            .then_inc(self.QM_ready.sem, 1)

    def pe_keys(self, pe, b, par, h):
        k, u, r = self.k, h // 4, slice(32 * (h % 4), 32 * (h % 4) + 32)
        if h % 4 == 0:
            pe.wait_ge(self.QM_ready.sem, self.QM_ready.value(b, u + 1))
        pe.wait_ge(self.exp_done.sem, self.exp_done.value(b, h - 1))
        T = self.t_bank(h)
        for c, q0, at in ((0, 0, 0), (1, 64, 256), (2, 192, 448)):
            n = 256 - q0
            pe.matmul(T[:, at:at + n], self.KT[r, par, u, c * P:(c + 1) * P], self.QM[r, u % 2, q0:256],
                      start=(c == 0), stop=False, skip_group_check=True)
        for at, n, m in ((0, 64, 0), (256, P, 64), (448, 64, 64)):
            last = pe.matmul(T[:, at:at + n], k.identB[:, :], k.maskk_x[:, m:m + n], start=False, stop=True,
                             skip_group_check=True)
        last.then_inc(self.t_ready.sem, 1)

    def act_exp(self, act, b, h):
        act.wait_ge(self.t_ready.sem, self.t_ready.value(b, h + 1))
        lo = self.elo_done[h % 2]
        act.wait_ge(lo.sem, lo.value(b, h // 2 - 1))
        act.activation(self.E32[:, h % self.EB, :], self.t_bank(h), ACT.Exp)
        act.wait_ge(self.pv_done.sem, self.pv_done.value(b, h - self.EB + 1))
        act.activation(self.Ehi[:, h % self.EB, :], self.t_bank(h), ACT.Exp).then_inc(self.exp_done.sem, 1)

    def split(self, eng, b, h):
        eng.wait_ge(self.exp_done.sem, self.exp_done.value(b, h + 1))
        w = h % self.EB
        eng.tensor_tensor(self.Elo[:, w, :], self.E32[:, w, :], self.Ehi[:, w, :], ALU.subtract)\
            .then_inc(self.elo_done[h % 2].sem, 1)

    def pe_values(self, pe, b, par, h):
        if h == 0:
            pe.wait_ge(self.O_ready.sem, self.O_ready.value(b, 1))
        lo = self.elo_done[h % 2]
        pe.wait_ge(lo.sem, lo.value(b, h // 2 + 1))
        w = h % self.EB
        blocks = ((0, 0, 0, 0), (0, 1, 256, 64), (1, 0, 128, 0), (1, 1, 320, 0), (1, 2, 448, 64))
        for s, c, at, p0 in blocks:
            n = P - p0
            for part, (E, cols) in enumerate(((self.Ehi, 18), (self.Elo, 9))):
                last = pe.matmul(self.o_bank(s)[p0:P, h * 18:h * 18 + cols], E[:, w, at:at + n],
                                 self.VS[:, par, c, h, 0:cols], start=(h == 0 and c == 0 and part == 0),
                                 stop=True, skip_group_check=True)
        last.then_inc(self.pv_done.sem, 1)

    def act_output(self, act, b1):
        act.wait_ge(self.pv_done.sem, self.pv_done.value(b1, 0))
        act.wait_ge(self.at_ready.sem, self.at_ready.value(b1, 0))
        act.copy(self.O[:, :, :], self.k.ps[:, 4:6, 0:self.HEADS * 18]).then_inc(self.O_ready.sem, 1)

    def tail(self, b1, dve=None, pe=None, act=None, j=0, st=None):
        k, H = self.k, self.HEADS
        O = self.O[:, :, :].rearrange("p s (h v) -> p (s h) v", h=H)
        Os = self.Os[:, :, :, :].rearrange("p s h v -> p (s h) v")
        if dve is not None and j == 0:
            dve.wait_ge(self.O_ready.sem, self.O_ready.value(b1, 1))
            st.done(dve.tensor_tensor(Os[:, :, 0:8], O[:, :, 0:8], O[:, :, 9:17], ALU.add))
            st.done(dve.reciprocal(self.r[:, :, :].rearrange("p s h -> p (s h)"), O[:, :, 8]))
            dve.tensor_tensor(self.at[:, :, :].rearrange("p s (h d) -> p (s h) d", h=H), Os[:, :, 0:8],
                              bc(self.r[:, :, :].rearrange("p s h -> p (s h)"), 2, self.D), ALU.mult)\
                .then_inc(self.at_ready.sem, 1)
        if pe is not None and j == 0:
            pe.wait_ge(self.at_ready.sem, self.at_ready.value(b1, 1))
            for s in range(2):
                last = pe.transpose(self.Y[:, s * P:(s + 1) * P], self.at[:, s, :], k.identF[:, :])
            last.then_inc(self.atT_ready.sem, 1)
        if act is not None and j == 0:
            act.wait_ge(self.atT_ready.sem, self.atT_ready.value(b1, 1))
            act.copy(self.aT[:, :], self.Y[:, 0:2 * P]).then_inc(self.aT_ready.sem, 1)
        if pe is not None and j == 1:
            pe.wait_ge(self.aT_ready.sem, self.aT_ready.value(b1, 1))
            for s in range(2):
                out = self.Y[:, s * P:(s + 1) * P]
                pe.matmul(out, k.one_row[:, :], k.bout_sb[:, :], start=(s == 0), stop=False, skip_group_check=True)
                last = pe.matmul(out, self.aT[:, s * P:(s + 1) * P], k.Wout_sb[:, :], start=False, stop=True,
                                 skip_group_check=True)
            last.then_inc(self.y_ready.sem, 1)
        if dve is not None and j == 1:
            dve.wait_ge(self.y_ready.sem, self.y_ready.value(b1, 1))
            x = k.x_all[:, bass.ds(b1 * 2, 2), :]
            dve.tensor_tensor(x, x, self.Y[:, 0:2 * P].rearrange("p (s d) -> p s d", s=2), ALU.add)\
                .then_inc(self.x_done.sem, 1)

    AHEAD = 6

    def head(self, b, par, h):
        n = h // self.HEADS
        return b + n, par if n == 0 else 1 - par, h % self.HEADS

    def tensor(self, pe):
        one = self.k.one_row
        for s in range(2):
            for at in range(0, self.HEADS * 18, P):
                n = min(P, self.HEADS * 18 - at)
                last = pe.matmul(self.o_bank(s)[:, at:at + n], one[:, :], one[:, 0:n], start=(at == 0), stop=True,
                                 skip_group_check=True)
        last.then_inc(self.pv_done.sem, self.pv_done.credit - 2)
        self.pe_early(pe, 0, 14, first=True)
        for j in range(self.HEADS):
            self.pe_front(pe, 0, 0, j)
        for h in range(self.AHEAD):
            self.pe_scores(pe, 0, 0, h)
            if h == 3:
                self.pe_shift(pe, 0, 0, 0)
                self.pe_keys(pe, 0, 0, 0)
        self.pe_early(pe, 1, 14)
        with pe.Fori(0, self.k.B // 2) as i:
            for par in range(2):
                b = i * 2 + par
                for h in range(self.HEADS):
                    self.pe_keys(pe, *self.head(b, par, h + 1))
                    if h % 4 == 2:
                        nb, npar, nh = self.head(b, par, h + 2)
                        self.pe_shift(pe, nb, npar, nh // 4)
                    self.pe_scores(pe, *self.head(b, par, h + self.AHEAD))
                    self.pe_front(pe, b + 1, 1 - par, h)
                    if h in (7, 9):
                        self.tail(b, pe=pe, j=(h - 7) // 2)
                    self.pe_values(pe, *self.head(b, par, h - 2))
                    self.pe_early(pe, b + 2, h)
        for h in range(2):
            self.pe_values(pe, *self.head(self.k.B, 0, h - 2))
        self.tail(self.k.B, pe=pe, j=0)
        self.tail(self.k.B, pe=pe, j=1)

    def vector(self, dve):
        st, shift_st = Steps(dve, self.steps), Steps(dve, self.shift_step)
        for j in (11, 13, 15):
            self.dve_early(dve, st, 0, j)
        for j in range(self.HEADS):
            self.dve_front(dve, 0, 0, j)
        self.dve_early(dve, st, 1, 11)
        for h in range(self.AHEAD):
            self.dve_max(dve, 0, h)
            if h == 3:
                self.dve_shift(dve, shift_st, 0, 0, 0)
                self.dve_shifted(dve, 0, 0)
        self.dve_early(dve, st, 1, 13)
        self.dve_early(dve, st, 1, 15)
        with dve.Fori(0, self.k.B // 2) as i:
            for par in range(2):
                b = i * 2 + par
                for h in range(self.HEADS):
                    if h % 2 == 1:
                        self.split(dve, b, h - 1)
                    if h % 4 == 2:
                        nb, _, nh = self.head(b, par, h + 2)
                        self.dve_shifted(dve, nb, nh // 4)
                    nb, _, nh = self.head(b, par, h + self.AHEAD)
                    self.dve_max(dve, nb, nh)
                    if h % 4 == 1:
                        nb, npar, nh = self.head(b, par, h + 3)
                        self.dve_shift(dve, shift_st, nb, npar, nh // 4)
                    self.dve_front(dve, b + 1, 1 - par, h)
                    if h in (5, 10):
                        self.tail(b, dve=dve, j=(h - 5) // 5, st=self.tail_steps(dve, b))
                    self.dve_early(dve, st, b + 2, h)
        self.tail(self.k.B, dve=dve, j=0, st=self.tail_steps(dve, self.k.B))
        self.tail(self.k.B, dve=dve, j=1)

    def tail_steps(self, dve, b1):
        st = Steps(dve, self.tail_step)
        st.start(b1)
        return st

    def scalar(self, act):
        self.act_early(act, 0, 14)
        for j in range(self.HEADS):
            self.act_front(act, 0, 0, j)
        self.act_early(act, 1, 14)
        with act.Fori(0, self.k.B // 2) as i:
            for par in range(2):
                b = i * 2 + par
                for h in range(self.HEADS):
                    self.act_exp(act, b, h)
                    if h == 2:
                        self.act_output(act, b)
                    if h == 8:
                        self.tail(b, act=act, j=0)
                    self.act_front(act, b + 1, 1 - par, h)
                    self.act_early(act, b + 2, h)
        self.act_output(act, self.k.B)
        self.tail(self.k.B, act=act, j=0)

    def gpsimd(self, pool):
        k = self.k

        def rstd(b):
            pool.wait_ge(self.ve_ready.sem, self.ve_ready.value(b, 1))
            pool.tensor_tensor(self.rstd[:, :], self.ve[:, :], k.minus_half[:, 0:2], ALU.pow)\
                .then_inc(self.rstd_ready.sem, 1)

        for w in (2, 3):
            pool.memset(self.Ehi[:, w, :], 1.0)
            pool.memset(self.Elo[:, w, :], 1.0).then_inc(self.elo_done[w % 2].sem, self.elo_done[w % 2].credit)
        rstd(0)
        rstd(1)
        with pool.Fori(0, k.B) as b:
            for h in range(1, self.HEADS, 2):
                self.split(pool, b, h)
                if h == 11:
                    rstd(b + 2)


class SelfAttention:

    H, D, CR = 8, 64, 32
    EB = 4
    DVE_HEADS = (1, 4)
    OLD, WIN, SINK = range(3)
    KBLOCKS = ((0, 128, 0, 0, 0), (128, 64, 128, 64, 1), (192, 64, 192, 128, 2),
               (256, 192, 64, 0, 0), (448, 64, 192, 128, 2))
    VBLOCKS = ((0, 1, 0, 128, 0, 0), (1, 1, 128, 64, 0, 1), (1, 1, 192, 64, 64, 2),
               (0, 0, 256, 64, 64, 0), (1, 0, 320, 128, 0, 0), (1, 0, 448, 64, 64, 2))

    def __init__(self, k):
        self.k = k
        sb, sem = k.sb, k.sem
        H, D = self.H, self.D
        self.NB = k.S // self.CR
        NB = self.NB
        self.stats = sb("a_stats", [P, 2, 6], F32)
        self.mv = sb("a_mv", [P, 2, 2], F32)
        self.ve = sb("a_ve", [P, 2], F32)
        self.rstd = sb("a_rstd", [P, 2], F32)
        self.hn = sb("a_hn", [P, 2, P], F32)
        self.hThi = sb("a_hThi", [P, k.S], F16)
        self.hTlo = sb("a_hTlo", [P, k.S], F16)
        self.qraw = sb("a_qraw", [P, 2, H + 1, D], F32)
        self.sq = sb("a_sq", [P, 2, H + 1, D], F32)
        self.ms = sb("a_ms", [P, 2 * (H + 1)], F32)
        self.rq = sb("a_rq", [P, 2 * (H + 1)], F32)
        self.rope1 = sb("a_rope1", [P, 2, H + 1, 32], F32)
        self.rope2 = sb("a_rope2", [P, 2, H + 1, 32], F32)
        self.qn = sb("a_qn", [P, 2, H + 1, D], F32)
        self.QS = sb("a_QS", [P, 2, H, 2, D], F16)
        self.KS = sb("a_KS", [P, 2, 4, D], F16)
        self.QT = sb("a_QT", [P, 2, H, k.S], F16)
        self.KT = sb("a_KT", [P, 2, 2, k.S], F16)
        self.VS = sb("a_VS", [P, 2, 3, 2 * D + 1], F16)
        self.ks = sb("a_ks", [P, 2, NB], F32)
        self.kc = sb("a_kc", [P, NB], F32)
        self.kcg = sb("a_kcg", [P, 2, NB + 3], F16)
        self.vcT = sb("a_vcT", [P, 4, H, NB], F32)
        self.VW = sb("a_VW", [H * NB, 2, P], F32)
        self.EX = sb("a_EX", [P, 2 * H * (NB + 1) + 2 * H * 3], F32)
        self.cz = self.EX[:, 0:2 * H * (NB + 1)].rearrange("p (g n) -> p g n", n=NB + 1)
        self.gz = self.EX[:, 2 * H * (NB + 1):].rearrange("p (g n) -> p g n", n=3)
        self.czr = sb("a_czr", [P, 2 * H, NB], F32)
        self.cm = sb("a_cm", [P, 2 * H], F32)
        self.cl = sb("a_cl", [P, 2 * H], F32)
        self.gsum = sb("a_gsum", [P, 2 * H], F32)
        self.gcl = sb("a_gcl", [P, 2 * H], F32)
        self.gate = sb("a_gate", [P, 2, 3, 2 * H], F32)
        self.pcs = sb("a_pcs", [P, 2, 2 * H, NB], F32)
        self.pcT = sb("a_pcT", [H * NB, k.S], F32)
        self.mneg = sb("a_mneg", [P, 2, 4, 2, 2], F32)
        self.mcl = sb("a_mcl", [P, 2, 4, 2, 2], F32)
        self.mst = sb("a_mst", [P, 2, H, 2, 2], F16)
        self.mT = sb("a_mT", [4 * H, 2, k.S], F16)
        self.nm = sb("a_nm", [P, 2, 3, 2, H], F32)
        self.E32 = sb("a_E32", [P, self.EB, 512], F32)
        self.Ehi = sb("a_Ehi", [P, self.EB, 512], F16)
        self.Elo = sb("a_Elo", [P, self.EB, 512], F16)
        self.O = sb("a_O", [P, 2, 2, 2, H, D + 1], F32)
        self.n12 = sb("a_n12", [P, 2, 2 * H], F32)
        self.dx = sb("a_dx", [P, 4, 2 * H], F32)
        self.ea = sb("a_ea", [P, 4, 2 * H], F32)
        self.pl = sb("a_pl", [P, 3, 2 * H], F32)
        self.LL = sb("a_LL", [P, 2, 2 * H], F32)
        self.rr = sb("a_rr", [P, 2, 2 * H], F32)
        self.co = sb("a_co", [P, 3, 2 * H], F32)
        self.mixw = sb("a_mixw", [P, 2, H, D], F32)
        self.mixo = sb("a_mixo", [P, 2, H, D], F32)
        self.mixT = sb("a_mixT", [P, 2, 4, P], F32)
        S = lambda name, per, credit=0: Count(sem("a_" + name), per, credit)
        self.ve_ready = S("ve_ready", 1)
        self.rstd_ready = S("rstd_ready", 1)
        self.hn_ready = S("hn_ready", 1)
        self.hT_ps = S("hT_ps", 1)
        self.hThi_ready = S("hThi_ready", 1)
        self.hTlo_ready = S("hTlo_ready", 1)
        self.kv_ps = S("kv_ps", 1)
        self.kvhi_ready = S("kvhi_ready", 1)
        self.kvlo_ready = S("kvlo_ready", 1)
        self.ms_ready = S("ms_ready", 1)
        self.rq_ready = S("rq_ready", 1)
        self.rope_ready = S("rope_ready", 1)
        self.qn_ready = S("qn_ready", 1)
        self.QShi_ready = S("QShi_ready", 1)
        self.QSlo_ready = S("QSlo_ready", 1)
        self.cg_ps = S("cg_ps", 1)
        self.vc_ps = S("vc_ps", 1)
        self.vcT_ready = S("vcT_ready", 1)
        self.VW_ps = S("VW_ps", 1)
        self.VW_ready = S("VW_ready", 1)
        self.ex_ready = S("ex_ready", 1)
        self.exp_ready = S("exp_ready", 1)
        self.pcT_ps = S("pcT_ps", 1)
        self.pcT_ready = S("pcT_ready", 1, 1)
        self.dx_ready = S("dx_ready", 1)
        self.ea_ready = S("ea_ready", 1)
        self.co_ready = S("co_ready", 1)
        self.mixo_ready = S("mixo_ready", 1)
        self.mix_ready = S("mix_ready", 1)
        self.mix_ps = S("mix_ps", 1)
        self.y_ps = S("y_ps", 1)
        self.kcg_ready = S("kcg_ready", 1)
        self.K_ps = S("K_ps", 1)
        self.K_ready = S("K_ready", 1)
        self.qs_done = S("qs_done", 1)
        self.q_ps = S("q_ps", 2)
        self.q_read = S("q_read", 2)
        self.Q_ps = S("Q_ps", 2)
        self.Q_ready = [S(f"Q_ready{s}", 1) for s in range(2)]
        self.mixT_ready = [S(f"mixT_ready{s}", 1, 1) for s in range(2)]
        self.x_done = S("x_done", 1, 2)
        self.s_ready = S("s_ready", H)
        self.max_done = S("max_done", H, 2)
        self.m_ready = S("m_ready", 2)
        self.m_ps = S("m_ps", 2)
        self.mT_ready = S("mT_ready", 2)
        self.t_ready = S("t_ready", H)
        self.exp_done = S("exp_done", H, 2)
        self.elo_done = [S(f"elo_done{i}", n, n) for i, n in enumerate((H - len(self.DVE_HEADS),
                                                                        len(self.DVE_HEADS)))]
        self.pv_done = S("pv_done", H, self.EB)
        self.o_done = S("o_done", H, 4)
        self.early_step = S("early_steps", 2)
        self.late_step = S("late_steps", 2)
        self.kc_step = S("kc_steps", 3)
        self.cg_step = S("cg_steps", 11)
        self.shift_step = S("shift_steps", 3)
        self.tail_step = S("tail_steps", 7)
        self.rope_step = S("rope_steps", 1)
        self.X, self.Y = k.ps[:, 6, :], k.ps[:, 7, :]

    def s_bank(self, h):
        return self.k.ps[:, h % 2, :]

    def t_bank(self, h):
        return self.k.ps[:, 2 + h % 2, :]

    def o_bank(self, h):
        return self.k.ps[:, 4 + h % 2, :]

    def credits(self, eng):
        for s in (self.max_done, self.exp_done, *self.elo_done, self.x_done, self.pcT_ready, *self.mixT_ready):
            eng.sem_inc(s.sem, s.credit)
        for s in (self.pv_done, self.o_done):
            eng.sem_inc(s.sem, s.credit - 2)

    def clear(self, pool):
        for t in (self.gate, self.nm, self.pcs, self.mst):
            pool.memset(t[:, :], 0.0)
        pool.memset(self.VW[:, :, :], 0.0)
        pool.memset(self.O[:, :], 1.0)
        pool.memset(self.Ehi[:, :, :], 1.0)
        pool.memset(self.Elo[:, :, :], 1.0)
        pool.memset(self.VS[:, :, :, :], 1.0)
        return pool.memset(self.kcg[:, :, :], 0.0)

    def dve_front(self, dve, st, n, par, j, early):
        k, H, D = self.k, self.H, self.D
        tile = lambda s: k.x_all[:, k.tile0 + n * 2 + s, :]
        if early and j == 4:
            st.start(n)
            for s in range(2):
                last = dve.bn_stats(self.stats[:, s, :], tile(s))
            st.done(last)
            st.carry(k.spare)
            for s in range(2):
                last = dve.bn_aggr(self.mv[:, s, :], self.stats[:, s, :])
            st.done(last)
            dve.tensor_scalar(self.ve[:, :], self.mv[:, :, 1], k.EPS, None, ALU.add)\
                .then_inc(self.ve_ready.sem, 1)
        if early and j == 5:
            dve.wait_ge(self.rstd_ready.sem, self.rstd_ready.value(n, 1))
            for s in range(2):
                last = dve.tensor_scalar(self.hn[:, s, :], tile(s), self.mv[:, s, 0:1],
                                         self.rstd[:, s:s + 1], ALU.subtract, ALU.mult)
            last.then_inc(self.hn_ready.sem, 1)
        if early and j == 7:
            dve.wait_ge(self.hThi_ready.sem, self.hThi_ready.value(n, 1))
            dve.tensor_tensor(self.hTlo[:, :], self.X[:, 0:k.S], self.hThi[:, :], ALU.subtract)\
                .then_inc(self.hTlo_ready.sem, 1)
        if early:
            return
        if j == 1:
            st.start(n)
            dve.wait_ge(self.qs_done.sem, self.qs_done.value(n, 1))
            st.done(dve.tensor_reduce(self.ms[:, :], self.sq[:, :, :, :].rearrange("p s h d -> p (s h) d"),
                                      AX.X, ALU.add))
            dve.tensor_scalar(self.ms[:, :], self.ms[:, :], 1 / D, WS * WS * 1e-6, ALU.mult, ALU.add)\
                .then_inc(self.ms_ready.sem, 1)
        if j == 2:
            dve.wait_ge(self.kvhi_ready.sem, self.kvhi_ready.value(n, 1))
            for o, at in enumerate((D, 4 * D, 3 * D)):
                last = dve.scalar_tensor_tensor(self.VS[:, par, o, D + 1:], self.X[:, at:at + D], 1 / WS,
                                                self.VS[:, par, o, 0:D], ALU.mult, ALU.subtract)
            last.then_inc(self.kvlo_ready.sem, 1)
        if j == 2.5:
            dve.wait_ge(self.rq_ready.sem, self.rq_ready.value(n, 1))
            flat = lambda t: t.rearrange("p s h d -> p (s h) d")
            dve.tensor_tensor(flat(self.qn[:, :, :, 32:D]), flat(self.qraw[:, :, :, 32:D]),
                              bc(self.rq[:, :], 2, D - 32), ALU.mult)
            dve.wait_ge(self.rope_ready.sem, self.rope_ready.value(n, 1))
            st.done(dve.tensor_tensor(flat(self.qn[:, :, :, 0:32]), flat(self.rope1[:, :, :, :]),
                                      bc(self.rq[:, :], 2, 32), ALU.mult))
            dve.tensor_tensor(self.qn[:, :, H, :], self.qn[:, :, H, :], bc(k.gqk_sb[:, :], 1, 2), ALU.mult)\
                .then_inc(self.qn_ready.sem, 1)
        if j == 3.5:
            dve.wait_ge(self.QShi_ready.sem, self.QShi_ready.value(n, 1))
            dve.tensor_tensor(self.KS[:, :, 2:4, :], bc(self.qn[:, :, H, :], 2, 2), self.KS[:, :, 0:2, :],
                              ALU.subtract)
            for s in range(2):
                last = dve.tensor_tensor(self.QS[:, s, :, 1, :], self.qn[:, s, 0:H, :], self.QS[:, s, :, 0, :],
                                         ALU.subtract)
            last.then_inc(self.QSlo_ready.sem, 1)
        if j == 4:
            dve.wait_ge(self.Q_ps.sem, self.Q_ps.value(n, 2))
            dve.tensor_copy(self.QT[:, par, :, P:2 * P], self.Y.bitcast(F16).rearrange("p (h q) -> p h q", h=H))\
                .then_inc(self.Q_ready[1].sem, 1)
        if j == 5:
            dve.wait_ge(self.K_ready.sem, self.K_ready.value(n, 1))
            st_ = self.kc_steps
            st_.start(n)
            st_.done(dve.tensor_reduce(self.ks[:, :, :], self.KT[:, par, :, :].rearrange(
                "p a (n c) -> p a n c", c=self.CR), AX.X, ALU.add))
            st_.done(dve.tensor_tensor(self.kc[:, :], self.ks[:, 0, :], self.ks[:, 1, :], ALU.add))
            st_.done(dve.tensor_scalar(self.kcg[:, 0, 0:self.NB], self.kc[:, :], 1 / self.CR, None, ALU.mult))
            dve.scalar_tensor_tensor(self.kcg[:, 1, 0:self.NB], self.kc[:, :], 1 / self.CR,
                                     self.kcg[:, 0, 0:self.NB], ALU.mult, ALU.subtract)\
                .then_inc(self.kcg_ready.sem, 1)
        if j == 5.5:
            dve.wait_ge(self.vc_ps.sem, self.vc_ps.value(n, 1))
            dve.tensor_tensor(self.vcT[:, :, :, :].rearrange("p c h n -> p (c h) n"),
                              bc(self.X[:, 0:self.NB], 1, 4 * H),
                              k.headmask[:, :, :, :].rearrange("p c h n -> p (c h) n"), ALU.mult)\
                .then_inc(self.vcT_ready.sem, 1)
        if j == 6:
            dve.wait_ge(self.cg_ps.sem, self.cg_ps.value(n, 1))
            cg = self.Y[:, 0:2 * H * (self.NB + 3)].rearrange("p (g n) -> p g n", n=self.NB + 3)
            cs = self.cg_steps
            cs.start(n)
            for s in range(2):
                g = slice(s * H, (s + 1) * H)
                dve.tensor_tensor(self.czr[:, g, :], cg[:, g, 0:self.NB], bc(k.maskc[:, s, :], 1, H), ALU.add)
            cs.done(dve.scalar_tensor_tensor(self.gz, cg[:, :, self.NB:], -1.0, bc(k.bgate_sb[:, :], 1, 2 * H),
                                             ALU.mult, ALU.subtract))
            cs.done(dve.tensor_reduce(self.cm[:, :], self.czr[:, :, :], AX.X, ALU.max))
            cs.done(dve.tensor_tensor(self.cm[:, :], self.cm[:, :], k.sink2[:, :], ALU.max))
            dve.tensor_tensor(self.cz[:, :, 0:self.NB], self.czr[:, :, :], bc(self.cm[:, :], 2, self.NB),
                              ALU.subtract)
            dve.tensor_tensor(self.cz[:, :, self.NB], k.sink2[:, :], self.cm[:, :], ALU.subtract)\
                .then_inc(self.ex_ready.sem, 1)
        if j == 7:
            cs = self.cg_steps
            g, NB = self.gate[:, par], self.NB
            dve.wait_ge(self.exp_ready.sem, self.exp_ready.value(n, 1))
            dve.tensor_reduce(self.cl[:, :], self.cz, AX.X, ALU.add)
            cs.done(dve.tensor_scalar(self.gz, self.gz, 1.0, None, ALU.add))
            cs.done(dve.reciprocal(self.gz, self.gz))
            cs.done(dve.tensor_reduce(self.gsum[:, :], self.gz, AX.X, ALU.add))
            cs.done(dve.tensor_scalar(self.gsum[:, :], self.gsum[:, :], 1e-6, None, ALU.max))
            dve.reciprocal(self.cl[:, :], self.cl[:, :])
            cs.done(dve.reciprocal(self.gsum[:, :], self.gsum[:, :]))
            cs.done(dve.tensor_tensor(g.rearrange("p n g -> p g n"), self.gz, bc(self.gsum[:, :], 2, 3), ALU.mult))
            cs.done(dve.tensor_tensor(self.gcl[:, :], g[:, 0, :], self.cl[:, :], ALU.mult))
            cs.done(dve.tensor_tensor(self.pcs[:, par, :, :], self.cz[:, :, 0:NB], bc(self.gcl[:, :], 2, NB),
                                      ALU.mult))

    def pe_front(self, pe, n, par, j, early, first=False):
        k, H, D = self.k, self.H, self.D
        parts = lambda whi, wlo: ((self.hThi, whi), (self.hTlo, whi), (self.hThi, wlo))
        if early and j == 6:
            pe.wait_ge(self.hn_ready.sem, self.hn_ready.value(n, 1))
            if not first:
                pe.wait_ge(self.vcT_ready.sem, self.vcT_ready.value(n - 1, 1))
            pe.wait_ge(self.x_done.sem, self.x_done.value(n - 1, 0))
            for s in range(2):
                last = pe.transpose(self.X[:, s * P:(s + 1) * P], self.hn[:, s, :], k.identF[:, :])
            last.then_inc(self.hT_ps.sem, 1)
        if early and j == 7:
            pe.wait_ge(self.hTlo_ready.sem, self.hTlo_ready.value(n, 1))
            for s in range(2):
                if s == 1 and not first:
                    pe.wait_ge(self.VW_ready.sem, self.VW_ready.value(n - 1, 1))
                for i, (a, w) in enumerate(parts(k.WQ_hi[:, :], k.WQ_lo[:, :])):
                    last = pe.matmul((self.X, self.Y)[s], a[:, s * P:(s + 1) * P], w, start=(i == 0), stop=(i == 2))
                last.then_inc(self.q_ps.sem, 1)
        if early:
            return
        if j == 0:
            pe.wait_ge(self.q_read.sem, self.q_read.value(n, 2))
            for at, w0, t0 in ((0, 0, 0), (P, 0, P), (2 * P, D, D)):
                for i, (a, w) in enumerate(parts(k.aKV_hi[:, w0:], k.aKV_lo[:, w0:])):
                    last = pe.matmul(self.X[:, at:at + P - w0], a[:, t0:t0 + P], w, start=(at == 0 and i == 0),
                                     stop=(i == 2), skip_group_check=True)
            last.then_inc(self.kv_ps.sem, 1)
        if j == 4:
            pe.wait_ge(self.QSlo_ready.sem, self.QSlo_ready.value(n, 1))
            pe.wait_ge(self.pcT_ready.sem, self.pcT_ready.value(n, 0))
            for s in range(2):
                for h in range(H):
                    last = pe.transpose((self.X, self.Y)[s].bitcast(F16)[:, h * P:(h + 1) * P],
                                        self.QS[:, s, h, :, :].rearrange("p a d -> p (a d)"), k.ident16[:, :])
                last.then_inc(self.Q_ps.sem, 1)
            pe.wait_ge(self.Q_ready[0].sem, self.Q_ready[0].value(n, 1))
            for s in range(2):
                for a in range(2):
                    last = pe.transpose(self.X.bitcast(F16)[:, a * k.S + s * P:a * k.S + (s + 1) * P],
                                        self.KS[:, s, 2 * a:2 * a + 2, :].rearrange("p a d -> p (a d)"),
                                        k.ident16[:, :])
            last.then_inc(self.K_ps.sem, 1)
        if j == 5:
            pe.wait_ge(self.kcg_ready.sem, self.kcg_ready.value(n, 1))
            for half in range(2):
                for s, o in ((0, 0), (1, 2)):
                    for a in (slice(0, D), slice(D + 1, 2 * D + 1)):
                        last = pe.matmul(self.X[half * D:(half + 1) * D, 0:self.NB], self.VS[:, par, o, a],
                                         k.blockmean[:, s, :], start=(s == 0 and a.start == 0),
                                         stop=(s == 1 and a.start > 0), skip_group_check=True)
            last.then_inc(self.vc_ps.sem, 1)
            pe.wait_ge(self.Q_ready[1].sem, self.Q_ready[1].value(n, 1))
            w = self.NB + 3
            for s in range(2):
                for h in range(H):
                    at = (s * H + h) * w
                    q = slice(s * P, (s + 1) * P)
                    pe.matmul(self.Y[:, at:at + w], self.QT[:, par, h, q], self.kcg[:, 0, :],
                              start=(s == 0 and h == 0), stop=False, skip_group_check=True)
                    last = pe.matmul(self.Y[:, at:at + w], self.QT[0:D, par, h, q], self.kcg[0:D, 1, :],
                                     start=False, stop=True, skip_group_check=True)
            last.then_inc(self.cg_ps.sem, 1)
        if j == 7:
            pe.wait_ge(self.vcT_ready.sem, self.vcT_ready.value(n, 1))
            pe.wait_ge(self.ex_ready.sem, self.ex_ready.value(n, 1))
            for c in range(4):
                last = pe.matmul(self.Y[0:H * self.NB, 0:P], self.vcT[:, c, :, :].rearrange("p h n -> p (h n)"),
                                 k.Weff[:, c, :], start=(c == 0), stop=(c == 3))
            last.then_inc(self.VW_ps.sem, 1)

    def act_front(self, act, n, par, j, early, first=False):
        k, H, D = self.k, self.H, self.D
        if early and j == 6:
            act.wait_ge(self.hT_ps.sem, self.hT_ps.value(n, 1))
            act.copy(self.hThi[:, :], self.X[:, 0:k.S]).then_inc(self.hThi_ready.sem, 1)
        if early and j == 7:
            for s in range(2):
                act.wait_ge(self.q_ps.sem, self.q_ps.value(n, s + 1))
                q = (self.X, self.Y)[s].rearrange("p (h d) -> p h d", h=H)
                act.copy(self.qraw[:, s, 0:H, :], q)
                act.activation(self.sq[:, s, 0:H, :], q, ACT.Square).then_inc(self.q_read.sem, 1)
        if early:
            return
        if j == 0:
            act.wait_ge(self.kv_ps.sem, self.kv_ps.value(n, 1))
            kx = self.X[:, 0:2 * P].rearrange("p (s d) -> p s d", s=2)[:, :, 0:D]
            act.copy(self.qraw[:, :, H, :], kx)
            act.activation(self.sq[:, :, H, :], kx, ACT.Square).then_inc(self.qs_done.sem, 1)
        if j == 2:
            if not first:
                act.wait_ge(self.pv_done.sem, self.pv_done.value(n - 1, 0))
            for o, at in enumerate((D, 4 * D, 3 * D)):
                last = act.activation(self.VS[:, par, o, 0:D], self.X[:, at:at + D], ACT.Copy, scale=1 / WS)
            last.then_inc(self.kvhi_ready.sem, 1)
        if j == 3:
            act.wait_ge(self.qn_ready.sem, self.qn_ready.value(n, 1))
            act.copy(self.KS[:, :, 0:2, :], bc(self.qn[:, :, H, :], 2, 2))
            for s in range(2):
                last = act.copy(self.QS[:, s, :, 0, :], self.qn[:, s, 0:H, :])
            last.then_inc(self.QShi_ready.sem, 1)
        if j == 4:
            act.wait_ge(self.Q_ps.sem, self.Q_ps.value(n, 1))
            act.copy(self.QT[:, par, :, 0:P], self.X.bitcast(F16).rearrange("p (h q) -> p h q", h=H))\
                .then_inc(self.Q_ready[0].sem, 1)
            act.wait_ge(self.K_ps.sem, self.K_ps.value(n, 1))
            act.copy(self.KT[:, par, :, :].rearrange("p a q -> p (a q)"), self.X.bitcast(F16)[:, 0:2 * k.S])\
                .then_inc(self.K_ready.sem, 1)
        if j == 7:
            act.wait_ge(self.ex_ready.sem, self.ex_ready.value(n, 1))
            act.activation(self.EX[:, :], self.EX[:, :], ACT.Exp).then_inc(self.exp_ready.sem, 1)
            act.wait_ge(self.VW_ps.sem, self.VW_ps.value(n, 1))
            act.copy(self.VW[:, par, :], self.Y[0:H * self.NB, 0:P]).then_inc(self.VW_ready.sem, 1)

    def pool_rstd(self, pool, n):
        pool.wait_ge(self.ve_ready.sem, self.ve_ready.value(n, 1))
        pool.tensor_tensor(self.rstd[:, :], self.ve[:, :], self.k.minus_half[:, 0:2], ALU.pow)\
            .then_inc(self.rstd_ready.sem, 1)

    def pool_rope(self, pool, n):
        k, H = self.k, self.H
        pool.wait_ge(self.qs_done.sem, self.qs_done.value(n, 1))
        x, r1, r2 = self.qraw, self.rope1, self.rope2
        for s in range(2):
            cos, sin = (bc(k.rope_sb[:, s, a * 32:(a + 1) * 32], 1, H + 1) for a in range(2))
            pool.tensor_tensor(r1[:, s, :, :], x[:, s, :, 0:32], cos, ALU.mult)
            pool.tensor_tensor(r2[:, s, :, 0:16], x[:, s, :, 16:32], sin[:, :, 0:16], ALU.mult)
            last = pool.tensor_tensor(r2[:, s, :, 16:32], x[:, s, :, 0:16], sin[:, :, 16:32], ALU.mult)
        self.rope_steps.start(n)
        self.rope_steps.done(last)
        flat = lambda t: t[:, :, :, :].rearrange("p s h d -> p (s h d)")
        pool.tensor_tensor(flat(r1), flat(r1), flat(r2), ALU.add).then_inc(self.rope_ready.sem, 1)
        pool.wait_ge(self.ms_ready.sem, self.ms_ready.value(n, 1))
        pool.tensor_tensor(self.rq[:, :], self.ms[:, :], k.minus_half[:, 0:2 * (H + 1)], ALU.pow)\
            .then_inc(self.rq_ready.sem, 1)

    def pe_scores(self, pe, b, par, h):
        k, D = self.k, self.D
        if h == 0:
            pe.wait_ge(self.K_ready.sem, self.K_ready.value(b, 1))
            pe.wait_ge(self.Q_ready[1].sem, self.Q_ready[1].value(b, 1))
        pe.wait_ge(self.max_done.sem, self.max_done.value(b, h - 1))
        if h < 2:
            pe.wait_ge(self.mixT_ready[h].sem, self.mixT_ready[h].value(b, 0))
        S, Q, K = self.s_bank(h), self.QT[0:D, par, h, :], self.KT[0:D, par, 0, :]
        pe.matmul(S, k.identB[:, :], k.maskq_a[:, :], start=True, stop=False)
        mm = lambda out, q, keys, stop=False: pe.matmul(out, Q[:, q], K[:, keys], start=False, stop=stop)
        mm(S[:, 0:128], slice(0, 128), slice(0, 128))
        mm(S[0:64, 128:256], slice(128, 192), slice(64, 192))
        mm(S[64:128, 128:256], slice(192, 256), slice(128, 256))
        mm(S[:, 256:320], slice(0, 128), slice(0, 64))
        mm(S[:, 320:512], slice(128, 256), slice(0, 192), True).then_inc(self.s_ready.sem, 1)

    def dve_max(self, dve, b, h):
        dve.wait_ge(self.s_ready.sem, self.s_ready.value(b, h + 1))
        S, m = self.s_bank(h), self.mneg[:, h // 4, h % 4]
        dve.tensor_reduce(m[:, self.WIN, :], S[:, 0:256].rearrange("p (s c) -> p s c", s=2), AX.X, ALU.max,
                          negate=True)
        dve.tensor_reduce(m[:, self.OLD, 0:1], S[:, 256:320], AX.X, ALU.max, negate=True)
        dve.tensor_reduce(m[:, self.OLD, 1:2], S[:, 320:512], AX.X, ALU.max, negate=True)\
            .then_inc(self.max_done.sem, 1)

    def dve_shift(self, dve, b, par, u):
        dve.wait_ge(self.max_done.sem, self.max_done.value(b, 4 * u + 4))
        st, hs = self.shift_steps, slice(4 * u, 4 * u + 4)
        st.start(b * 2 + u)
        st.done(dve.tensor_scalar(self.mcl[:, u], self.mneg[:, u], CLAMP, -CLAMP, ALU.min, ALU.max))
        m = lambda a: self.mst[:, :, hs, :, a].rearrange("p s h w -> p h w s")
        st.done(dve.tensor_copy(m(0), self.mcl[:, u]))
        st.done(dve.tensor_tensor(m(1), self.mcl[:, u], m(0), ALU.subtract))
        for w in (self.OLD, self.WIN):
            last = dve.tensor_tensor(self.nm[:, par, w, :, hs], self.mst[:, :, hs, w, 0], self.mst[:, :, hs, w, 1],
                                     ALU.add)
        last.then_inc(self.m_ready.sem, 1)

    def pe_shift(self, pe, b, u):
        k = self.k
        pe.wait_ge(self.m_ready.sem, self.m_ready.value(b, u + 1))
        for s in range(2):
            last = pe.transpose(self.s_bank(1)[0:4 * self.H].bitcast(F16)[:, s * P:(s + 1) * P],
                                self.mst[:, s, :, :, :].rearrange("p h w a -> p (h w a)"), k.ident16[:, :])
        last.then_inc(self.m_ps.sem, 1)

    def dve_shifted(self, dve, b, u):
        dve.wait_ge(self.m_ps.sem, self.m_ps.value(b, u + 1))
        dve.tensor_copy(self.mT[:, u, :], self.s_bank(1)[0:4 * self.H].bitcast(F16)[:, 0:2 * P])\
            .then_inc(self.mT_ready.sem, 1)

    def pe_keys(self, pe, b, par, h):
        k, D = self.k, self.D
        if h % 4 == 0:
            pe.wait_ge(self.mT_ready.sem, self.mT_ready.value(b, h // 4 + 1))
        pe.wait_ge(self.exp_done.sem, self.exp_done.value(b, h - 1))
        T = self.t_bank(h)
        pe.matmul(T, k.identB[:, :], k.maskk_a[:, :], start=True, stop=False)
        mT = self.mT[:, h // 4, :]
        for at, n, q0, wo in ((0, 256, 0, self.WIN), (256, 192, 64, self.OLD), (448, 64, 192, self.OLD)):
            pe.matmul(T[:, at:at + n], k.select[:, 2 * h + wo, :], mT[:, q0:q0 + n], start=False, stop=False)
        for at, n, q0, k0, _ in self.KBLOCKS:
            pe.matmul(T[:, at:at + n], self.KT[0:D, par, 1, k0:k0 + P], self.QT[0:D, par, h, q0:q0 + n],
                      start=False, stop=False)
        for at, n, q0, k0, _ in self.KBLOCKS:
            last = pe.matmul(T[:, at:at + n], self.KT[:, par, 0, k0:k0 + P], self.QT[:, par, h, q0:q0 + n],
                             start=False, stop=(at == 448))
        last.then_inc(self.t_ready.sem, 1)

    def wait_split(self, eng, b, h):
        b, _, h = self.head(b, 0, h)
        dve = h in self.DVE_HEADS
        done = self.elo_done[dve]
        eng.wait_ge(done.sem, done.value(b, sum((x in self.DVE_HEADS) == dve for x in range(h + 1))))

    def act_exp(self, act, b, h):
        act.wait_ge(self.t_ready.sem, self.t_ready.value(b, h + 1))
        self.wait_split(act, b, h - self.EB)
        act.activation(self.E32[:, h % self.EB, :], self.t_bank(h), ACT.Exp)
        act.wait_ge(self.pv_done.sem, self.pv_done.value(b, h - self.EB + 1))
        act.activation(self.Ehi[:, h % self.EB, :], self.t_bank(h), ACT.Exp).then_inc(self.exp_done.sem, 1)

    def split(self, eng, b, h):
        eng.wait_ge(self.exp_done.sem, self.exp_done.value(b, h + 1))
        w = h % self.EB
        eng.tensor_tensor(self.Elo[:, w, :], self.E32[:, w, :], self.Ehi[:, w, :], ALU.subtract)\
            .then_inc(self.elo_done[h in self.DVE_HEADS].sem, 1)

    def pe_values(self, pe, b, par, h):
        k, D = self.k, self.D
        if h == 0:
            pe.wait_ge(self.kvlo_ready.sem, self.kvlo_ready.value(b, 1))
        pe.wait_ge(self.o_done.sem, self.o_done.value(b, h - 1))
        self.wait_split(pe, b, h)
        O = self.o_bank(h)[:, 0:4 * (D + 1)].rearrange("p (s w d) -> p s w d", s=2, w=2)
        pe.matmul(O[:, 0, self.OLD, :], k.zero16[:, :], self.VS[:, par, 0, 0:D + 1], start=True, stop=False,
                  skip_group_check=True)
        for s, wo, at, m, p0, o in self.VBLOCKS:
            for E, v in ((self.Ehi, slice(0, D + 1)), (self.Ehi, slice(D + 1, 2 * D + 1)), (self.Elo, slice(0, D + 1))):
                last = pe.matmul(O[p0:p0 + m, s, wo, 0:v.stop - v.start], E[:, h % self.EB, at:at + m],
                                 self.VS[:, par, o, v], start=False, stop=True, skip_group_check=True)
        last.then_inc(self.pv_done.sem, 1)

    def act_output(self, act, b, par, h):
        act.wait_ge(self.pv_done.sem, self.pv_done.value(b, h + 1))
        act.copy(self.O[:, par, :, :, h, :].rearrange("p s w d -> p (s w) d"),
                 self.o_bank(h)[:, 0:4 * (self.D + 1)].rearrange("p (g d) -> p g d", g=4))\
            .then_inc(self.o_done.sem, 1)

    def dve_tail(self, dve, b1, par, j):
        k, H, D = self.k, self.H, self.D
        st = self.tail_steps
        nm = self.nm[:, par].rearrange("p w s h -> p w (s h)")
        L = self.O[:, par, :, :, :, D]
        sh = lambda t: t.rearrange("p (s h) -> p s h", s=2)
        if j == 0:
            st.start(b1)
            dve.tensor_tensor(self.n12[:, 0, :], nm[:, self.OLD, :], nm[:, self.WIN, :], ALU.min)
            st.done(dve.tensor_tensor(self.n12[:, 1, :], nm[:, self.WIN, :], nm[:, self.SINK, :], ALU.min))
            for a in range(2):
                last = dve.tensor_tensor(self.dx[:, 2 * a:2 * a + 2, :], bc(self.n12[:, a, :], 1, 2),
                                         nm[:, a:a + 2, :], ALU.subtract)
            last.then_inc(self.dx_ready.sem, 1)
        if j == 3:
            dve.wait_ge(self.ea_ready.sem, self.ea_ready.value(b1, 1))
            dve.wait_ge(self.o_done.sem, self.o_done.value(b1, 0))
            for i, (e, w) in enumerate(((0, self.OLD), (1, self.WIN), (2, self.WIN))):
                last = dve.tensor_tensor(sh(self.pl[:, i, :]), sh(self.ea[:, e, :]), L[:, :, w, :], ALU.mult)
            st.done(last)
            dve.tensor_tensor(self.LL[:, 0, :], self.pl[:, 0, :], self.pl[:, 1, :], ALU.add)
            st.done(dve.tensor_tensor(self.LL[:, 1, :], self.pl[:, 2, :], self.ea[:, 3, :], ALU.add))
            st.done(dve.reciprocal(self.LL[:, :, :], self.LL[:, :, :]))
            st.done(dve.tensor_tensor(self.rr[:, :, :], self.LL[:, :, :], self.gate[:, par, 1:3, :], ALU.mult))
            dve.tensor_tensor(self.co[:, 0:2, :], self.ea[:, 0:2, :], bc(self.rr[:, 0, :], 1, 2), ALU.mult)
            st.done(dve.tensor_tensor(self.co[:, 2, :], self.ea[:, 2, :], self.rr[:, 1, :], ALU.mult))
            dve.tensor_tensor(self.co[:, 1, :], self.co[:, 1, :], self.co[:, 2, :], ALU.add)\
                .then_inc(self.co_ready.sem, 1)
            dve.wait_ge(self.co_ready.sem, self.co_ready.value(b1, 1))
            for s in range(2):
                last = dve.tensor_tensor(self.mixw[:, s, :, :], self.O[:, par, s, self.WIN, :, 0:D],
                                         bc(self.co[:, 1, s * H:(s + 1) * H], 2, D), ALU.mult)
            st.done(last)
            dve.wait_ge(self.mixo_ready.sem, self.mixo_ready.value(b1, 1))
            dve.tensor_tensor(self.mixw[:, :, :, :], self.mixw[:, :, :, :], self.mixo[:, :, :, :], ALU.add)\
                .then_inc(self.mix_ready.sem, 1)
        if j == 4:
            dve.wait_ge(self.mix_ps.sem, self.mix_ps.value(b1, 1))
            dve.tensor_copy(self.mixT[:, 1, :, :].rearrange("p c q -> p (c q)"), self.s_bank(1))\
                .then_inc(self.mixT_ready[1].sem, 1)
        if j == 6:
            dve.wait_ge(self.y_ps.sem, self.y_ps.value(b1, 1))
            x = k.x_all[:, bass.ds(b1 * 2, 2), :]
            dve.tensor_tensor(x, x, self.X[:, 2 * P:].rearrange("p (s d) -> p s d", s=2), ALU.add)\
                .then_inc(self.x_done.sem, 1)

    def act_tail(self, act, b1, par, j):
        if j == 0:
            act.wait_ge(self.dx_ready.sem, self.dx_ready.value(b1, 1))
            act.activation(self.ea[:, :, :], self.dx[:, :, :], ACT.Exp).then_inc(self.ea_ready.sem, 1)
            act.wait_ge(self.pcT_ps.sem, self.pcT_ps.value(b1, 1))
            act.copy(self.pcT[:, :], self.Y[0:self.H * self.NB, 0:2 * P]).then_inc(self.pcT_ready.sem, 1)
        if j == 4:
            act.wait_ge(self.mix_ps.sem, self.mix_ps.value(b1, 1))
            act.copy(self.mixT[:, 0, :, :].rearrange("p c q -> p (c q)"), self.s_bank(0))\
                .then_inc(self.mixT_ready[0].sem, 1)

    def pool_tail(self, pool, b1, par):
        pool.wait_ge(self.co_ready.sem, self.co_ready.value(b1, 1))
        for s in range(2):
            last = pool.tensor_tensor(self.mixo[:, s, :, :], self.O[:, par, s, self.OLD, :, 0:self.D],
                                      bc(self.co[:, 0, s * self.H:(s + 1) * self.H], 2, self.D), ALU.mult)
        last.then_inc(self.mixo_ready.sem, 1)

    def pe_tail(self, pe, b1, par, j):
        k, H = self.k, self.H
        if j == 0:
            for s in range(2):
                last = pe.transpose(self.Y[0:H * self.NB, s * P:(s + 1) * P],
                                    self.pcs[:, par, s * H:(s + 1) * H, :].rearrange("p h n -> p (h n)"),
                                    k.identF[:, :])
            last.then_inc(self.pcT_ps.sem, 1)
        if j == 4:
            pe.wait_ge(self.mix_ready.sem, self.mix_ready.value(b1, 1))
            for s in range(2):
                for c in range(4):
                    last = pe.transpose(self.s_bank(s)[:, c * P:(c + 1) * P],
                                        self.mixw[:, s, 2 * c:2 * c + 2, :].rearrange("p h d -> p (h d)"),
                                        k.identF[:, :])
            last.then_inc(self.mix_ps.sem, 1)
        if j == 5:
            pe.wait_ge(self.pcT_ready.sem, self.pcT_ready.value(b1, 1))
            for s in range(2):
                pe.wait_ge(self.mixT_ready[s].sem, self.mixT_ready[s].value(b1, 1))
                out = self.X[:, (2 + s) * P:(3 + s) * P]
                pe.matmul(out, self.pcT[:, s * P:(s + 1) * P], self.VW[:, par, :], start=(s == 0), stop=False,
                          skip_group_check=True)
                for c in range(4):
                    last = pe.matmul(out, self.mixT[:, s, c, :], k.Weff[:, c, :], start=False, stop=(c == 3),
                                     skip_group_check=True)
            last.then_inc(self.y_ps.sem, 1)

    def head(self, b, par, h):
        n = h // self.H
        return b + n, par if n == 0 else 1 - par, h % self.H

    def tensor(self, pe):
        for n, j, early in self.prologue():
            self.pe_front(pe, n, n % 2, j, early, first=(n == 0))
        for h in range(4):
            self.pe_scores(pe, 0, 0, h)
        self.pe_shift(pe, 0, 0)
        self.pe_keys(pe, 0, 0, 0)
        with pe.Fori(0, self.k.B // 2) as i:
            for par in range(2):
                b = i * 2 + par
                for h in range(self.H):
                    nb, npar, nu = (b, par, 1) if h < 4 else (b + 1, 1 - par, 0)
                    if h % 4 == 3:
                        self.pe_values(pe, *self.head(b, par, h - 2))
                        self.pe_shift(pe, nb, nu)
                        self.pe_keys(pe, *self.head(b, par, h + 1))
                    else:
                        self.pe_keys(pe, *self.head(b, par, h + 1))
                        self.pe_values(pe, *self.head(b, par, h - 2))
                    for x in ((), (0, 1), (2, 3), ())[h % 4]:
                        self.pe_scores(pe, nb, npar, 4 * nu + x)
                    self.pe_front(pe, b + 1, 1 - par, h, False)
                    self.pe_tail(pe, b, 1 - par, h)
                    self.pe_front(pe, b + 2, par, h, True)
        for h in range(2):
            self.pe_values(pe, *self.head(self.k.B, 0, h - 2))
        pe.wait_ge(self.q_read.sem, self.q_read.value(self.k.B + 1, 2))
        for j in range(6):
            self.pe_tail(pe, self.k.B, 1, j)

    def prologue(self):
        return [(0, j, True) for j in (4, 5, 6, 7)] + [(0, j, False) for j in range(8)] + \
            [(1, j, True) for j in (4, 5, 6, 7)]

    def vector(self, dve):
        st, late = Steps(dve, self.early_step), Steps(dve, self.late_step)
        self.kc_steps, self.cg_steps = Steps(dve, self.kc_step), Steps(dve, self.cg_step)
        self.shift_steps, self.tail_steps = Steps(dve, self.shift_step), Steps(dve, self.tail_step)
        for n, j, early in self.prologue():
            self.dve_front(dve, st if early else late, n, n % 2, j, early)
            if j in (2, 3, 5) and not early:
                self.dve_front(dve, late, n, n % 2, j + 0.5, False)
        for h in range(4):
            self.dve_max(dve, 0, h)
        self.dve_shift(dve, 0, 0, 0)
        self.dve_shifted(dve, 0, 0)
        with dve.Fori(0, self.k.B // 2) as i:
            for par in range(2):
                b = i * 2 + par
                for h in range(self.H):
                    u, j = h // 4, h % 4
                    nb, npar, nu = (b, par, 1) if u == 0 else (b + 1, 1 - par, 0)
                    if h - 1 in self.DVE_HEADS:
                        self.split(dve, b, h - 1)
                    if h == 5:
                        self.dve_front(dve, late, b + 1, 1 - par, 5, False)
                    if h in (3, 4):
                        self.dve_front(dve, late, b + 1, 1 - par, h - 0.5, False)
                    if h == 6:
                        self.dve_tail(dve, b, 1 - par, 6)
                        self.dve_front(dve, late, b + 1, 1 - par, 5.5, False)
                    for x in ((), (0, 1), (2, 3), ())[j]:
                        self.dve_max(dve, nb, 4 * nu + x)
                    if j == 2:
                        self.dve_shift(dve, nb, npar, nu)
                    if j == 3:
                        self.dve_shifted(dve, nb, nu)
                    if h == 7:
                        self.dve_front(dve, st, b + 2, par, h, True)
                    if h != 5:
                        self.dve_front(dve, late, b + 1, 1 - par, h, False)
                    if h != 6:
                        self.dve_tail(dve, b, 1 - par, h)
                    if h < 7:
                        self.dve_front(dve, st, b + 2, par, h, True)
            self.k.split_expert(dve, i)
        for j in range(7):
            self.dve_tail(dve, self.k.B, 1, j)

    def scalar(self, act):
        for n, j, early in self.prologue():
            self.act_front(act, n, n % 2, j, early, first=(n == 0))
        with act.Fori(0, self.k.B // 2) as i:
            for par in range(2):
                b = i * 2 + par
                for h in range(self.H):
                    self.act_exp(act, b, h)
                    self.act_front(act, b + 1, 1 - par, h, False)
                    self.act_tail(act, b, 1 - par, h)
                    self.act_front(act, b + 2, par, h, True)
                    self.act_output(act, *self.head(b, par, h - 2))
        for h in range(2):
            self.act_output(act, *self.head(self.k.B, 0, h - 2))
        for j in range(5):
            self.act_tail(act, self.k.B, 1, j)

    def gpsimd(self, pool):
        self.rope_steps = Steps(pool, self.rope_step)
        self.pool_rstd(pool, 0)
        self.pool_rope(pool, 0)
        self.pool_rstd(pool, 1)
        with pool.Fori(0, self.k.B // 2) as i:
            for par in range(2):
                b = i * 2 + par
                for h in range(self.H):
                    if h not in self.DVE_HEADS:
                        self.split(pool, b, h)
                    if h == 1:
                        self.pool_rope(pool, b + 1)
                    if h == 3:
                        self.pool_tail(pool, b, 1 - par)
                    if h == 4:
                        self.pool_rstd(pool, b + 2)
        self.pool_tail(pool, self.k.B, 1)


class SelfWeights:

    def self_alloc(self):
        sb, sem = self.sb, self.sem
        H, D = SelfAttention.H, SelfAttention.D
        NB = self.S // SelfAttention.CR
        self.wqc_raw = sb("wqc_raw", [P, 32], F32)
        self.wqup_raw = sb("wqup_raw", [32, H * D], F32)
        self.wkv_raw = sb("wkv_raw", [P, 2, D], F32)
        self.wog_raw = sb("wog_raw", [P, 4, D], F32)
        self.wout_raw = sb("wout_raw", [D, 2, P], F32)
        self.wqcT = sb("wqcT", [32, P], F32)
        self.wogT = sb("wogT", [D, 4, P], F32)
        self.wgate_raw = sb("wgate_raw", [P, 3], F32)
        self.gq_col = sb("gq_col", [P, 1], F32)
        self.gq_row = sb("gq_row", [P, D], F32)
        self.gk_row = sb("gk_row", [P, D], F32)
        self.gqk_sb = sb("gqk_sb", [P, D], F32)
        self.wg_sb = sb("wg_sb", [P, 3], F32)
        self.bgate_sb = sb("bgate_sb", [P, 3], F32)
        self.sink2 = sb("sink2", [P, 2 * H], F32)
        self.rope_sb = sb("rope_sb", [P, self.S // P, 64], F32)
        self.WQ_hi = sb("WQ_hi", [P, H * D], F16)
        self.WQ_lo = sb("WQ_lo", [P, H * D], F16)
        self.aKV_hi = sb("aKV_hi", [P, 2 * D], F16)
        self.aKV_lo = sb("aKV_lo", [P, 2 * D], F16)
        self.Weff = sb("Weff", [P, 4, P], F32)
        self.maskq_a = sb("maskq_a", [P, 512], BF16)
        self.maskk_a = sb("maskk_a", [P, 512], BF16)
        self.maskc = sb("maskc", [P, 2, NB], F32)
        self.headmask = sb("headmask", [P, 4, H, NB], F32)
        self.blockmean = sb("blockmean", [P, 2, NB], F16)
        self.select = sb("select", [4 * H, 2 * H, P], F16)
        self.zero16 = sb("zero16", [P, P], F16)
        self.self_loaded = sem("self_loaded")
        self.self_small = sem("self_small_loaded")
        self.self_T_ps = sem("self_T_ps")
        self.self_T = sem("self_T")
        self.self_ps = sem("self_ps")
        self.self_ready = sem("self_ready")

    SELF_LOADS, SELF_SMALL = 6, 10

    def self_sync(self, sp):
        ap, D = self.ap, SelfAttention.D
        load = lambda dst, src, s: sp.dma_start(dst, src).then_inc(s, 16)
        load(self.wqc_raw[:, :], ap["L0_attn_w_qc"], self.self_loaded)
        load(self.wog_raw[:, :, :], ap["L0_attn_w_out_group"].rearrange("g (c p) i -> p (g c) i", p=P),
             self.self_loaded)
        load(self.wqup_raw[:, :], ap["L0_attn_w_qup"], self.self_loaded)
        load(self.wout_raw[:, :, :], ap["L0_attn_w_out"].rearrange("(g i) d -> i g d", i=D), self.self_loaded)
        load(self.wkv_raw[:, 0, :], ap["L0_attn_w_k"], self.self_loaded)
        load(self.wkv_raw[:, 1, :], ap["L0_attn_w_v"], self.self_loaded)

    def self_sync_small(self, sp):
        ap, D = self.ap, SelfAttention.D
        load = lambda dst, src: sp.dma_start(dst, src).then_inc(self.self_small, 16)
        row = lambda name: ap[name].rearrange("(a d) -> a d", a=1)
        for half in range(2):
            rows = slice(half * D, (half + 1) * D)
            load(self.wgate_raw[rows, :], ap["L0_attn_w_gate"])
            load(self.gq_col[rows, :], ap["L0_attn_g_qnorm"].rearrange("(d a) -> d a", a=1))
            h = SelfAttention.H
            load(self.sink2[:, half * h:(half + 1) * h], row("L0_attn_sink_logit").broadcast_to([P, h]))
        load(self.gq_row[:, :], row("L0_attn_g_qnorm").broadcast_to([P, D]))
        load(self.gk_row[:, :], row("L0_attn_g_knorm").broadcast_to([P, D]))
        load(self.bgate_sb[:, :], row("L0_attn_b_gate").broadcast_to([P, 3]))
        load(self.rope_sb[:, :, :], ap["rope"].rearrange("(s p) d -> p s d", p=P))

    def self_pool(self, pool):
        H, D, CR = SelfAttention.H, SelfAttention.D, SelfAttention.CR
        NB = self.S // CR
        pool.memset(self.maskq_a[:, :], 0.0)
        pool.memset(self.maskk_a[:, :], 0.0)
        pool.memset(self.maskc[:, :, :], 0.0)
        pool.memset(self.headmask[:, :, :, :], 1.0)
        pool.memset(self.blockmean[:, :, :], 1.0 / CR)
        pool.memset(self.select[:, :, :], 1.0)
        pool.memset(self.zero16[:, :], 0.0)
        self.self_st.done(self.selfatt.clear(pool))

        def keep(t, base, mult, pattern, fill=NEG):
            return pool.affine_select(out=t, in_=t, compare_op=ALU.is_ge, fill=fill, base=base, pattern=pattern,
                                      channel_multiplier=mult)

        step = self.self_st.done
        q, k, hm = self.maskq_a, self.maskk_a, self.headmask
        halves = [(half, slice(half * 64, (half + 1) * 64)) for half in range(2)]
        keep(q[:, 0:128], 0, 1, [[-1, 128]])
        keep(q[:, 256:320], -64, 1, [[-1, 64]])
        keep(q[:, 320:512], 64, 1, [[-1, 192]])
        keep(k[:, 0:128], 0, -1, [[1, 128]])
        keep(k[:, 128:256], 64, -1, [[0, 2], [1, 64]])
        keep(k[:, 256:448], 0, -1, [[1, 192]])
        keep(k[:, 448:512], 0, -1, [[1, 64]])
        keep(self.maskc[:, :, :], 1 - CR, 1, [[P, 2], [-CR, NB]])
        keep(self.blockmean[:, :, :], 0, 1, [[P, 2], [-CR, NB]], 0.0)
        step(keep(self.select[:, :, :], 0, 1, [[-2, 2 * H], [0, P]], 0.0))
        keep(q[:, 0:128], 63, -1, [[1, 128]])
        keep(k[:, 0:128], 63, 1, [[-1, 128]])
        keep(k[:, 128:256], -1, 1, [[0, 2], [-1, 64]])
        keep(self.blockmean[:, :, :], CR - 1, -1, [[-P, 2], [CR, NB]], 0.0)
        step(keep(self.select[:, :, :], 1, -1, [[2, 2 * H], [0, P]], 0.0))
        for half, rows in halves:
            step(keep(q[rows, 128:256], 64, 1, [[-1, 128]]))
            step(keep(q[rows, 128:256], -1, -1, [[1, 128]]))
            for sign in (-1, 1):
                step(keep(hm[rows, :, :, :].rearrange("p c h n -> p (c h n)"), sign * half, 0,
                          [[2 * sign, 4], [-sign, H], [0, NB]], 0.0))
        pool.memset(self.zero16[:, :], 0.0).then_inc(self.consts_ready, 1)

    def self_tensor(self, pe):
        ps, D = self.ps, SelfAttention.D
        pe.wait_ge(self.self_loaded, 16 * self.SELF_LOADS)
        pe.transpose(ps[0:32, 2, 0:P], self.wqc_raw[:, :], self.identF[:, :])
        for c in range(4):
            last = pe.transpose(ps[0:D, 1, c * P:(c + 1) * P], self.wog_raw[:, c, :], self.identF[:, :])
        last.then_inc(self.self_T_ps, 1)
        pe.wait_ge(self.self_T, 2)
        pe.matmul(ps[:, 0, :], self.wqcT[:, :], self.wqup_raw[:, :], start=True, stop=True)
        for c in range(4):
            last = pe.matmul(ps[:, 3, c * P:(c + 1) * P], self.wogT[:, c, :], self.wout_raw[:, c // 2, :],
                             start=(c == 0), stop=(c == 3), skip_group_check=True)
        last.then_inc(self.self_ps, 1)

    def self_vector(self, dve):
        ps, st = self.ps, self.self_dst
        H, NB = SelfAttention.H, self.S // SelfAttention.CR
        dve.wait_ge(self.self_loaded, 16 * self.SELF_LOADS)
        raw = self.wkv_raw[:, :, :].rearrange("p a d -> p (a d)")
        st.done(dve.tensor_scalar(self.aKV_hi[:, :], raw, WS, None, ALU.mult))
        dve.scalar_tensor_tensor(self.aKV_lo[:, :], raw, WS, self.aKV_hi[:, :], ALU.mult, ALU.subtract)
        dve.wait_ge(self.self_T_ps, 1)
        dve.tensor_copy(self.wqcT[:, :], ps[0:32, 2, 0:P]).then_inc(self.self_T, 1)
        dve.tensor_copy(self.wogT[:, :, :].rearrange("p c d -> p (c d)"), ps[0:64, 1, :]).then_inc(self.self_T, 1)
        dve.wait_ge(self.self_small, 16 * self.SELF_SMALL)
        dve.wait_ge(self.consts_ready, 2)
        dve.scalar_tensor_tensor(self.gqk_sb[:, :], self.gq_row[:, :], 0.125, self.gk_row[:, :], ALU.mult, ALU.mult)
        for par in range(2):
            dve.tensor_scalar(self.selfatt.nm[:, par, SelfAttention.SINK, :, :].rearrange("p s h -> p (s h)"),
                              self.sink2[:, :], -1.0, None, ALU.mult)
        st.done(dve.tensor_scalar(self.wg_sb[:, :], self.wgate_raw[:, :], self.gq_col[:, 0:1], None, ALU.mult))
        kcg = self.selfatt.kcg
        st.done(dve.tensor_copy(kcg[:, 0, NB:], self.wg_sb[:, :]))
        dve.tensor_tensor(kcg[:, 1, NB:], self.wg_sb[:, :], kcg[:, 0, NB:], ALU.subtract)
        dve.wait_ge(self.self_ps, 1)
        st.done(dve.tensor_scalar(self.WQ_hi[:, :], ps[:, 0, :], WS, None, ALU.mult))
        dve.tensor_copy(self.Weff[:, :, :].rearrange("p c d -> p (c d)"), ps[:, 3, :])
        dve.scalar_tensor_tensor(self.WQ_lo[:, :], ps[:, 0, :], WS, self.WQ_hi[:, :], ALU.mult, ALU.subtract)\
            .then_inc(self.self_ready, 1)


class Layer(SelfWeights):

    EPS = 1e-5

    def __init__(self, nc, ctx, ap):
        self.nc, self.ctx, self.ap = nc, ctx, ap
        self.scope = ctx
        self.B, self.S, _ = ap["x"].shape
        self.tiles = self.B * self.S // P
        self.tile0 = self.S // P
        self.after = 4
        self.W1, self.W2 = ap["L0_ffn_W1"], ap["L0_ffn_W2"]
        self.E = self.W1.shape[0]
        C = self.W1.shape[2] // P
        self.C = C
        self.ps = ctx.enter_context(nc.psum_tensor("ps", [P, 8, 512], F32))
        sb = self.sb
        self.x_all = sb("x_all", [P, self.tile0 + self.tiles + self.after, P], F32)
        self.x_v = ap["x"].rearrange("b (s p) d -> p (b s) d", p=P)
        self.out_v = ap["out"].rearrange("b (s p) d -> p (b s) d", p=P)
        self.ffn_raw = sb("ffn_raw", [P, 2, C * P], F32)
        self.W1hi = sb("W1hi", [P, self.E, C * P], F16)
        self.W1lo = sb("W1lo", [P, self.E, C * P], F16)
        self.W2hi = sb("W2hi", [P, self.E, C, P], F16)
        self.W2lo = sb("W2lo", [P, self.E, C, P], F16)
        self.b1_raw = sb("b1_raw", [self.E * C, P], F32)
        self.b1_sb = sb("b1_sb", [P, self.E * C], F32)
        self.Wg_sb = sb("Wg_sb", [P, self.E], F32)
        self.bg_sb = sb("bg_sb", [P, self.E], F32)
        self.b2_raw = sb("b2_raw", [32, P], F32)
        self.b2_rest = sb("b2_rest", [32, P], F32)
        self.b2parts = sb("b2parts", [32, 3, P], BF16)
        self.identF = sb("identF", [P, P], F32)
        self.identB = sb("identB", [P, P], BF16)
        self.ident16 = sb("ident16", [P, P], F16)
        self.pick = sb("pick", [32, self.E, P], BF16)
        self.gp = sb("f_gp", [P, self.C * P // P, 32], BF16)
        self.iota8 = sb("iota8", [P, 8], F32)
        self.minus_half = sb("minus_half", [P, 64], F32)
        self.spare = sb("spare", [P, 2], F32)
        self.euler = sb("euler", [P, 64], F32)
        sem = self.sem
        self.pool_step = Count(sem("pool_setup_steps"), 0)
        self.dve_step = Count(sem("dve_setup_steps"), 0)
        self.consts_ready = sem("consts_ready")
        self.x_loaded = [sem(f"x_loaded{i}") for i in range(2)]
        self.ffn_loaded = sem("ffn_loaded")
        self.small_loaded = sem("small_loaded")
        self.ffn_split = Count(sem("ffn_split"), 1, 1)
        self.split_step = Count(sem("ffn_split_steps"), 1)
        self.b2_split = sem("b2_split")
        self.b2_zero = sem("b2_zero")
        self.b1T_ready = sem("b1T_ready")
        self.b1_ready = sem("b1_ready")
        B, H = self.B, P
        self.ctx_all = sb("ctx_all", [ap["ctx_1024"].shape[1], B + 2, P], F32)
        self.xw_raw = sb("xw_raw", [P, 3, P], F32)
        self.xw_hi = sb("xw_hi", [P, 3, P], F16)
        self.xw_lo = sb("xw_lo", [P, 3, P], F16)
        self.Wq_hi, self.Wq_lo = self.xw_hi[:, 0, :], self.xw_lo[:, 0, :]
        self.Wkv_hi, self.Wkv_lo = (w[:, 1:3, :].rearrange("p a d -> p (a d)") for w in (self.xw_hi, self.xw_lo))
        self.Wout_sb = sb("Wout_sb", [P, P], F32)
        self.bout_sb = sb("bout_sb", [1, P], F32)
        self.one_row = sb("one_row", [1, P], F32)
        self.maskq_x = sb("maskq_x", [P, P], BF16)
        self.maskk_x = sb("maskk_x", [P, 64 + P], BF16)
        self.x_weights_loaded = sem("x_weights_loaded")
        self.ctx_loaded = sem("ctx_loaded")
        self.x_split = sem("x_split")
        self.x_used = sem("x_phase_done")
        self.cross = Cross(self)
        with ExitStack() as self.scope:
            self.self_alloc()
            self.selfatt = SelfAttention(self)
        with ExitStack() as self.scope:
            self.cross.alloc()
        self.scope = ctx
        self.experts = Experts(self)

    def sb(self, name, shape, dt):
        return self.scope.enter_context(self.nc.sbuf_tensor(name, shape, dt))

    def sem(self, name):
        return self.ctx.enter_context(self.nc.semaphore(name))

    SMALL = 6

    def sync_setup(self, sp):
        ap, first = self.ap, 4
        t0 = self.tile0
        self.self_sync(sp)
        sp.dma_start(self.x_all[:, t0:t0 + first, :], self.x_v[:, 0:first, :]).then_inc(self.x_loaded[0], 16)
        sp.dma_start(self.x_all[:, t0 + first:t0 + self.tiles, :], self.x_v[:, first:self.tiles, :])\
            .then_inc(self.x_loaded[1], 16)
        self.self_sync_small(sp)
        sp.dma_start(self.b1_raw[:, :], ap["L0_ffn_b1"].rearrange("e (c p) -> (e c) p", p=P))\
            .then_inc(self.small_loaded, 16)
        sp.dma_start(self.Wg_sb[:, :], ap["L0_ffn_Wg"]).then_inc(self.small_loaded, 16)
        sp.dma_start(self.bg_sb[:, :], ap["L0_ffn_bg"].rearrange("(a e) -> a e", a=1).broadcast_to([P, self.E]))\
            .then_inc(self.small_loaded, 16)
        sp.dma_start(self.xw_raw[:, 0, :], ap["L0_xattn_Wq"]).then_inc(self.x_weights_loaded, 16)
        sp.dma_start(self.xw_raw[:, 1:3, :].rearrange("p a d -> p (a d)"), ap["L0_xattn_Wkv"])\
            .then_inc(self.x_weights_loaded, 16)
        sp.dma_start(self.Wout_sb[:, :], ap["L0_xattn_Wout"]).then_inc(self.x_weights_loaded, 16)
        sp.dma_start(self.bout_sb[:, :], ap["L0_xattn_bout"].rearrange("(a d) -> a d", a=1))\
            .then_inc(self.x_weights_loaded, 16)
        sp.dma_start(self.ctx_all[:, 0:self.B, :], ap["ctx_1024"].rearrange("b m d -> m b d"))\
            .then_inc(self.ctx_loaded, 16)
        sp.wait_ge(self.b2_zero, 1)
        for m in range(3):
            sp.dma_start(self.b2_raw[m * self.E:(m + 1) * self.E, :], ap["L0_ffn_b2"])\
                .then_inc(self.small_loaded, 16)
        self.sync_experts(sp)

    def sync_experts(self, sp):
        with sp.Fori(0, self.E) as e:
            sp.wait_ge(self.ffn_split.sem, self.ffn_split.value(e, 0))
            sp.dma_start(self.ffn_raw[:, 0, :], self.W1[e]).then_inc(self.ffn_loaded, 16)
            sp.dma_start(self.ffn_raw[:, 1, :].rearrange("p (c d) -> p c d", d=P),
                         self.W2[e].rearrange("(c p) d -> p c d", p=P)).then_inc(self.ffn_loaded, 16)

    def split_expert(self, dve, e):
        dve.wait_ge(self.ffn_loaded, e * 32 + 32)
        st = Steps(dve, self.split_step)
        st.start(e)
        W2hi, W2lo = (w[:, e, :, :].rearrange("p c d -> p (c d)") for w in (self.W2hi, self.W2lo))
        dve.tensor_scalar(self.W1hi[:, e, :], self.ffn_raw[:, 0, :], WS, None, ALU.mult)
        st.done(dve.tensor_scalar(W2hi, self.ffn_raw[:, 1, :], WS, None, ALU.mult))
        dve.scalar_tensor_tensor(self.W1lo[:, e, :], self.ffn_raw[:, 0, :], WS, self.W1hi[:, e, :],
                                 ALU.mult, ALU.subtract)
        dve.scalar_tensor_tensor(W2lo, self.ffn_raw[:, 1, :], WS, W2hi, ALU.mult, ALU.subtract)\
            .then_inc(self.ffn_split.sem, 1)

    def gpsimd_setup(self, pool):
        st = Steps(pool, self.pool_step)
        pool.memset(self.b2_raw[:, :], 0.0).then_inc(self.b2_zero, 1)
        pool.memset(self.x_all[:, 0:self.tile0, :], 0.0)
        pool.memset(self.x_all[:, self.tile0 + self.tiles:, :], 0.0)
        pool.memset(self.minus_half[:, :], -0.5)
        pool.memset(self.spare[:, :], 0.0)
        pool.memset(self.euler[:, :], 2.718281828459045)
        pool.memset(self.gp[:, :, :], 0.0)
        pool.memset(self.ctx_all[:, self.B:, :], 0.0)
        pool.memset(self.one_row[:, :], 1.0)
        pool.memset(self.maskq_x[:, :], 0.0)
        pool.memset(self.maskk_x[:, :], 0.0)
        st.done(self.cross.clear(pool))
        st.done(self.cross.ones(pool))
        pool.memset(self.identF[:, :], 0.0)
        st.done(pool.memset(self.pick[:, :, :], 0.0))
        st.done(pool.affine_select(out=self.identF[:, :], in_=self.identF[:, :], compare_op=ALU.not_equal, fill=1.0,
                                   base=0, pattern=[[-1, P]], channel_multiplier=1))
        pool.tensor_copy(self.ident16[:, :], self.identF[:, :])
        for m in range(3):
            st.done(pool.affine_select(out=self.pick[:, :, :], in_=self.pick[:, :, :], compare_op=ALU.not_equal,
                                       fill=1.0 / WS, base=-m * self.E, pattern=[[-1, self.E], [0, P]],
                                       channel_multiplier=1))
        pool.affine_select(out=self.maskq_x[:, :], in_=self.maskq_x[:, :], compare_op=ALU.is_ge, fill=NEG,
                           base=0, pattern=[[-1, P]], channel_multiplier=1)
        pool.affine_select(out=self.maskk_x[:, 0:64], in_=self.maskk_x[:, 0:64], compare_op=ALU.is_ge, fill=NEG,
                           base=64, pattern=[[1, 64]], channel_multiplier=-1)
        pool.affine_select(out=self.maskk_x[:, 64:], in_=self.maskk_x[:, 64:], compare_op=ALU.is_ge, fill=NEG,
                           base=0, pattern=[[1, P]], channel_multiplier=-1)
        pool.iota(self.iota8[:, :], pattern=[[1, 8]], base=0, channel_multiplier=0,
                  allow_small_or_imprecise_dtypes=True)
        pool.tensor_copy(self.identB[:, :], self.identF[:, :]).then_inc(self.consts_ready, 1)
        self.self_st = st
        self.self_pool(pool)
        self.selfatt.credits(pool)
        pool.sem_inc(self.ffn_split.sem, self.ffn_split.credit)
        self.cross.credits(pool)
        self.experts.credits(pool)

    def vector_setup(self, dve):
        st = self.self_dst = Steps(dve, self.dve_step)
        self.self_vector(dve)
        dve.wait_ge(self.x_weights_loaded, 16 * 4)
        st.done(dve.tensor_scalar(self.xw_hi[:, :, :], self.xw_raw[:, :, :], WS, None, ALU.mult))
        dve.scalar_tensor_tensor(self.xw_lo[:, :, :], self.xw_raw[:, :, :], WS, self.xw_hi[:, :, :],
                                 ALU.mult, ALU.subtract).then_inc(self.x_split, 1)
        dve.wait_ge(self.ctx_loaded, 16)
        dve.wait_ge(self.small_loaded, 16 * self.SMALL)
        st.done(dve.tensor_copy(self.b2parts[:, 0, :], self.b2_raw[:, :]))
        st.done(dve.tensor_tensor(self.b2_rest[:, :], self.b2_raw[:, :], self.b2parts[:, 0, :], ALU.subtract))
        st.done(dve.tensor_copy(self.b2parts[:, 1, :], self.b2_rest[:, :]))
        dve.tensor_tensor(self.b2parts[:, 2, :], self.b2_rest[:, :], self.b2parts[:, 1, :], ALU.subtract)\
            .then_inc(self.b2_split, 1)
        dve.wait_ge(self.b1T_ready, 1)
        dve.tensor_copy(self.b1_sb[:, :], self.ps[:, 7, 0:self.E * self.C]).then_inc(self.b1_ready, 1)
        for s in self.x_loaded:
            dve.wait_ge(s, 16)
        dve.wait_ge(self.consts_ready, 1)

    def tensor_setup(self, pe):
        pe.wait_ge(self.consts_ready, 1)
        pe.wait_ge(self.small_loaded, 16 * self.SMALL)
        self.self_tensor(pe)
        pe.wait_ge(self.self_ready, 1)
        pe.wait_ge(self.consts_ready, 2)
        n = self.E * self.C
        pe.transpose(self.ps[:, 7, 0:n], self.b1_raw[:, :], self.identF[0:n, 0:n]).then_inc(self.b1T_ready, 1)
        pe.wait_ge(self.b1_ready, 1)
        pe.wait_ge(self.b2_split, 1)
        pe.wait_ge(self.x_split, 1)
        pe.wait_ge(self.x_weights_loaded, 16 * 4)

    def scalar_setup(self, act):
        act.wait_ge(self.b1_ready, 1)

    def build(self):
        block = self.ctx.enter_context(self.nc.Block())

        @block.sync
        def _(sp):
            self.sync_setup(sp)
            self.experts.sync(sp)

        @block.gpsimd
        def _(pool):
            self.gpsimd_setup(pool)
            self.selfatt.gpsimd(pool)
            pool.wait_ge(self.selfatt.x_done.sem, self.selfatt.x_done.value(self.B, 1))
            self.cross.gpsimd(pool)
            self.experts.gpsimd(pool)

        @block.vector
        def _(dve):
            self.vector_setup(dve)
            self.selfatt.vector(dve)
            dve.wait_ge(self.selfatt.x_done.sem, self.selfatt.x_done.value(self.B, 1))
            self.cross.vector(dve)
            dve.wait_ge(self.cross.x_done.sem, self.cross.x_done.value(self.B, 1))
            self.experts.vector(dve)

        @block.scalar
        def _(act):
            self.scalar_setup(act)
            self.selfatt.scalar(act)
            self.cross.scalar(act)
            self.experts.scalar(act)

        @block.tensor
        def _(pe):
            self.tensor_setup(pe)
            self.selfatt.tensor(pe)
            self.cross.tensor(pe)
            pe.wait_ge(self.ffn_split.sem, self.ffn_split.value(self.E, 0))
            self.experts.tensor(pe)


def decoder_layer(nc, ap):
    with ExitStack() as ctx:
        Layer(nc, ctx, ap).build()


_OUT = ((16, 256, 128), 'float32')


def rope_table(positions, half, theta=10000.0):
    import numpy as np
    inv = np.float32(1.0) / np.float32(theta) ** (np.arange(half, dtype=np.float32) * np.float32(2.0)
                                                  / np.float32(2 * half))
    ang = np.arange(positions, dtype=np.float32)[:, None] * inv[None, :]
    cos, sin = np.cos(ang), np.sin(ang)
    return np.concatenate([cos, cos, -sin, sin], axis=1)


def kernel(**inputs):
    import numpy as _np
    import concourse.bacc as _bacc
    from concourse import mybir as _mybir
    from concourse.bass_utils import run_bass_kernel_spmd as _run

    nc = _bacc.Bacc("TRN2", target_bir_lowering=False, num_devices=1)
    arrays, ap = {}, {}
    inputs["rope"] = rope_table(inputs["x"].shape[1], 16)
    for name, value in inputs.items():
        a = _np.ascontiguousarray(value)
        arrays[f"in_{name}_dram"] = a
        ap[name] = nc.dram_tensor(f"in_{name}_dram", a.shape, _mybir.dt.from_np(a.dtype), kind="ExternalInput").ap()
    ap["out"] = nc.dram_tensor("out_dram", _OUT[0], _mybir.dt.from_np(_np.dtype(_OUT[1])), kind="ExternalOutput").ap()
    decoder_layer(nc, ap)
    r = _run(nc, [arrays], core_ids=[0])
    return r.results[0]["out_dram"]
```

```python
from contextlib import ExitStack

import concourse.bass as bass
from concourse import mybir

F32 = mybir.dt.float32
F16 = mybir.dt.float16
BF16 = mybir.dt.bfloat16
U32 = mybir.dt.uint32
ALU = mybir.AluOpType
ACT = mybir.ActivationFunctionType
AX = mybir.AxisListType

P = 128
NEG = -1e30
WS = 64.0
CLAMP = 60000.0


class Count:

    def __init__(self, sem, per, credit=0):
        self.sem, self.per, self.credit = sem, per, credit

    def value(self, rounds, k):
        return rounds * self.per + (k + self.credit)


class Steps:

    def __init__(self, eng, count):
        self.eng, self.count, self.rounds, self.k = eng, count, 0, 0

    def start(self, rounds):
        self.rounds, self.k = rounds, 0

    def done(self, ins):
        self.k += 1
        ins.then_inc(self.count.sem, 1)
        self.eng.wait_ge(self.count.sem, self.count.value(self.rounds, self.k))

    def carry(self, spare):
        self.eng.tensor_copy(spare[:, 1:2], spare[:, 0:1])

    def finish(self):
        assert self.k == self.count.per, f"{self.k} steps in a round, not {self.count.per}"


def bc(ap, axis, n):
    ap = ap.unsqueeze(axis)
    shape = list(ap.shape)
    shape[axis] = n
    return ap.broadcast_to(shape)


class Experts:

    TOK = 512
    T = TOK // P
    LEAD = 3
    HB = 4
    DVE_STEPS = 20

    def __init__(self, k):
        self.k = k
        sb, sem = k.sb, k.sem
        self.E, self.F, self.H = k.E, P, k.W1.shape[2]
        self.C = self.H // P
        self.J = self.E * self.C
        self.G = k.tiles // self.T
        self.xn = sb("f_xn", [P, self.T, P], F32)
        self.x32 = sb("f_x32", [P, self.TOK], F32)
        self.xhi = sb("f_xhi", [P, 2, self.TOK], F16)
        self.xlo = sb("f_xlo", [P, 2, self.TOK], F16)
        self.stats = sb("f_stats", [P, self.T, 6], F32)
        self.mv = sb("f_mv", [P, self.T, 2], F32)
        self.ve = sb("f_ve", [P, self.T], F32)
        self.rstd = sb("f_rstd", [P, self.T], F32)
        E, T = self.E, self.T
        self.lg = sb("f_lg", [P, T, E], F32)
        self.mx = sb("f_mx", [P, T], F32)
        self.ex = sb("f_ex", [P, T, E], F32)
        self.z = sb("f_z", [P, T], F32)
        self.zr = sb("f_zr", [P, T], F32)
        self.pr = sb("f_pr", [P, T, E], F32)
        self.top = sb("f_top", [P, T, 8], F32)
        self.topi = sb("f_topi", [P, T, 8], U32)
        self.topf = sb("f_topf", [P, T, 8], F32)
        self.m1 = sb("f_m1", [P, T, E], F32)
        self.m2 = sb("f_m2", [P, T, E], F32)
        self.gs = sb("f_gs", [P, T, E], F32)
        self.gp = k.gp
        self.gT = sb("f_gT", [32, 2, self.TOK], BF16)
        self.Gb = sb("f_Gb", [P, 2, E, self.TOK], F32)
        self.h32 = sb("f_h32", [P, self.HB, self.TOK], F32)
        self.hhi = sb("f_hhi", [P, self.HB, self.TOK], F16)
        self.hlo = sb("f_hlo", [P, self.HB, self.TOK], F16)
        self.acc = sb("f_acc", [P, self.TOK], F32)
        self.tmp = sb("f_tmp", [P, 2, self.TOK], F32)
        self.ost = sb("f_ost", [P, 2, T, P], F32)
        S = lambda name, per, credit=0: Count(sem("f_" + name), per, credit)
        self.h_ready = S("h_ready", self.J)
        self.gelu_done = S("gelu_done", self.J, self.HB)
        self.lo_done = S("lo_done", self.J, self.HB)
        self.h_used = S("h_used", self.J, self.HB)
        self.o_used = S("o_used", E, 2)
        self.acc_ready = S("acc_ready", 1)
        self.out_ready = S("out_ready", 1)
        self.out_sum = S("out_sum", 1, 1)
        self.stored = [S(f"stored{i}", 16, 16 + 16 * i) for i in range(2)]
        self.zeroed = sem("f_zeroed")
        self.ve_ready = S("ve_ready", 1)
        self.rstd_ready = S("rstd_ready", 1)
        self.xn_ready = S("xn_ready", 1)
        self.xT_ready = S("xT_ready", 1)
        self.xhi_ready = S("xhi_ready", 1)
        self.xlo_ready = S("xlo_ready", 1)
        self.lg_ready = S("lg_ready", 1)
        self.shift_ready = S("shift_ready", 1)
        self.ex_ready = S("ex_ready", 1)
        self.gp_ready = S("gp_ready", 1)
        self.gpT_ready = S("gpT_ready", 1)
        self.gT_ready = S("gT_ready", 1)
        self.Gps_ready = S("Gps_ready", E)
        self.added = S("added", E - 2, E - 2)
        self.Gb_ready = [S(f"Gb_ready{i}", E // 2, 1) for i in range(2)]
        self.steps = S("dve_steps", self.DVE_STEPS)
        self.M0, self.M1 = k.ps[:, 6, :], k.ps[:, 7, :]

    def h_bank(self, j):
        return self.k.ps[:, j % self.HB, :]

    def o_bank(self, e):
        return self.k.ps[:, 4 + e % 2, :]

    def credits(self, eng):
        for s in (self.gelu_done, self.lo_done, self.out_sum, self.added, *self.Gb_ready, *self.stored):
            eng.sem_inc(s.sem, s.credit)
        for s in (self.h_used, self.o_used):
            eng.sem_inc(s.sem, s.credit - 1)

    def pe_prep(self, pe, n, par, j, n_out=None):
        k = self.k
        if j == 4:
            pe.wait_ge(self.xn_ready.sem, self.xn_ready.value(n, 1))
            pe.wait_ge(self.Gb_ready[0].sem, self.Gb_ready[0].value(n, 0))
            for i in range(self.T):
                last = pe.transpose(self.M0[:, i * P:(i + 1) * P], self.xn[:, i, :], k.identF[:, :])
            last.then_inc(self.xT_ready.sem, 1)
        if j == 7:
            pe.wait_ge(self.xlo_ready.sem, self.xlo_ready.value(n, 1))
            for i in range(self.T):
                last = pe.matmul(self.M0[:, i * self.E:(i + 1) * self.E], self.x32[:, i * P:(i + 1) * P],
                                 k.Wg_sb[:, :], start=True, stop=True)
            last.then_inc(self.lg_ready.sem, 1)
        if j == 20:
            pe.wait_ge(self.gp_ready.sem, self.gp_ready.value(n, 1))
            for i in range(self.T):
                last = pe.transpose(self.M0[0:32, :].bitcast(BF16)[:, i * P:(i + 1) * P], self.gp[:, i, :],
                                    k.identB[:, :])
            last.then_inc(self.gpT_ready.sem, 1)
        if 22 <= j < 22 + self.E:
            e = j - 22
            if e == 0:
                pe.wait_ge(self.gT_ready.sem, self.gT_ready.value(n, 1))
                if n_out is not None:
                    pe.wait_ge(self.out_sum.sem, self.out_sum.value(n_out, 1))
            if e > 1:
                pe.wait_ge(self.Gb_ready[e % 2].sem, self.Gb_ready[e % 2].value(n, e // 2))
            pe.matmul((self.M0, self.M1)[e % 2], k.pick[:, e, :], self.gT[:, par, :], start=True,
                      stop=True).then_inc(self.Gps_ready.sem, 1)

    def pe_first(self, pe, g, par, j):
        k, e, c = self.k, j // self.C, j % self.C
        w = slice(c * P, (c + 1) * P)
        if j == 0:
            pe.wait_ge(self.xlo_ready.sem, self.xlo_ready.value(g, 1))
        pe.wait_ge(self.gelu_done.sem, self.gelu_done.value(g, j - self.HB + 1))
        H = self.h_bank(j)
        pe.matmul(H, k.W1hi[:, e, w], self.xhi[:, par, :], start=True, stop=False)
        pe.matmul(H, k.W1hi[:, e, w], self.xlo[:, par, :], start=False, stop=False)
        pe.matmul(H, k.W1lo[:, e, w], self.xhi[:, par, :], start=False, stop=True)\
            .then_inc(self.h_ready.sem, 1)

    def pe_second(self, pe, g, j):
        k, e, c = self.k, j // self.C, j % self.C
        if c == 0:
            pe.wait_ge(self.o_used.sem, self.o_used.value(g, e - 1))
        pe.wait_ge(self.gelu_done.sem, self.gelu_done.value(g, j + 1))
        O, b = self.o_bank(e), j % self.HB
        pe.matmul(O, k.W2hi[:, e, c, :], self.hhi[:, b, :], start=(c == 0), stop=False)
        pe.matmul(O, k.W2lo[:, e, c, :], self.hhi[:, b, :], start=False, stop=False)
        pe.wait_ge(self.lo_done.sem, self.lo_done.value(g, j + 1))
        last = pe.matmul(O, k.W2hi[:, e, c, :], self.hlo[:, b, :], start=False, stop=(c == self.C - 1))
        last.then_inc(self.h_used.sem, 1)

    def tensor(self, pe):
        k = self.k
        pe.wait_ge(self.zeroed, 1)
        pe.matmul(self.o_bank(self.E - 1), k.pick[:, 0, :], self.gT[:, 1, :], start=True, stop=True)\
            .then_inc(self.h_used.sem, 1)
        for j in range(self.J):
            self.pe_prep(pe, 0, 0, j)
        for j in range(self.LEAD):
            self.pe_first(pe, 0, 0, j)
        with pe.Fori(0, self.G // 2) as i:
            for par in range(2):
                g = i * 2 + par
                for j in range(self.J):
                    self.pe_prep(pe, g + 1, 1 - par, j, n_out=g)
                    if j + self.LEAD < self.J:
                        self.pe_first(pe, g, par, j + self.LEAD)
                    else:
                        self.pe_first(pe, g + 1, 1 - par, j + self.LEAD - self.J)
                    self.pe_second(pe, g, j)
                    if j == 4:
                        self.pe_output(pe, g, 1 - par)
        self.pe_output(pe, self.G, 1)

    def pe_output(self, pe, g1, par):
        k = self.k
        pe.wait_ge(self.Gb_ready[1].sem, self.Gb_ready[1].value(g1, self.E // 2))
        for t in range(self.T):
            for m in range(3):
                pe.matmul(self.M1[:, t * P:(t + 1) * P], self.gT[:, par, t * P:(t + 1) * P],
                          k.b2parts[:, m, :], start=(t == 0 and m == 0), stop=False, skip_group_check=True)
        pe.wait_ge(self.acc_ready.sem, self.acc_ready.value(g1, 1))
        for t in range(self.T):
            last = pe.matmul(self.M1[:, t * P:(t + 1) * P], self.acc[:, t * P:(t + 1) * P],
                             k.identF[:, :], start=False, stop=True, skip_group_check=True)
        last.then_inc(self.out_ready.sem, 1)

    def act_prep(self, act, n, par, j):
        if j == 6:
            act.wait_ge(self.xT_ready.sem, self.xT_ready.value(n, 1))
            act.copy(self.xhi[:, par, :], self.M0)
            act.copy(self.x32[:, :], self.M0).then_inc(self.xhi_ready.sem, 1)
        if j == 23:
            act.wait_ge(self.gpT_ready.sem, self.gpT_ready.value(n, 1))
            act.copy(self.gT[:, par, :], self.M0[0:32, :].bitcast(BF16)[:, 0:self.TOK])\
                .then_inc(self.gT_ready.sem, 1)
        if 25 <= j < 25 + self.E and j % 2 == 1:
            e = j - 25
            act.wait_ge(self.Gps_ready.sem, self.Gps_ready.value(n, e + 1))
            act.copy(self.Gb[:, par, e, :], self.M0).then_inc(self.Gb_ready[0].sem, 1)

    def scalar(self, act):
        k = self.k
        for j in range(self.J):
            if j == 7:
                act.wait_ge(self.shift_ready.sem, self.shift_ready.value(0, 1))
                act.activation(self.ex[:, :, :].rearrange("p t e -> p (t e)"),
                               self.lg[:, :, :].rearrange("p t e -> p (t e)"), ACT.Exp).then_inc(self.ex_ready.sem, 1)
            self.act_prep(act, 0, 0, j)
        with act.Fori(0, self.G // 2) as i:
            for par in range(2):
                g = i * 2 + par
                for j in range(self.J):
                    act.wait_ge(self.h_ready.sem, self.h_ready.value(g, j + 1))
                    act.wait_ge(self.lo_done.sem, self.lo_done.value(g, j - self.HB + 1))
                    act.activation(self.h32[:, j % self.HB, :], self.h_bank(j), ACT.Gelu_apprx_tanh,
                                   bias=k.b1_sb[:, j:j + 1], scale=1.0 / WS)
                    act.wait_ge(self.h_used.sem, self.h_used.value(g, j - self.HB + 1))
                    act.activation(self.hhi[:, j % self.HB, :], self.h_bank(j), ACT.Gelu_apprx_tanh,
                                   bias=k.b1_sb[:, j:j + 1], scale=1.0 / WS)\
                        .then_inc(self.gelu_done.sem, 1)
                    self.act_prep(act, g + 1, 1 - par, j)

    def gpsimd(self, pool):
        k = self.k
        pool.memset(self.gT[:, 1, :], 0.0)
        pool.memset(self.Gb[:, 1, self.E - 1, :], 0.0)
        pool.memset(self.acc[:, :], 0.0).then_inc(self.zeroed, 1)
        self.pool_rstd(pool, 0)
        with pool.Fori(1, self.G + 1) as n:
            self.pool_rstd(pool, n)
            pool.wait_ge(self.shift_ready.sem, self.shift_ready.value(n, 1))
            pool.tensor_tensor(self.ex[:, :, :].rearrange("p t e -> p (t e)"), k.euler[:, 0:self.T * self.E],
                               self.lg[:, :, :].rearrange("p t e -> p (t e)"), ALU.pow)\
                .then_inc(self.ex_ready.sem, 1)
            for e in range(1, self.E - 1):
                pool.wait_ge(self.o_used.sem, self.o_used.value(n - 1, e + 1))
                if e > 1:
                    pool.wait_ge(self.added.sem, self.added.value(n - 1, e - 1))
                pool.tensor_tensor(self.acc[:, :], self.acc[:, :], self.tmp[:, e % 2, :], ALU.add)\
                    .then_inc(self.added.sem, 1)

    def pool_rstd(self, pool, n):
        pool.wait_ge(self.ve_ready.sem, self.ve_ready.value(n, 1))
        pool.tensor_tensor(self.rstd[:, :], self.ve[:, :], self.k.minus_half[:, 0:self.T], ALU.pow)\
            .then_inc(self.rstd_ready.sem, 1)

    def dve_prep(self, dve, st, n, par, j):
        k, T = self.k, self.T
        if j == 0:
            st.start(n)
            for i in range(T):
                last = dve.bn_stats(self.stats[:, i, :], k.x_all[:, k.tile0 + n * T + i, :])
            st.done(last)
            st.carry(k.spare)
            for i in range(T):
                last = dve.bn_aggr(self.mv[:, i, :], self.stats[:, i, :])
            st.done(last)
            dve.tensor_scalar(self.ve[:, :], self.mv[:, :, 1], k.EPS, None, ALU.add)\
                .then_inc(self.ve_ready.sem, 1)
        if j == 2:
            dve.wait_ge(self.rstd_ready.sem, self.rstd_ready.value(n, 1))
            for i in range(T):
                last = dve.tensor_scalar(self.xn[:, i, :], k.x_all[:, k.tile0 + n * T + i, :],
                                         self.mv[:, i, 0:1], self.rstd[:, i:i + 1], ALU.subtract, ALU.mult)
            last.then_inc(self.xn_ready.sem, 1)
        if j == 6:
            dve.wait_ge(self.xhi_ready.sem, self.xhi_ready.value(n, 1))
            dve.tensor_tensor(self.xlo[:, par, :], self.M0, self.xhi[:, par, :], ALU.subtract)\
                .then_inc(self.xlo_ready.sem, 1)
        if j == 9:
            dve.wait_ge(self.lg_ready.sem, self.lg_ready.value(n, 1))
            st.done(dve.tensor_tensor(self.lg[:, :, :], self.M0[:, 0:T * self.E].rearrange("p (t e) -> p t e", t=T),
                                      bc(k.bg_sb[:, :], 1, T), ALU.add))
            st.done(dve.tensor_reduce(self.mx[:, :], self.lg[:, :, :], AX.X, ALU.max))
            dve.tensor_tensor(self.lg[:, :, :], self.lg[:, :, :], bc(self.mx[:, :], 2, self.E), ALU.subtract)\
                .then_inc(self.shift_ready.sem, 1)
        if j == 13:
            dve.wait_ge(self.ex_ready.sem, self.ex_ready.value(n, 1))
            st.done(dve.tensor_reduce(self.z[:, :], self.ex[:, :, :], AX.X, ALU.add))
            st.done(dve.reciprocal(self.zr[:, :], self.z[:, :]))
            st.done(dve.tensor_tensor(self.pr[:, :, :], self.ex[:, :, :], bc(self.zr[:, :], 2, self.E), ALU.mult))
        if j == 15:
            for i in range(T):
                last = dve.max(self.top[:, i, :], self.pr[:, i, :])
            st.done(last)
            st.carry(k.spare)
            for i in range(T):
                last = dve.max_index(self.topi[:, i, :], self.top[:, i, :], self.pr[:, i, :])
            st.done(last)
        if j == 16:
            st.done(dve.tensor_copy(self.topf[:, :, :], self.topi[:, :, :]))
        if j in (16, 17):
            for i in range((j - 16) * T // 2, (j - 15) * T // 2):
                dve.tensor_scalar(self.m1[:, i, :], k.iota8[:, :], self.topf[:, i, 0:1], None, ALU.is_equal)
                last = dve.tensor_scalar(self.m2[:, i, :], k.iota8[:, :], self.topf[:, i, 1:2], None, ALU.is_equal)
        if j == 17:
            st.done(last)
            st.done(dve.tensor_tensor(self.m1[:, :, :], self.m1[:, :, :], self.m2[:, :, :], ALU.add))
            st.done(dve.tensor_tensor(self.pr[:, :, :], self.pr[:, :, :], self.m1[:, :, :], ALU.mult))
        if j == 19:
            st.done(dve.tensor_reduce(self.z[:, :], self.pr[:, :, :], AX.X, ALU.add))
            st.done(dve.tensor_scalar(self.z[:, :], self.z[:, :], 1e-8, None, ALU.add))
            st.done(dve.reciprocal(self.zr[:, :], self.z[:, :]))
            st.done(dve.tensor_tensor(self.gs[:, :, :], self.pr[:, :, :], bc(self.zr[:, :], 2, self.E), ALU.mult))
            E = self.E
            g1, g2, g3 = (self.gp[:, :, m * E:(m + 1) * E] for m in range(3))
            st.done(dve.tensor_copy(g1, self.gs[:, :, :]))
            st.done(dve.tensor_tensor(self.m1[:, :, :], self.gs[:, :, :], g1, ALU.subtract))
            st.done(dve.tensor_copy(g2, self.m1[:, :, :]))
            dve.tensor_tensor(g3, self.m1[:, :, :], g2, ALU.subtract).then_inc(self.gp_ready.sem, 1)
            st.finish()
        if 23 <= j < 23 + self.E and j % 2 == 0:
            e = j - 23
            dve.wait_ge(self.Gps_ready.sem, self.Gps_ready.value(n, e + 1))
            dve.tensor_copy(self.Gb[:, par, e, :], self.M1).then_inc(self.Gb_ready[1].sem, 1)

    def dve_weigh(self, dve, g, par, e):
        dve.wait_ge(self.h_used.sem, self.h_used.value(g, (e + 1) * self.C))
        if e == 0:
            for s in self.Gb_ready:
                dve.wait_ge(s.sem, s.value(g, self.E // 2))
        if e > 2:
            dve.wait_ge(self.added.sem, self.added.value(g, e - 2))
        out = self.acc[:, :] if e == 0 else self.tmp[:, e % 2, :]
        dve.tensor_tensor(out, self.o_bank(e), self.Gb[:, par, e, :], ALU.mult).then_inc(self.o_used.sem, 1)
        if e == self.E - 1:
            dve.wait_ge(self.added.sem, self.added.value(g, e - 1))
            dve.wait_ge(self.o_used.sem, self.o_used.value(g, e + 1))
            dve.tensor_tensor(self.acc[:, :], self.acc[:, :], self.tmp[:, e % 2, :], ALU.add)\
                .then_inc(self.acc_ready.sem, 1)

    def vector(self, dve):
        k = self.k
        st = Steps(dve, self.steps)
        for j in range(self.J):
            self.dve_prep(dve, st, 0, 0, j)
        dve.wait_ge(self.zeroed, 1)
        with dve.Fori(0, self.G // 2) as i:
            for par in range(2):
                g = i * 2 + par
                for j in range(self.J):
                    dve.wait_ge(self.gelu_done.sem, self.gelu_done.value(g, j + 1))
                    dve.tensor_tensor(self.hlo[:, j % self.HB, :], self.h32[:, j % self.HB, :],
                                      self.hhi[:, j % self.HB, :], ALU.subtract)\
                        .then_inc(self.lo_done.sem, 1)
                    if j == 6:
                        self.dve_output(dve, g, 1 - par, i)
                    if j % self.C == 2:
                        if j < self.C:
                            self.dve_weigh(dve, g - 1, 1 - par, self.E - 1)
                        else:
                            self.dve_weigh(dve, g, par, j // self.C - 1)
                    self.dve_prep(dve, st, g + 1, 1 - par, j)
        self.dve_weigh(dve, self.G - 1, 1, self.E - 1)
        self.dve_output(dve, self.G, 1, self.G // 2)

    def dve_output(self, dve, g1, par, i):
        dve.wait_ge(self.out_ready.sem, self.out_ready.value(g1, 1))
        stored = self.stored[par]
        dve.wait_ge(stored.sem, stored.value(i - par, 0))
        dve.tensor_tensor(self.ost[:, par, :, :], self.k.x_all[:, bass.ds(g1 * self.T, self.T), :],
                          self.M1.rearrange("p (t d) -> p t d", t=self.T), ALU.add)\
            .then_inc(self.out_sum.sem, 1)

    def sync(self, sp):
        k = self.k
        with sp.Fori(0, self.G // 2) as i:
            for par in range(2):
                g = i * 2 + par
                sp.wait_ge(self.out_sum.sem, self.out_sum.value(g + 1, 1))
                sp.dma_start(k.out_v[:, bass.ds(g * self.T, self.T), :], self.ost[:, par, :, :])\
                    .then_inc(self.stored[par].sem, 16)
        for s in self.stored:
            sp.wait_ge(s.sem, s.value(self.G // 2, 0))


class Cross:

    HEADS, D, ROWS = 16, 8, 24
    UNITS = 4
    EB = 4
    DVE_STEPS = 2

    def __init__(self, k):
        self.k = k
        sb, sem = k.sb, k.sem
        H = self.HEADS
        self.MEM = k.ap["ctx_1024"].shape[1]
        self.KEYS = self.MEM + k.S
        self.QS = sb("x_QS", [P, 2, 2, H, 32], F16)
        self.KS = sb("x_KS", [P, 3, H, 32], F16)
        self.VS = sb("x_VS", [P, 2, 3, H, 18], F16)
        self.O = sb("x_O", [P, 2, H * 18], F32)
        self.Os = sb("x_Os", [P, 2, H, 9], F32)
        S = lambda name, per, credit=0: Count(sem("x_" + name), per, credit)
        self.ve_ready = S("ve_ready", 1)
        self.rstd_ready = S("rstd_ready", 1)
        self.h2_ready = S("h2_ready", 1)
        self.bias_added = S("bias_added", 1)
        self.XT_ready = S("XT_ready", 1)
        self.XThi_ready = S("XThi_ready", 1)
        self.XTlo_ready = S("XTlo_ready", 1)
        self.kv01_ready = S("kv01_ready", 1)
        self.kvq_ready = S("kvq_ready", 1)
        self.hi_ready = S("hi_ready", 2)
        self.lo_ready = S("lo_ready", 2)
        self.KT_ps = S("KT_ps", 2)
        self.KT_ready = S("KT_ready", 2)
        self.QT_ps = S("QT_ps", 1)
        self.QT_ready = S("QT_ready", 1)
        self.s_ready = S("s_ready", H)
        self.max_done = S("max_done", H, 2)
        self.m_ready = S("m_ready", 4)
        self.QM_ps = S("QM_ps", 4)
        self.QM_ready = S("QM_ready", 4)
        self.t_ready = S("t_ready", H)
        self.exp_done = S("exp_done", H, 2)
        self.elo_done = [S(f"elo_done{i}", H // 2, 2) for i in range(2)]
        self.pv_done = S("pv_done", H, self.EB)
        self.O_ready = S("O_ready", 1)
        self.at_ready = S("at_ready", 1, 1)
        self.atT_ready = S("atT_ready", 1)
        self.aT_ready = S("aT_ready", 1)
        self.y_ready = S("y_ready", 1)
        self.x_done = S("x_done", 1, 2)
        self.shift_step = S("shift_steps", 2)
        self.tail_step = S("tail_steps", 2)
        self.steps = S("dve_steps", self.DVE_STEPS)
        self.X, self.Y = k.ps[:, 6, :], k.ps[:, 7, :]

    def alloc(self):
        k, sb, H = self.k, self.k.sb, self.HEADS
        self.mem = sb("x_mem", [self.MEM, P], F32)
        self.h2 = sb("x_h2", [P, 2, P], F32)
        self.stats = sb("x_stats", [P, 2, 6], F32)
        self.mv = sb("x_mv", [P, 2, 2], F32)
        self.ve = sb("x_ve", [P, 2], F32)
        self.rstd = sb("x_rstd", [P, 2], F32)
        self.XThi = sb("x_XThi", [P, self.KEYS], F16)
        self.XTlo = sb("x_XTlo", [P, self.KEYS], F16)
        self.QT = sb("x_QT", [P, 2, 4, k.S], F16)
        self.KT = sb("x_KT", [P, 2, 4, 3 * P], F16)
        self.QM = sb("x_QM", [P, 2, k.S], F16)
        self.mneg = sb("x_mneg", [P, 2, 4, 2], F32)
        self.mcl = sb("x_mcl", [P, 2, 4, 2], F32)
        self.E32 = sb("x_E32", [P, self.EB, 512], F32)
        self.Ehi = sb("x_Ehi", [P, self.EB, 512], F16)
        self.Elo = sb("x_Elo", [P, self.EB, 512], F16)
        self.r = sb("x_r", [P, 2, H], F32)
        self.at = sb("x_at", [P, 2, P], F32)
        self.aT = sb("x_aT", [P, k.S], F32)

    def s_bank(self, h):
        return self.k.ps[:, h % 2, :]

    def t_bank(self, h):
        return self.k.ps[:, 2 + h % 2, :]

    def o_bank(self, s):
        return self.k.ps[:, 4 + s, :]

    def credits(self, eng):
        for s in (self.max_done, self.exp_done, self.at_ready, self.x_done):
            eng.sem_inc(s.sem, s.credit)

    def clear(self, pool):
        H = self.HEADS
        pool.memset(self.QS[:, :, :, :, :], 0.0)
        pool.memset(self.VS[:, :, :, :, :], 0.0)
        return pool.memset(self.KS[:, :, :, :], 0.0)

    def ones(self, pool):
        pool.memset(self.KS[:, :, :, 24:26], 1.0)
        return pool.memset(self.VS[:, :, :, :, 8:9], 1.0)

    def dve_early(self, dve, st, b, j):
        k = self.k
        tile = lambda s: k.x_all[:, k.tile0 + b * 2 + s, :]
        if j == 11:
            st.start(b)
            for s in range(2):
                last = dve.bn_stats(self.stats[:, s, :], tile(s))
            st.done(last)
            st.carry(k.spare)
            for s in range(2):
                last = dve.bn_aggr(self.mv[:, s, :], self.stats[:, s, :])
            st.done(last)
            dve.tensor_scalar(self.ve[:, :], self.mv[:, :, 1], k.EPS, None, ALU.add)\
                .then_inc(self.ve_ready.sem, 1)
        if j == 13:
            dve.tensor_copy(self.mem[:, :], k.ctx_all[:, b, :])
            dve.wait_ge(self.rstd_ready.sem, self.rstd_ready.value(b, 1))
            for s in range(2):
                last = dve.tensor_scalar(self.h2[:, s, :], tile(s), self.mv[:, s, 0:1],
                                         self.rstd[:, s:s + 1], ALU.subtract, ALU.mult)
            last.then_inc(self.h2_ready.sem, 1)
            x = k.x_all[:, bass.ds(k.tile0 + b * 2, 2), :]
            dve.wait_ge(self.h2_ready.sem, self.h2_ready.value(b, 1))
            dve.tensor_tensor(x, x, bc(k.bout_sb[:, :], 1, 2), ALU.add).then_inc(self.bias_added.sem, 1)
        if j == 15:
            dve.wait_ge(self.XThi_ready.sem, self.XThi_ready.value(b, 1))
            dve.tensor_tensor(self.XTlo[:, :], self.X[:, 0:self.KEYS], self.XThi[:, :], ALU.subtract)\
                .then_inc(self.XTlo_ready.sem, 1)

    def dve_front(self, dve, b, par, j):
        k = self.k
        if j in (3, 4):
            dve.wait_ge(self.hi_ready.sem, self.hi_ready.value(b, j - 2))
            for c in (0, 1) if j == 3 else (2,):
                n = P if c < 2 else self.KEYS - 2 * P
                kv = (self.Y[:, c * 256:(c + 1) * 256] if c < 2 else self.X[:, 0:256])[0:n]
                kh = lambda lo: kv[:, lo:lo + P].rearrange("p (h d) -> p h d", h=self.HEADS)
                dve.scalar_tensor_tensor(self.KS[0:n, c, :, 16:24], kh(0), 1 / WS, self.KS[0:n, c, :, 0:8],
                                         ALU.mult, ALU.subtract)
                last = dve.scalar_tensor_tensor(self.VS[0:n, par, c, :, 9:17], kh(P), 1 / WS,
                                                self.VS[0:n, par, c, :, 0:8], ALU.mult, ALU.subtract)
            if j == 4:
                for s in range(2):
                    q = self.X[:, 256 + s * P:256 + (s + 1) * P].rearrange("p (h d) -> p h d", h=self.HEADS)
                    last = dve.scalar_tensor_tensor(self.QS[:, par, s, :, 8:16], q, self.D ** -0.5 / WS,
                                                    self.QS[:, par, s, :, 0:8], ALU.mult, ALU.subtract)
            last.then_inc(self.lo_ready.sem, 1)
        if j == 7:
            dve.wait_ge(self.QT_ps.sem, self.QT_ps.value(b, 1))
            dve.tensor_copy(self.QT[:, par, :, :].rearrange("p g q -> p (g q)"), self.X.bitcast(F16))\
                .then_inc(self.QT_ready.sem, 1)

    def pe_early(self, pe, b, j, first=False):
        k = self.k
        if j == 14:
            pe.wait_ge(self.h2_ready.sem, self.h2_ready.value(b, 1))
            if not first:
                pe.wait_ge(self.QT_ready.sem, self.QT_ready.value(b - 1, 1))
            for s in range(2):
                pe.transpose(self.X[:, self.MEM + s * P:self.MEM + (s + 1) * P], self.h2[:, s, :], k.identF[:, :])
            last = pe.transpose(self.X[:, 0:self.MEM], self.mem[:, :], k.identF[0:self.MEM, 0:self.MEM])
            last.then_inc(self.XT_ready.sem, 1)

    def pe_front(self, pe, b, par, j):
        k = self.k
        if j == 0:
            pe.wait_ge(self.XTlo_ready.sem, self.XTlo_ready.value(b, 1))
            pe.wait_ge(self.x_done.sem, self.x_done.value(b, -1))

            def project(out, cols, whi, wlo, first):
                n = cols.stop - cols.start
                for i, (a, w) in enumerate(((self.XThi, whi), (self.XTlo, whi), (self.XThi, wlo))):
                    last = pe.matmul(out[0:n], a[:, cols], w, start=(first and i == 0), stop=(i == 2),
                                     skip_group_check=True)
                return last

            for c in range(2):
                last = project(self.Y[:, c * 256:(c + 1) * 256], slice(c * P, (c + 1) * P),
                               k.Wkv_hi[:, :], k.Wkv_lo[:, :], c == 0)
            last.then_inc(self.kv01_ready.sem, 1)
            for s in range(2):
                project(self.X[:, 256 + s * P:256 + (s + 1) * P],
                        slice(self.MEM + s * P, self.MEM + (s + 1) * P), k.Wq_hi[:, :], k.Wq_lo[:, :], s == 0)
            project(self.X[:, 0:256], slice(2 * P, self.KEYS), k.Wkv_hi[:, :], k.Wkv_lo[:, :], False)\
                .then_inc(self.kvq_ready.sem, 1)
        if j == 5:
            pe.wait_ge(self.lo_ready.sem, self.lo_ready.value(b, 2))
            for half, bank in enumerate((self.Y, self.X)):
                for u in (2 * half, 2 * half + 1):
                    for c in range(3):
                        at = ((u % 2) * 3 + c) * P
                        last = pe.transpose(bank.bitcast(F16)[:, at:at + P],
                                            self.KS[:, c, 4 * u:4 * u + 4, :].rearrange("p h r -> p (h r)"),
                                            k.ident16[:, :])
                last.then_inc(self.KT_ps.sem, 1)
        if j == 7:
            pe.wait_ge(self.KT_ready.sem, self.KT_ready.value(b, 2))
            for u in range(4):
                for s in range(2):
                    last = pe.transpose(self.X.bitcast(F16)[:, (2 * u + s) * P:(2 * u + s + 1) * P],
                                        self.QS[:, par, s, 4 * u:4 * u + 4, :].rearrange("p h r -> p (h r)"),
                                        k.ident16[:, :])
            last.then_inc(self.QT_ps.sem, 1)

    def act_early(self, act, b, j):
        if j == 14:
            act.wait_ge(self.XT_ready.sem, self.XT_ready.value(b, 1))
            act.copy(self.XThi[:, :], self.X[:, 0:self.KEYS]).then_inc(self.XThi_ready.sem, 1)

    def act_front(self, act, b, par, j):
        k = self.k
        if j in (2, 3):
            ready = self.kv01_ready if j == 2 else self.kvq_ready
            act.wait_ge(ready.sem, ready.value(b, 1))
            for c in (0, 1) if j == 2 else (2,):
                n = P if c < 2 else self.KEYS - 2 * P
                kv = (self.Y[:, c * 256:(c + 1) * 256] if c < 2 else self.X[:, 0:256])[0:n]
                kh = lambda lo: kv[:, lo:lo + P].rearrange("p (h d) -> p h d", h=self.HEADS)
                act.activation(self.KS[0:n, c, :, 0:16].rearrange("p h (t d) -> p h t d", t=2), bc(kh(0), 2, 2),
                               ACT.Copy, scale=1 / WS)
                last = act.activation(self.VS[0:n, par, c, :, 0:8], kh(P), ACT.Copy, scale=1 / WS)
            if j == 3:
                for s in range(2):
                    q = self.X[:, 256 + s * P:256 + (s + 1) * P].rearrange("p (h d) -> p h d", h=self.HEADS)
                    act.activation(self.QS[:, par, s, :, 0:8], q, ACT.Copy, scale=self.D ** -0.5 / WS)
                    last = act.activation(self.QS[:, par, s, :, 16:24], q, ACT.Copy, scale=self.D ** -0.5 / WS)
            last.then_inc(self.hi_ready.sem, 1)
        if j in (5, 6):
            half = j - 5
            act.wait_ge(self.KT_ps.sem, self.KT_ps.value(b, half + 1))
            act.copy(self.KT[:, par, 2 * half:2 * half + 2, :].rearrange("p g q -> p (g q)"),
                     (self.Y, self.X)[half].bitcast(F16)[:, 0:6 * P]).then_inc(self.KT_ready.sem, 1)

    def scores_products(self, pe, b, par, h):
        u, r, S = h // 4, slice(32 * (h % 4), 32 * (h % 4) + self.ROWS), self.s_bank(h)
        if h == 0:
            pe.wait_ge(self.QT_ready.sem, self.QT_ready.value(b, 1))
        pe.wait_ge(self.max_done.sem, self.max_done.value(b, h - 1))
        return [(S[:, at:at + n], self.QT[r, par, u, q0:q0 + P], self.KT[r, par, u, 0:n], at == 0)
                for at, n, q0 in ((0, 192, 0), (192, 320, P))]

    def scores_mask(self, pe, h):
        for at in (64, 384):
            last = pe.matmul(self.s_bank(h)[:, at:at + P], self.k.identB[:, :], self.k.maskq_x[:, :], start=False,
                             stop=True, skip_group_check=True)
        last.then_inc(self.s_ready.sem, 1)

    def pe_multiply(self, pe, products):
        for out, weights, moving, start in products:
            pe.matmul(out, weights, moving, start=start, stop=False, skip_group_check=True)

    def pe_scores(self, pe, b, par, h):
        self.pe_multiply(pe, self.scores_products(pe, b, par, h))
        self.scores_mask(pe, h)

    def dve_max(self, dve, b, h):
        dve.wait_ge(self.s_ready.sem, self.s_ready.value(b, h + 1))
        S, m = self.s_bank(h), self.mneg[:, (h // 4) % 2, h % 4, :]
        dve.tensor_reduce(m[:, 0:1], S[:, 0:192], AX.X, ALU.max, negate=True)
        dve.tensor_reduce(m[:, 1:2], S[:, 192:512], AX.X, ALU.max, negate=True)\
            .then_inc(self.max_done.sem, 1)

    def dve_shift(self, dve, st, b, par, u):
        dve.wait_ge(self.max_done.sem, self.max_done.value(b, 4 * u + 4))
        w = u % 2
        st.start(b * 4 + u)
        st.done(dve.tensor_scalar(self.mcl[:, w], self.mneg[:, w], CLAMP, -CLAMP, ALU.min, ALU.max))
        rows = self.QS[:, par, :, 4 * u:4 * u + 4, :].rearrange("p s h r -> p h s r")
        st.done(dve.tensor_copy(rows[:, :, :, 24], self.mcl[:, w]))
        dve.tensor_tensor(rows[:, :, :, 25], self.mcl[:, w], rows[:, :, :, 24], ALU.subtract)\
            .then_inc(self.m_ready.sem, 1)

    def pe_shift(self, pe, b, par, u):
        k = self.k
        pe.wait_ge(self.m_ready.sem, self.m_ready.value(b, u + 1))
        for s in range(2):
            last = pe.transpose(self.s_bank(1).bitcast(F16)[:, s * P:(s + 1) * P],
                                self.QS[:, par, s, 4 * u:4 * u + 4, :].rearrange("p h r -> p (h r)"),
                                k.ident16[:, :])
        last.then_inc(self.QM_ps.sem, 1)

    def dve_shifted(self, dve, b, u):
        dve.wait_ge(self.QM_ps.sem, self.QM_ps.value(b, u + 1))
        dve.tensor_copy(self.QM[:, u % 2, :], self.s_bank(1).bitcast(F16)[:, 0:2 * P])\
            .then_inc(self.QM_ready.sem, 1)

    def keys_products(self, pe, b, par, h):
        u, r, T = h // 4, slice(32 * (h % 4), 32 * (h % 4) + 32), self.t_bank(h)
        if h % 4 == 0:
            pe.wait_ge(self.QM_ready.sem, self.QM_ready.value(b, u + 1))
        pe.wait_ge(self.exp_done.sem, self.exp_done.value(b, h - 1))
        return [(T[:, at:at + 256 - q0], self.KT[r, par, u, c * P:(c + 1) * P], self.QM[r, u % 2, q0:256], c == 0)
                for c, q0, at in ((0, 0, 0), (1, 64, 256), (2, 192, 448))]

    def keys_mask(self, pe, h):
        for at, n, m in ((0, 64, 0), (256, P, 64), (448, 64, 64)):
            last = pe.matmul(self.t_bank(h)[:, at:at + n], self.k.identB[:, :], self.k.maskk_x[:, m:m + n],
                             start=False, stop=True, skip_group_check=True)
        last.then_inc(self.t_ready.sem, 1)

    def pe_keys(self, pe, b, par, h):
        self.pe_multiply(pe, self.keys_products(pe, b, par, h))
        self.keys_mask(pe, h)

    def pe_both(self, pe, keys, scores):
        K, S = self.keys_products(pe, *keys), self.scores_products(pe, *scores)
        self.pe_multiply(pe, (K[0], S[0], K[1], S[1], K[2]))
        self.keys_mask(pe, keys[2])
        self.scores_mask(pe, scores[2])

    def act_exp(self, act, b, h):
        act.wait_ge(self.t_ready.sem, self.t_ready.value(b, h + 1))
        lo = self.elo_done[h % 2]
        act.wait_ge(lo.sem, lo.value(b, h // 2 - 1))
        act.activation(self.E32[:, h % self.EB, :], self.t_bank(h), ACT.Exp)
        act.wait_ge(self.pv_done.sem, self.pv_done.value(b, h - self.EB + 1))
        act.activation(self.Ehi[:, h % self.EB, :], self.t_bank(h), ACT.Exp).then_inc(self.exp_done.sem, 1)

    def split(self, eng, b, h):
        eng.wait_ge(self.exp_done.sem, self.exp_done.value(b, h + 1))
        w = h % self.EB
        eng.tensor_tensor(self.Elo[:, w, :], self.E32[:, w, :], self.Ehi[:, w, :], ALU.subtract)\
            .then_inc(self.elo_done[h % 2].sem, 1)

    def pe_values(self, pe, b, par, h):
        if h == 0:
            pe.wait_ge(self.O_ready.sem, self.O_ready.value(b, 1))
        lo = self.elo_done[h % 2]
        pe.wait_ge(lo.sem, lo.value(b, h // 2 + 1))
        w = h % self.EB
        blocks = ((0, 0, 0, 0), (0, 1, 256, 64), (1, 0, 128, 0), (1, 1, 320, 0), (1, 2, 448, 64))
        for s, c, at, p0 in blocks:
            n = P - p0
            for part, (E, cols) in enumerate(((self.Ehi, 18), (self.Elo, 9))):
                last = pe.matmul(self.o_bank(s)[p0:P, h * 18:h * 18 + cols], E[:, w, at:at + n],
                                 self.VS[:, par, c, h, 0:cols], start=(h == 0 and c == 0 and part == 0),
                                 stop=True, skip_group_check=True)
        last.then_inc(self.pv_done.sem, 1)

    def act_output(self, act, b1):
        act.wait_ge(self.pv_done.sem, self.pv_done.value(b1, 0))
        act.wait_ge(self.at_ready.sem, self.at_ready.value(b1, 0))
        act.copy(self.O[:, :, :], self.k.ps[:, 4:6, 0:self.HEADS * 18]).then_inc(self.O_ready.sem, 1)

    def tail(self, b1, dve=None, pe=None, act=None, j=0, st=None):
        k, H = self.k, self.HEADS
        O = self.O[:, :, :].rearrange("p s (h v) -> p (s h) v", h=H)
        Os = self.Os[:, :, :, :].rearrange("p s h v -> p (s h) v")
        if dve is not None and j == 0:
            dve.wait_ge(self.O_ready.sem, self.O_ready.value(b1, 1))
            st.done(dve.tensor_tensor(Os[:, :, 0:8], O[:, :, 0:8], O[:, :, 9:17], ALU.add))
            st.done(dve.reciprocal(self.r[:, :, :].rearrange("p s h -> p (s h)"), O[:, :, 8]))
            dve.tensor_tensor(self.at[:, :, :].rearrange("p s (h d) -> p (s h) d", h=H), Os[:, :, 0:8],
                              bc(self.r[:, :, :].rearrange("p s h -> p (s h)"), 2, self.D), ALU.mult)\
                .then_inc(self.at_ready.sem, 1)
        if pe is not None and j == 0:
            pe.wait_ge(self.at_ready.sem, self.at_ready.value(b1, 1))
            for s in range(2):
                last = pe.transpose(self.Y[:, s * P:(s + 1) * P], self.at[:, s, :], k.identF[:, :])
            last.then_inc(self.atT_ready.sem, 1)
        if act is not None and j == 0:
            act.wait_ge(self.atT_ready.sem, self.atT_ready.value(b1, 1))
            act.copy(self.aT[:, :], self.Y[:, 0:2 * P]).then_inc(self.aT_ready.sem, 1)
        if pe is not None and j == 1:
            pe.wait_ge(self.aT_ready.sem, self.aT_ready.value(b1, 1))
            for s in range(2):
                out = self.Y[:, s * P:(s + 1) * P]
                last = pe.matmul(out, self.aT[:, s * P:(s + 1) * P], k.Wout_sb[:, :], start=(s == 0), stop=True,
                                 skip_group_check=True)
            last.then_inc(self.y_ready.sem, 1)
        if dve is not None and j == 1:
            dve.wait_ge(self.y_ready.sem, self.y_ready.value(b1, 1))
            dve.wait_ge(self.bias_added.sem, self.bias_added.value(b1, 0))
            x = k.x_all[:, bass.ds(b1 * 2 + (k.tile0 - 2), 2), :]
            dve.tensor_tensor(x, x, self.Y[:, 0:2 * P].rearrange("p (s d) -> p s d", s=2), ALU.add)\
                .then_inc(self.x_done.sem, 1)

    AHEAD = 6

    def head(self, b, par, h):
        n = h // self.HEADS
        return b + n, par if n == 0 else 1 - par, h % self.HEADS

    def tensor(self, pe):
        one = self.k.one_row
        for s in range(2):
            for at in range(0, self.HEADS * 18, P):
                n = min(P, self.HEADS * 18 - at)
                last = pe.matmul(self.o_bank(s)[:, at:at + n], one[:, :], one[:, 0:n], start=(at == 0), stop=True,
                                 skip_group_check=True)
        last.then_inc(self.pv_done.sem, self.pv_done.credit - 2)
        self.pe_early(pe, 0, 14, first=True)
        for j in range(self.HEADS):
            self.pe_front(pe, 0, 0, j)
        pe.wait_ge(self.k.consts_ready, 5)
        for h in range(self.AHEAD):
            self.pe_scores(pe, 0, 0, h)
            if h == 3:
                self.pe_shift(pe, 0, 0, 0)
                self.pe_keys(pe, 0, 0, 0)
        self.pe_early(pe, 1, 14)
        with pe.Fori(0, self.k.B // 2) as i:
            for par in range(2):
                b = i * 2 + par
                for h in range(self.HEADS):
                    self.pe_both(pe, self.head(b, par, h + 1), self.head(b, par, h + self.AHEAD))
                    if h % 4 == 2:
                        nb, npar, nh = self.head(b, par, h + 2)
                        self.pe_shift(pe, nb, npar, nh // 4)
                    self.pe_front(pe, b + 1, 1 - par, h)
                    if h in (7, 9):
                        self.tail(b, pe=pe, j=(h - 7) // 2)
                    self.pe_values(pe, *self.head(b, par, h - 2))
                    self.pe_early(pe, b + 2, h)
        for h in range(2):
            self.pe_values(pe, *self.head(self.k.B, 0, h - 2))
        self.tail(self.k.B, pe=pe, j=0)
        self.tail(self.k.B, pe=pe, j=1)

    def vector(self, dve):
        st, shift_st = Steps(dve, self.steps), Steps(dve, self.shift_step)
        for j in (11, 13, 15):
            self.dve_early(dve, st, 0, j)
        for j in range(self.HEADS):
            self.dve_front(dve, 0, 0, j)
        self.dve_early(dve, st, 1, 11)
        for h in range(self.AHEAD):
            self.dve_max(dve, 0, h)
            if h == 3:
                self.dve_shift(dve, shift_st, 0, 0, 0)
                self.dve_shifted(dve, 0, 0)
        self.dve_early(dve, st, 1, 13)
        self.dve_early(dve, st, 1, 15)
        with dve.Fori(0, self.k.B // 2) as i:
            for par in range(2):
                b = i * 2 + par
                for h in range(self.HEADS):
                    if h % 2 == 1:
                        self.split(dve, b, h - 1)
                    if h % 4 == 2:
                        nb, _, nh = self.head(b, par, h + 2)
                        self.dve_shifted(dve, nb, nh // 4)
                    nb, _, nh = self.head(b, par, h + self.AHEAD)
                    self.dve_max(dve, nb, nh)
                    if h % 4 == 1:
                        nb, npar, nh = self.head(b, par, h + 3)
                        self.dve_shift(dve, shift_st, nb, npar, nh // 4)
                    self.dve_front(dve, b + 1, 1 - par, h)
                    if h in (5, 10):
                        self.tail(b, dve=dve, j=(h - 5) // 5, st=self.tail_steps(dve, b))
                    self.dve_early(dve, st, b + 2, h)
        self.tail(self.k.B, dve=dve, j=0, st=self.tail_steps(dve, self.k.B))
        self.tail(self.k.B, dve=dve, j=1)

    def tail_steps(self, dve, b1):
        st = Steps(dve, self.tail_step)
        st.start(b1)
        return st

    def scalar(self, act):
        self.act_early(act, 0, 14)
        for j in range(self.HEADS):
            self.act_front(act, 0, 0, j)
        self.act_early(act, 1, 14)
        with act.Fori(0, self.k.B // 2) as i:
            for par in range(2):
                b = i * 2 + par
                for h in range(self.HEADS):
                    self.act_exp(act, b, h)
                    if h == 2:
                        self.act_output(act, b)
                    if h == 8:
                        self.tail(b, act=act, j=0)
                    self.act_front(act, b + 1, 1 - par, h)
                    self.act_early(act, b + 2, h)
        self.act_output(act, self.k.B)
        self.tail(self.k.B, act=act, j=0)

    def gpsimd(self, pool):
        k = self.k

        def rstd(b):
            pool.wait_ge(self.ve_ready.sem, self.ve_ready.value(b, 1))
            pool.tensor_tensor(self.rstd[:, :], self.ve[:, :], k.minus_half[:, 0:2], ALU.pow)\
                .then_inc(self.rstd_ready.sem, 1)

        rstd(0)
        for w in (2, 3):
            pool.memset(self.Ehi[:, w, :], 1.0)
            pool.memset(self.Elo[:, w, :], 1.0).then_inc(self.elo_done[w % 2].sem, self.elo_done[w % 2].credit)
        rstd(1)
        with pool.Fori(0, k.B) as b:
            for h in range(1, self.HEADS, 2):
                self.split(pool, b, h)
                if h == 11:
                    rstd(b + 2)


class SelfAttention:

    H, D, CR = 8, 64, 32
    EB = 4
    OLD, WIN, SINK = range(3)
    KBLOCKS = ((0, 128, 0, 0, 0), (128, 64, 128, 64, 1), (192, 64, 192, 128, 2),
               (256, 192, 64, 0, 0), (448, 64, 192, 128, 2))
    VBLOCKS = ((0, 1, 0, 128, 0, 0), (1, 1, 128, 64, 0, 1), (1, 1, 192, 64, 64, 2),
               (0, 0, 256, 64, 64, 0), (1, 0, 320, 128, 0, 0), (1, 0, 448, 64, 64, 2))

    def __init__(self, k):
        self.k = k
        sb, sem = k.sb, k.sem
        H, D = self.H, self.D
        self.NB = k.S // self.CR
        NB = self.NB
        self.stats = sb("a_stats", [P, 2, 6], F32)
        self.mv = sb("a_mv", [P, 2, 2], F32)
        self.ve = sb("a_ve", [P, 2], F32)
        self.rstd = sb("a_rstd", [P, 2], F32)
        self.hn = sb("a_hn", [P, 2, P], F32)
        self.hThi = sb("a_hThi", [P, k.S], F16)
        self.hTlo = sb("a_hTlo", [P, k.S], F16)
        self.qraw = sb("a_qraw", [P, 2, H + 1, D], F32)
        self.sq = sb("a_sq", [P, 2, H + 1, D], F32)
        self.ms = sb("a_ms", [P, 2, H + 1], F32)
        self.rq = sb("a_rq", [P, 2, H + 1], F32)
        self.rope1 = sb("a_rope1", [P, 2, H + 1, 32], F32)
        self.rope2 = sb("a_rope2", [P, 2, H + 1, 32], F32)
        self.qn = sb("a_qn", [P, 2, H + 1, D], F32)
        self.QS = sb("a_QS", [P, 2, H, 2, D], F16)
        self.KS = sb("a_KS", [P, 2, 4, D], F16)
        self.QT = sb("a_QT", [P, 2, H, k.S], F16)
        self.KT = sb("a_KT", [P, 2, 2, k.S], F16)
        self.VS = sb("a_VS", [P, 2, 3, 2 * D + 1], F16)
        self.ks = sb("a_ks", [P, 2, NB], F32)
        self.kc = sb("a_kc", [P, NB], F32)
        self.kcg = sb("a_kcg", [P, 2, NB + 3], F16)
        self.vcT = sb("a_vcT", [P, 4, H, NB], F32)
        self.VW = sb("a_VW", [H * NB, 2, P], F32)
        self.EX = sb("a_EX", [P, 2 * H * (NB + 1) + 2 * H * 3], F32)
        self.cz = self.EX[:, 0:2 * H * (NB + 1)].rearrange("p (g n) -> p g n", n=NB + 1)
        self.gz = self.EX[:, 2 * H * (NB + 1):].rearrange("p (g n) -> p g n", n=3)
        self.czr = sb("a_czr", [P, 2 * H, NB], F32)
        self.cm = sb("a_cm", [P, 2 * H], F32)
        self.cl = sb("a_cl", [P, 2 * H], F32)
        self.gsum = sb("a_gsum", [P, 2 * H], F32)
        self.gcl = sb("a_gcl", [P, 2 * H], F32)
        self.gate = sb("a_gate", [P, 2, 3, 2 * H], F32)
        self.pcs = sb("a_pcs", [P, 2, 2 * H, NB], F32)
        self.pcT = sb("a_pcT", [H * NB, k.S], F32)
        self.mneg = sb("a_mneg", [P, 2, 4, 2, 2], F32)
        self.mcl = sb("a_mcl", [P, 2, 4, 2, 2], F32)
        self.mst = sb("a_mst", [P, 2, H, 2, 2], F16)
        self.mT = sb("a_mT", [4 * H, 2, k.S], F16)
        self.nm = sb("a_nm", [P, 2, 3, 2, H], F32)
        self.E32 = sb("a_E32", [P, self.EB, 512], F32)
        self.Ehi = sb("a_Ehi", [P, self.EB, 512], F16)
        self.Elo = sb("a_Elo", [P, self.EB, 512], F16)
        self.O = sb("a_O", [P, 2, 2, 2, H, D + 1], F32)
        self.n12 = sb("a_n12", [P, 2, 2 * H], F32)
        self.dx = sb("a_dx", [P, 4, 2 * H], F32)
        self.ea = sb("a_ea", [P, 4, 2 * H], F32)
        self.pl = sb("a_pl", [P, 3, 2 * H], F32)
        self.LL = sb("a_LL", [P, 2, 2 * H], F32)
        self.rr = sb("a_rr", [P, 2, 2 * H], F32)
        self.co = sb("a_co", [P, 3, 2 * H], F32)
        self.mixw = sb("a_mixw", [P, 2, H, D], F32)
        self.mixo = sb("a_mixo", [P, 2, H, D], F32)
        self.mixT = sb("a_mixT", [P, 2, 4, P], F32)
        S = lambda name, per, credit=0: Count(sem("a_" + name), per, credit)
        self.ve_ready = S("ve_ready", 1)
        self.rstd_ready = S("rstd_ready", 1)
        self.hn_ready = S("hn_ready", 1)
        self.hT_ps = S("hT_ps", 1)
        self.hThi_ready = S("hThi_ready", 1)
        self.hTlo_ready = S("hTlo_ready", 1)
        self.kv_ps = S("kv_ps", 1)
        self.kvhi_ready = S("kvhi_ready", 1)
        self.kvlo_ready = S("kvlo_ready", 1)
        self.msq_ready = S("msq_ready", 1)
        self.msk_ready = S("msk_ready", 1)
        self.rq_ready = S("rq_ready", 2)
        self.rope_ready = S("rope_ready", 1)
        self.qn_ready = S("qn_ready", 1)
        self.QShi_ready = S("QShi_ready", 2)
        self.QSlo_ready = S("QSlo_ready", 2)
        self.cg_ps = S("cg_ps", 1)
        self.vc_ps = S("vc_ps", 1)
        self.vcT_ready = S("vcT_ready", 1)
        self.VW_ps = S("VW_ps", 1)
        self.VW_ready = S("VW_ready", 1, 1)
        self.ex_ready = S("ex_ready", 1)
        self.exp_ready = S("exp_ready", 1)
        self.pcT_ps = S("pcT_ps", 1)
        self.pcT_ready = S("pcT_ready", 1, 1)
        self.dx_ready = S("dx_ready", 1)
        self.ea_ready = S("ea_ready", 1)
        self.co_ready = S("co_ready", 1)
        self.mixo_ready = S("mixo_ready", 1)
        self.mix_ready = S("mix_ready", 1)
        self.mix_ps = S("mix_ps", 1)
        self.y_ps = S("y_ps", 1)
        self.kcg_ready = S("kcg_ready", 1)
        self.K_ps = S("K_ps", 1)
        self.K_ready = S("K_ready", 1)
        self.qs_done = S("qs_done", 1)
        self.q_ps = S("q_ps", 2)
        self.q_read = S("q_read", 2)
        self.Q_ps = S("Q_ps", 2)
        self.Q_ready = [S(f"Q_ready{s}", 1) for s in range(2)]
        self.mixT_ready = [S(f"mixT_ready{s}", 1, 1) for s in range(2)]
        self.x_done = S("x_done", 1, 2)
        self.s_ready = S("s_ready", H)
        self.max_done = S("max_done", H, 2)
        self.m_ready = S("m_ready", 2)
        self.m_ps = S("m_ps", 2)
        self.mT_ready = S("mT_ready", 2)
        self.t_ready = S("t_ready", H)
        self.exp_done = S("exp_done", H, 2)
        self.elo_done = S("elo_done", H, self.EB)
        self.pv_done = S("pv_done", H, self.EB)
        self.o_done = S("o_done", H, 4)
        self.early_step = S("early_steps", 2)
        self.late_step = S("late_steps", 5)
        self.kc_step = S("kc_steps", 3)
        self.cg_step = S("cg_steps", 3)
        self.gate_step = S("gate_steps", 8)
        self.shift_step = S("shift_steps", 3)
        self.tail_step = S("tail_steps", 7)
        self.X, self.Y = k.ps[:, 6, :], k.ps[:, 7, :]

    def s_bank(self, h):
        return self.k.ps[:, h % 2, :]

    def t_bank(self, h):
        return self.k.ps[:, 2 + h % 2, :]

    def o_bank(self, h):
        return self.k.ps[:, 4 + h % 2, :]

    def credits(self, eng):
        for s in (self.max_done, self.exp_done, self.elo_done, self.x_done, self.pcT_ready, self.VW_ready, *self.mixT_ready):
            eng.sem_inc(s.sem, s.credit)
        for s in (self.pv_done, self.o_done):
            eng.sem_inc(s.sem, s.credit - 2)

    def clear(self, dve):
        for t in (self.gate, self.nm, self.pcs, self.mst):
            dve.memset(t[:, :], 0.0)
        dve.memset(self.VW[:, :, :], 0.0)
        dve.memset(self.VS[:, :, :, :], 1.0)
        return dve.memset(self.kcg[:, :, :], 0.0)

    def clear_probs(self, dve):
        dve.memset(self.Ehi[:, :, :], 1.0)
        dve.memset(self.Elo[:, :, :], 1.0).then_inc(self.k.cleared, 1)

    def dve_front(self, dve, st, n, par, j, early):
        k, H, D = self.k, self.H, self.D
        tile = lambda s: k.x_all[:, k.tile0 + n * 2 + s, :]
        if early and j == 4:
            st.start(n)
            for s in range(2):
                last = dve.bn_stats(self.stats[:, s, :], tile(s))
            st.done(last)
            st.carry(k.spare)
            for s in range(2):
                last = dve.bn_aggr(self.mv[:, s, :], self.stats[:, s, :])
            st.done(last)
            dve.tensor_scalar(self.ve[:, :], self.mv[:, :, 1], k.EPS, None, ALU.add)\
                .then_inc(self.ve_ready.sem, 1)
        if early and j == 5:
            dve.wait_ge(self.rstd_ready.sem, self.rstd_ready.value(n, 1))
            for s in range(2):
                last = dve.tensor_scalar(self.hn[:, s, :], tile(s), self.mv[:, s, 0:1],
                                         self.rstd[:, s:s + 1], ALU.subtract, ALU.mult)
            last.then_inc(self.hn_ready.sem, 1)
        if early and j == 7:
            dve.wait_ge(self.hThi_ready.sem, self.hThi_ready.value(n, 1))
            dve.tensor_tensor(self.hTlo[:, :], self.X[:, 0:k.S], self.hThi[:, :], ALU.subtract)\
                .then_inc(self.hTlo_ready.sem, 1)
        if early:
            return
        if j in (0, 1):
            ready, done, heads = ((self.q_read, self.msq_ready, slice(0, H)),
                                  (self.qs_done, self.msk_ready, slice(H, H + 1)))[j]
            if j == 0:
                st.start(n)
            ms = self.ms[:, :, heads]
            dve.wait_ge(ready.sem, ready.value(n, ready.per))
            st.done(dve.tensor_reduce(ms, self.sq[:, :, heads, :], AX.X, ALU.add))
            dve.tensor_scalar(ms, ms, 1 / D, WS * WS * 1e-6, ALU.mult, ALU.add).then_inc(done.sem, 1)
        if j == 2:
            dve.wait_ge(self.kvhi_ready.sem, self.kvhi_ready.value(n, 1))
            for o, at in enumerate((D, 4 * D, 3 * D)):
                last = dve.scalar_tensor_tensor(self.VS[:, par, o, D + 1:], self.X[:, at:at + D], 1 / WS,
                                                self.VS[:, par, o, 0:D], ALU.mult, ALU.subtract)
            last.then_inc(self.kvlo_ready.sem, 1)
        if j == 2.3:
            for s in range(2):
                cos = bc(k.rope_sb[:, s, 0:32], 1, H + 1)
                last = dve.tensor_tensor(self.rope1[:, s, :, :], self.qraw[:, s, :, 0:32], cos, ALU.mult)
            st.done(last)
            flat = lambda t: t[:, :, :, :].rearrange("p s h d -> p (s h d)")
            dve.wait_ge(self.rope_ready.sem, self.rope_ready.value(n, 1))
            st.done(dve.tensor_tensor(flat(self.rope1), flat(self.rope1), flat(self.rope2), ALU.add))
        if j == 2.5:
            dve.wait_ge(self.rq_ready.sem, self.rq_ready.value(n, 2))
            rq = self.rq[:, :, :].rearrange("p s h -> p (s h)")
            flat = lambda t: t.rearrange("p s h d -> p (s h) d")
            dve.tensor_tensor(flat(self.qn[:, :, :, 32:D]), flat(self.qraw[:, :, :, 32:D]),
                              bc(rq, 2, D - 32), ALU.mult)
            st.done(dve.tensor_tensor(flat(self.qn[:, :, :, 0:32]), flat(self.rope1[:, :, :, :]),
                                      bc(rq, 2, 32), ALU.mult))
            dve.tensor_tensor(self.qn[:, :, H, :], self.qn[:, :, H, :], bc(k.gqk_sb[:, :], 1, 2), ALU.mult)\
                .then_inc(self.qn_ready.sem, 1)
        if j == 3.5:
            for s in range(2):
                dve.wait_ge(self.QShi_ready.sem, self.QShi_ready.value(n, s + 1))
                if s == 1:
                    dve.tensor_tensor(self.KS[:, :, 2:4, :], bc(self.qn[:, :, H, :], 2, 2), self.KS[:, :, 0:2, :],
                                      ALU.subtract)
                dve.tensor_tensor(self.QS[:, s, :, 1, :], self.qn[:, s, 0:H, :], self.QS[:, s, :, 0, :],
                                  ALU.subtract).then_inc(self.QSlo_ready.sem, 1)
        if j == 5:
            dve.wait_ge(self.K_ready.sem, self.K_ready.value(n, 1))
            st_ = self.kc_steps
            st_.start(n)
            st_.done(dve.tensor_reduce(self.ks[:, :, :], self.KT[:, par, :, :].rearrange(
                "p a (n c) -> p a n c", c=self.CR), AX.X, ALU.add))
            st_.done(dve.tensor_tensor(self.kc[:, :], self.ks[:, 0, :], self.ks[:, 1, :], ALU.add))
            st_.done(dve.tensor_scalar(self.kcg[:, 0, 0:self.NB], self.kc[:, :], 1 / self.CR, None, ALU.mult))
            dve.scalar_tensor_tensor(self.kcg[:, 1, 0:self.NB], self.kc[:, :], 1 / self.CR,
                                     self.kcg[:, 0, 0:self.NB], ALU.mult, ALU.subtract)\
                .then_inc(self.kcg_ready.sem, 1)
        if j == 5.5:
            dve.wait_ge(self.vc_ps.sem, self.vc_ps.value(n, 1))
            dve.tensor_tensor(self.vcT[:, :, :, :].rearrange("p c h n -> p (c h) n"),
                              bc(self.X[:, 0:self.NB], 1, 4 * H),
                              k.headmask[:, :, :, :].rearrange("p c h n -> p (c h) n"), ALU.mult)\
                .then_inc(self.vcT_ready.sem, 1)
        if j == 6:
            dve.wait_ge(self.cg_ps.sem, self.cg_ps.value(n, 1))
            cg = self.Y[:, 0:2 * H * (self.NB + 3)].rearrange("p (g n) -> p g n", n=self.NB + 3)
            cs = self.cg_steps
            cs.start(n)
            for s in range(2):
                g = slice(s * H, (s + 1) * H)
                dve.tensor_tensor(self.czr[:, g, :], cg[:, g, 0:self.NB], bc(k.maskc[:, s, :], 1, H), ALU.add)
            cs.done(dve.scalar_tensor_tensor(self.gz, cg[:, :, self.NB:], -1.0, bc(k.bgate_sb[:, :], 1, 2 * H),
                                             ALU.mult, ALU.subtract))
            cs.done(dve.tensor_reduce(self.cm[:, :], self.czr[:, :, :], AX.X, ALU.max))
            cs.done(dve.tensor_tensor(self.cm[:, :], self.cm[:, :], k.sink2[:, :], ALU.max))
            dve.tensor_tensor(self.cz[:, :, 0:self.NB], self.czr[:, :, :], bc(self.cm[:, :], 2, self.NB),
                              ALU.subtract)
            dve.tensor_tensor(self.cz[:, :, self.NB], k.sink2[:, :], self.cm[:, :], ALU.subtract)\
                .then_inc(self.ex_ready.sem, 1)

    def dve_gates(self, dve, n, par):
        cs = self.gate_steps
        cs.start(n)
        g, NB = self.gate[:, par], self.NB
        dve.wait_ge(self.exp_ready.sem, self.exp_ready.value(n, 1))
        dve.tensor_reduce(self.cl[:, :], self.cz, AX.X, ALU.add)
        cs.done(dve.tensor_scalar(self.gz, self.gz, 1.0, None, ALU.add))
        cs.done(dve.reciprocal(self.gz, self.gz))
        cs.done(dve.tensor_reduce(self.gsum[:, :], self.gz, AX.X, ALU.add))
        cs.done(dve.tensor_scalar(self.gsum[:, :], self.gsum[:, :], 1e-6, None, ALU.max))
        dve.reciprocal(self.cl[:, :], self.cl[:, :])
        cs.done(dve.reciprocal(self.gsum[:, :], self.gsum[:, :]))
        cs.done(dve.tensor_tensor(g.rearrange("p n g -> p g n"), self.gz, bc(self.gsum[:, :], 2, 3), ALU.mult))
        cs.done(dve.tensor_tensor(self.gcl[:, :], g[:, 0, :], self.cl[:, :], ALU.mult))
        cs.done(dve.tensor_tensor(self.pcs[:, par, :, :], self.cz[:, :, 0:NB], bc(self.gcl[:, :], 2, NB),
                          ALU.mult))

    def pe_front(self, pe, n, par, j, early, first=False):
        k, H, D = self.k, self.H, self.D
        parts = lambda whi, wlo: ((self.hThi, whi), (self.hTlo, whi), (self.hThi, wlo))
        if early and j == 6:
            pe.wait_ge(self.hn_ready.sem, self.hn_ready.value(n, 1))
            if not first:
                pe.wait_ge(self.vcT_ready.sem, self.vcT_ready.value(n - 1, 1))
            pe.wait_ge(self.x_done.sem, self.x_done.value(n - 1, 0))
            for s in range(2):
                last = pe.transpose(self.X[:, s * P:(s + 1) * P], self.hn[:, s, :], k.identF[:, :])
            last.then_inc(self.hT_ps.sem, 1)
        if early and j == 7:
            pe.wait_ge(self.hTlo_ready.sem, self.hTlo_ready.value(n, 1))
            for s in range(2):
                if s == 1 and not first:
                    pe.wait_ge(self.ex_ready.sem, self.ex_ready.value(n - 1, 1))
                for i, (a, w) in enumerate(parts(k.WQ_hi[:, :], k.WQ_lo[:, :])):
                    last = pe.matmul((self.X, self.Y)[s], a[:, s * P:(s + 1) * P], w, start=(i == 0), stop=(i == 2))
                last.then_inc(self.q_ps.sem, 1)
        if early:
            return
        if j == 0:
            pe.wait_ge(self.q_read.sem, self.q_read.value(n, 2))
            for at, w0, t0 in ((0, 0, 0), (P, 0, P), (2 * P, D, D)):
                for i, (a, w) in enumerate(parts(k.aKV_hi[:, w0:], k.aKV_lo[:, w0:])):
                    last = pe.matmul(self.X[:, at:at + P - w0], a[:, t0:t0 + P], w, start=(at == 0 and i == 0),
                                     stop=(i == 2), skip_group_check=True)
            last.then_inc(self.kv_ps.sem, 1)
        if j == 4:
            pe.wait_ge(self.VW_ready.sem, self.VW_ready.value(n, 0))
            pe.wait_ge(self.QSlo_ready.sem, self.QSlo_ready.value(n, 2))
            for s in range(2):
                for h in range(H):
                    last = pe.transpose((self.X, self.Y)[s].bitcast(F16)[:, h * P:(h + 1) * P],
                                        self.QS[:, s, h, :, :].rearrange("p a d -> p (a d)"), k.ident16[:, :])
                last.then_inc(self.Q_ps.sem, 1)
            pe.wait_ge(self.Q_ready[0].sem, self.Q_ready[0].value(n, 1))
            for s in range(2):
                for a in range(2):
                    last = pe.transpose(self.X.bitcast(F16)[:, a * k.S + s * P:a * k.S + (s + 1) * P],
                                        self.KS[:, s, 2 * a:2 * a + 2, :].rearrange("p a d -> p (a d)"),
                                        k.ident16[:, :])
            last.then_inc(self.K_ps.sem, 1)
        if j == 5:
            pe.wait_ge(self.kcg_ready.sem, self.kcg_ready.value(n, 1))
            for half in range(2):
                for s, o in ((0, 0), (1, 2)):
                    for a in (slice(0, D), slice(D + 1, 2 * D + 1)):
                        last = pe.matmul(self.X[half * D:(half + 1) * D, 0:self.NB], self.VS[:, par, o, a],
                                         k.blockmean[:, s, :], start=(s == 0 and a.start == 0),
                                         stop=(s == 1 and a.start > 0), skip_group_check=True)
            last.then_inc(self.vc_ps.sem, 1)
            pe.wait_ge(self.Q_ready[1].sem, self.Q_ready[1].value(n, 1))
            w = self.NB + 3
            for s in range(2):
                for h in range(H):
                    at = (s * H + h) * w
                    q = slice(s * P, (s + 1) * P)
                    pe.matmul(self.Y[:, at:at + w], self.QT[:, par, h, q], self.kcg[:, 0, :],
                              start=(s == 0 and h == 0), stop=False, skip_group_check=True)
                    last = pe.matmul(self.Y[:, at:at + w], self.QT[0:D, par, h, q], self.kcg[0:D, 1, :],
                                     start=False, stop=True, skip_group_check=True)
            last.then_inc(self.cg_ps.sem, 1)

    def pe_project(self, pe, b):
        pe.wait_ge(self.pcT_ready.sem, self.pcT_ready.value(b, 1))
        for c in range(4):
            last = pe.matmul(self.Y[0:self.H * self.NB, 0:P], self.vcT[:, c, :, :].rearrange("p h n -> p (h n)"),
                             self.k.Weff[:, c, :], start=(c == 0), stop=(c == 3))
        last.then_inc(self.VW_ps.sem, 1)

    def act_project(self, act, b, par):
        act.wait_ge(self.VW_ps.sem, self.VW_ps.value(b, 1))
        act.copy(self.VW[:, par, :], self.Y[0:self.H * self.NB, 0:P]).then_inc(self.VW_ready.sem, 1)

    def act_front(self, act, n, par, j, early, first=False):
        k, H, D = self.k, self.H, self.D
        if early and j == 6:
            act.wait_ge(self.hT_ps.sem, self.hT_ps.value(n, 1))
            act.copy(self.hThi[:, :], self.X[:, 0:k.S]).then_inc(self.hThi_ready.sem, 1)
        if early and j == 7:
            for s in range(2):
                act.wait_ge(self.q_ps.sem, self.q_ps.value(n, s + 1))
                q = (self.X, self.Y)[s].rearrange("p (h d) -> p h d", h=H)
                act.copy(self.qraw[:, s, 0:H, :], q)
                act.activation(self.sq[:, s, 0:H, :], q, ACT.Square).then_inc(self.q_read.sem, 1)
        if early:
            return
        if j == 0:
            act.wait_ge(self.kv_ps.sem, self.kv_ps.value(n, 1))
            kx = self.X[:, 0:2 * P].rearrange("p (s d) -> p s d", s=2)[:, :, 0:D]
            act.copy(self.qraw[:, :, H, :], kx)
            act.activation(self.sq[:, :, H, :], kx, ACT.Square).then_inc(self.qs_done.sem, 1)
        if j == 2:
            if not first:
                act.wait_ge(self.pv_done.sem, self.pv_done.value(n - 1, 0))
            for o, at in enumerate((D, 4 * D, 3 * D)):
                last = act.activation(self.VS[:, par, o, 0:D], self.X[:, at:at + D], ACT.Copy, scale=1 / WS)
            last.then_inc(self.kvhi_ready.sem, 1)
        if j == 3:
            act.wait_ge(self.qn_ready.sem, self.qn_ready.value(n, 1))
            for s in range(2):
                if s == 1:
                    act.copy(self.KS[:, :, 0:2, :], bc(self.qn[:, :, H, :], 2, 2))
                act.copy(self.QS[:, s, :, 0, :], self.qn[:, s, 0:H, :]).then_inc(self.QShi_ready.sem, 1)
        if j == 4:
            act.wait_ge(self.Q_ps.sem, self.Q_ps.value(n, 1))
            act.copy(self.QT[:, par, :, 0:P], self.X.bitcast(F16).rearrange("p (h q) -> p h q", h=H))\
                .then_inc(self.Q_ready[0].sem, 1)
            act.wait_ge(self.Q_ps.sem, self.Q_ps.value(n, 2))
            act.copy(self.QT[:, par, :, P:2 * P], self.Y.bitcast(F16).rearrange("p (h q) -> p h q", h=H))\
                .then_inc(self.Q_ready[1].sem, 1)
            act.wait_ge(self.K_ps.sem, self.K_ps.value(n, 1))
            act.copy(self.KT[:, par, :, :].rearrange("p a q -> p (a q)"), self.X.bitcast(F16)[:, 0:2 * k.S])\
                .then_inc(self.K_ready.sem, 1)
        if j == 7:
            act.wait_ge(self.ex_ready.sem, self.ex_ready.value(n, 1))
            act.activation(self.EX[:, :], self.EX[:, :], ACT.Exp).then_inc(self.exp_ready.sem, 1)

    def pool_rstd(self, pool, n):
        pool.wait_ge(self.ve_ready.sem, self.ve_ready.value(n, 1))
        pool.tensor_tensor(self.rstd[:, :], self.ve[:, :], self.k.minus_half[:, 0:2], ALU.pow)\
            .then_inc(self.rstd_ready.sem, 1)

    def pool_rope(self, pool, n):
        k, H = self.k, self.H
        pool.wait_ge(self.qs_done.sem, self.qs_done.value(n, 1))
        x, r2 = self.qraw, self.rope2
        for s in range(2):
            sin = bc(k.rope_sb[:, s, 32:64], 1, H + 1)
            pool.tensor_tensor(r2[:, s, :, 0:16], x[:, s, :, 16:32], sin[:, :, 0:16], ALU.mult)
            last = pool.tensor_tensor(r2[:, s, :, 16:32], x[:, s, :, 0:16], sin[:, :, 16:32], ALU.mult)
        last.then_inc(self.rope_ready.sem, 1)

    def pool_norms(self, pool, n, ready, heads):
        pool.wait_ge(ready.sem, ready.value(n, 1))
        half = self.k.minus_half[:, 0:2 * (heads.stop - heads.start)].rearrange("p (s h) -> p s h", s=2)
        pool.tensor_tensor(self.rq[:, :, heads], self.ms[:, :, heads], half, ALU.pow).then_inc(self.rq_ready.sem, 1)

    def pool_query_norms(self, pool, n):
        self.pool_norms(pool, n, self.msq_ready, slice(0, self.H))

    def pool_key_norms(self, pool, n):
        self.pool_norms(pool, n, self.msk_ready, slice(self.H, self.H + 1))

    def pe_scores(self, pe, b, par, h):
        k, D = self.k, self.D
        if h == 0:
            pe.wait_ge(self.K_ready.sem, self.K_ready.value(b, 1))
            pe.wait_ge(self.Q_ready[1].sem, self.Q_ready[1].value(b, 1))
        pe.wait_ge(self.max_done.sem, self.max_done.value(b, h - 1))
        if h < 2:
            pe.wait_ge(self.mixT_ready[h].sem, self.mixT_ready[h].value(b, 0))
        S, Q, K = self.s_bank(h), self.QT[:, par, h, :], self.KT[:, par, 0, :]
        pe.matmul(S, k.identB[:, :], k.maskq_a[:, :], start=True, stop=False)
        mm = lambda out, q, keys, stop=False: pe.matmul(out, Q[:, q], K[:, keys], start=False, stop=stop)
        mm(S[:, 0:128], slice(0, 128), slice(0, 128))
        mm(S[0:64, 128:256], slice(128, 192), slice(64, 192))
        mm(S[64:128, 128:256], slice(192, 256), slice(128, 256))
        mm(S[:, 256:320], slice(0, 128), slice(0, 64))
        mm(S[:, 320:512], slice(128, 256), slice(0, 192), True).then_inc(self.s_ready.sem, 1)

    def dve_max(self, dve, b, h):
        dve.wait_ge(self.s_ready.sem, self.s_ready.value(b, h + 1))
        S, m = self.s_bank(h), self.mneg[:, h // 4, h % 4]
        dve.tensor_reduce(m[:, self.WIN, :], S[:, 0:256].rearrange("p (s c) -> p s c", s=2), AX.X, ALU.max,
                          negate=True)
        dve.tensor_reduce(m[:, self.OLD, 0:1], S[:, 256:320], AX.X, ALU.max, negate=True)
        dve.tensor_reduce(m[:, self.OLD, 1:2], S[:, 320:512], AX.X, ALU.max, negate=True)\
            .then_inc(self.max_done.sem, 1)

    def dve_shift(self, dve, b, par, u):
        dve.wait_ge(self.max_done.sem, self.max_done.value(b, 4 * u + 4))
        st, hs = self.shift_steps, slice(4 * u, 4 * u + 4)
        st.start(b * 2 + u)
        st.done(dve.tensor_scalar(self.mcl[:, u], self.mneg[:, u], CLAMP, -CLAMP, ALU.min, ALU.max))
        m = lambda a: self.mst[:, :, hs, :, a].rearrange("p s h w -> p h w s")
        st.done(dve.tensor_copy(m(0), self.mcl[:, u]))
        st.done(dve.tensor_tensor(m(1), self.mcl[:, u], m(0), ALU.subtract))
        for w in (self.OLD, self.WIN):
            last = dve.tensor_tensor(self.nm[:, par, w, :, hs], self.mst[:, :, hs, w, 0], self.mst[:, :, hs, w, 1],
                                     ALU.add)
        last.then_inc(self.m_ready.sem, 1)

    def pe_shift(self, pe, b, u):
        k = self.k
        pe.wait_ge(self.m_ready.sem, self.m_ready.value(b, u + 1))
        for s in range(2):
            last = pe.transpose(self.s_bank(1)[0:4 * self.H].bitcast(F16)[:, s * P:(s + 1) * P],
                                self.mst[:, s, :, :, :].rearrange("p h w a -> p (h w a)"), k.ident16[:, :])
        last.then_inc(self.m_ps.sem, 1)

    def dve_shifted(self, dve, b, u):
        dve.wait_ge(self.m_ps.sem, self.m_ps.value(b, u + 1))
        dve.tensor_copy(self.mT[:, u, :], self.s_bank(1)[0:4 * self.H].bitcast(F16)[:, 0:2 * P])\
            .then_inc(self.mT_ready.sem, 1)

    def pe_keys(self, pe, b, par, h):
        k, D = self.k, self.D
        if h % 4 == 0:
            pe.wait_ge(self.mT_ready.sem, self.mT_ready.value(b, h // 4 + 1))
        pe.wait_ge(self.exp_done.sem, self.exp_done.value(b, h - 1))
        T = self.t_bank(h)
        pe.matmul(T, k.identB[:, :], k.maskk_a[:, :], start=True, stop=False)
        mT = self.mT[:, h // 4, :]
        for at, n, q0, wo in ((0, 256, 0, self.WIN), (256, 192, 64, self.OLD), (448, 64, 192, self.OLD)):
            pe.matmul(T[:, at:at + n], k.select[:, 2 * h + wo, :], mT[:, q0:q0 + n], start=False, stop=False)
        for at, n, q0, k0, _ in self.KBLOCKS:
            pe.matmul(T[:, at:at + n], self.KT[:, par, 1, k0:k0 + P], self.QT[:, par, h, q0:q0 + n],
                      start=False, stop=False)
        for at, n, q0, k0, _ in self.KBLOCKS:
            last = pe.matmul(T[:, at:at + n], self.KT[:, par, 0, k0:k0 + P], self.QT[:, par, h, q0:q0 + n],
                             start=False, stop=(at == 448))
        last.then_inc(self.t_ready.sem, 1)

    def act_exp(self, act, b, h):
        act.wait_ge(self.t_ready.sem, self.t_ready.value(b, h + 1))
        act.wait_ge(self.elo_done.sem, self.elo_done.value(b, h - self.EB + 1))
        act.activation(self.E32[:, h % self.EB, :], self.t_bank(h), ACT.Exp)
        act.wait_ge(self.pv_done.sem, self.pv_done.value(b, h - self.EB + 1))
        act.activation(self.Ehi[:, h % self.EB, :], self.t_bank(h), ACT.Exp).then_inc(self.exp_done.sem, 1)

    def split(self, eng, b, h):
        eng.wait_ge(self.exp_done.sem, self.exp_done.value(b, h + 1))
        w = h % self.EB
        eng.tensor_tensor(self.Elo[:, w, :], self.E32[:, w, :], self.Ehi[:, w, :], ALU.subtract)\
            .then_inc(self.elo_done.sem, 1)

    def pe_values(self, pe, b, par, h):
        k, D = self.k, self.D
        if h == 0:
            pe.wait_ge(self.kvlo_ready.sem, self.kvlo_ready.value(b, 1))
        pe.wait_ge(self.o_done.sem, self.o_done.value(b, h - 1))
        pe.wait_ge(self.elo_done.sem, self.elo_done.value(b, h + 1))
        O = self.o_bank(h)[:, 0:4 * (D + 1)].rearrange("p (s w d) -> p s w d", s=2, w=2)
        pe.matmul(O[:, 0, self.OLD, :], k.zero16[:, :], self.VS[:, par, 0, 0:D + 1], start=True, stop=False,
                  skip_group_check=True)
        for s, wo, at, m, p0, o in self.VBLOCKS:
            for E, v in ((self.Ehi, slice(0, D + 1)), (self.Ehi, slice(D + 1, 2 * D + 1)), (self.Elo, slice(0, D + 1))):
                last = pe.matmul(O[p0:p0 + m, s, wo, 0:v.stop - v.start], E[:, h % self.EB, at:at + m],
                                 self.VS[:, par, o, v], start=False, stop=True, skip_group_check=True)
        last.then_inc(self.pv_done.sem, 1)

    def act_output(self, act, b, par, h):
        act.wait_ge(self.pv_done.sem, self.pv_done.value(b, h + 1))
        act.copy(self.O[:, par, :, :, h, :].rearrange("p s w d -> p (s w) d"),
                 self.o_bank(h)[:, 0:4 * (self.D + 1)].rearrange("p (g d) -> p g d", g=4))\
            .then_inc(self.o_done.sem, 1)

    def dve_tail(self, dve, b1, par, j):
        k, H, D = self.k, self.H, self.D
        st = self.tail_steps
        nm = self.nm[:, par].rearrange("p w s h -> p w (s h)")
        L = self.O[:, par, :, :, :, D]
        sh = lambda t: t.rearrange("p (s h) -> p s h", s=2)
        if j == 0:
            st.start(b1)
            dve.tensor_tensor(self.n12[:, 0, :], nm[:, self.OLD, :], nm[:, self.WIN, :], ALU.min)
            st.done(dve.tensor_tensor(self.n12[:, 1, :], nm[:, self.WIN, :], nm[:, self.SINK, :], ALU.min))
            for a in range(2):
                last = dve.tensor_tensor(self.dx[:, 2 * a:2 * a + 2, :], bc(self.n12[:, a, :], 1, 2),
                                         nm[:, a:a + 2, :], ALU.subtract)
            last.then_inc(self.dx_ready.sem, 1)
        if j == 2:
            dve.wait_ge(self.ea_ready.sem, self.ea_ready.value(b1, 1))
            dve.wait_ge(self.o_done.sem, self.o_done.value(b1, 0))
            for i, (e, w) in enumerate(((0, self.OLD), (1, self.WIN), (2, self.WIN))):
                last = dve.tensor_tensor(sh(self.pl[:, i, :]), sh(self.ea[:, e, :]), L[:, :, w, :], ALU.mult)
            st.done(last)
            dve.tensor_tensor(self.LL[:, 0, :], self.pl[:, 0, :], self.pl[:, 1, :], ALU.add)
            st.done(dve.tensor_tensor(self.LL[:, 1, :], self.pl[:, 2, :], self.ea[:, 3, :], ALU.add))
            st.done(dve.reciprocal(self.LL[:, :, :], self.LL[:, :, :]))
            st.done(dve.tensor_tensor(self.rr[:, :, :], self.LL[:, :, :], self.gate[:, par, 1:3, :], ALU.mult))
            dve.tensor_tensor(self.co[:, 0:2, :], self.ea[:, 0:2, :], bc(self.rr[:, 0, :], 1, 2), ALU.mult)
            st.done(dve.tensor_tensor(self.co[:, 2, :], self.ea[:, 2, :], self.rr[:, 1, :], ALU.mult))
            dve.tensor_tensor(self.co[:, 1, :], self.co[:, 1, :], self.co[:, 2, :], ALU.add)\
                .then_inc(self.co_ready.sem, 1)
        if j == 2.2:
            dve.wait_ge(self.co_ready.sem, self.co_ready.value(b1, 1))
            for s in range(2):
                last = dve.tensor_tensor(self.mixw[:, s, :, :], self.O[:, par, s, self.WIN, :, 0:D],
                                         bc(self.co[:, 1, s * H:(s + 1) * H], 2, D), ALU.mult)
            st.done(last)
        if j == 2.5:
            dve.wait_ge(self.mixo_ready.sem, self.mixo_ready.value(b1, 1))
            dve.tensor_tensor(self.mixw[:, :, :, :], self.mixw[:, :, :, :], self.mixo[:, :, :, :], ALU.add)\
                .then_inc(self.mix_ready.sem, 1)
        if j == 6:
            dve.wait_ge(self.y_ps.sem, self.y_ps.value(b1, 1))
            x = k.x_all[:, bass.ds(b1 * 2 + (k.tile0 - 2), 2), :]
            dve.tensor_tensor(x, x, self.X[:, 2 * P:].rearrange("p (s d) -> p s d", s=2), ALU.add)\
                .then_inc(self.x_done.sem, 1)

    def act_tail(self, act, b1, par, j):
        if j == 0:
            act.wait_ge(self.dx_ready.sem, self.dx_ready.value(b1, 1))
            act.activation(self.ea[:, :, :], self.dx[:, :, :], ACT.Exp).then_inc(self.ea_ready.sem, 1)
            act.wait_ge(self.pcT_ps.sem, self.pcT_ps.value(b1, 1))
            act.copy(self.pcT[:, :], self.Y[0:self.H * self.NB, 0:2 * P]).then_inc(self.pcT_ready.sem, 1)
        if j == 4:
            act.wait_ge(self.mix_ps.sem, self.mix_ps.value(b1, 1))
            for s in range(2):
                act.copy(self.mixT[:, s, :, :].rearrange("p c q -> p (c q)"), self.s_bank(s))\
                    .then_inc(self.mixT_ready[s].sem, 1)

    def pool_tail(self, pool, b1, par):
        pool.wait_ge(self.co_ready.sem, self.co_ready.value(b1, 1))
        for s in range(2):
            last = pool.tensor_tensor(self.mixo[:, s, :, :], self.O[:, par, s, self.OLD, :, 0:self.D],
                                      bc(self.co[:, 0, s * self.H:(s + 1) * self.H], 2, self.D), ALU.mult)
        last.then_inc(self.mixo_ready.sem, 1)

    def pe_tail(self, pe, b1, par, j):
        k, H = self.k, self.H
        if j == 0:
            for s in range(2):
                last = pe.transpose(self.Y[0:H * self.NB, s * P:(s + 1) * P],
                                    self.pcs[:, par, s * H:(s + 1) * H, :].rearrange("p h n -> p (h n)"),
                                    k.identF[:, :])
            last.then_inc(self.pcT_ps.sem, 1)
        if j == 4:
            pe.wait_ge(self.mix_ready.sem, self.mix_ready.value(b1, 1))
            for s in range(2):
                for c in range(4):
                    last = pe.transpose(self.s_bank(s)[:, c * P:(c + 1) * P],
                                        self.mixw[:, s, 2 * c:2 * c + 2, :].rearrange("p h d -> p (h d)"),
                                        k.identF[:, :])
            last.then_inc(self.mix_ps.sem, 1)
        if j == 5:
            pe.wait_ge(self.pcT_ready.sem, self.pcT_ready.value(b1, 1))
            for s in range(2):
                pe.wait_ge(self.mixT_ready[s].sem, self.mixT_ready[s].value(b1, 1))
                out = self.X[:, (2 + s) * P:(3 + s) * P]
                pe.matmul(out, self.pcT[:, s * P:(s + 1) * P], self.VW[:, par, :], start=(s == 0), stop=False,
                          skip_group_check=True)
                for c in range(4):
                    last = pe.matmul(out, self.mixT[:, s, c, :], k.Weff[:, c, :], start=False, stop=(c == 3),
                                     skip_group_check=True)
            last.then_inc(self.y_ps.sem, 1)

    def head(self, b, par, h):
        n = h // self.H
        return b + n, par if n == 0 else 1 - par, h % self.H

    def tensor(self, pe):
        for j, early in self.FRONT:
            self.pe_front(pe, 0, 0, j, early, first=True)
        pe.wait_ge(self.k.consts_ready, 3)
        for h in range(4):
            self.pe_scores(pe, 0, 0, h)
        pe.wait_ge(self.k.consts_ready, 4)
        pe.wait_ge(self.k.cleared, 2)
        self.pe_shift(pe, 0, 0)
        self.pe_keys(pe, 0, 0, 0)
        for j, early in self.FRONT[:4]:
            self.pe_front(pe, 1, 1, j, early)
        with pe.Fori(0, self.k.B // 2) as i:
            for par in range(2):
                b = i * 2 + par
                for h in range(self.H):
                    nb, npar, nu = (b, par, 1) if h < 4 else (b + 1, 1 - par, 0)
                    if h % 4 == 3:
                        self.pe_shift(pe, nb, nu)
                        self.pe_values(pe, *self.head(b, par, h - 2))
                        self.pe_keys(pe, *self.head(b, par, h + 1))
                    else:
                        for x in ((), (0, 1), (2, 3))[h % 4]:
                            self.pe_scores(pe, nb, npar, 4 * nu + x)
                        self.pe_keys(pe, *self.head(b, par, h + 1))
                        self.pe_values(pe, *self.head(b, par, h - 2))
                    if h == 5:
                        self.pe_tail(pe, b, 1 - par, h)
                    self.pe_front(pe, b + 1, 1 - par, h, False)
                    if h == 1:
                        self.pe_project(pe, b)
                    if h != 5:
                        self.pe_tail(pe, b, 1 - par, h)
                    self.pe_front(pe, b + 2, par, h, True)
        for h in range(2):
            self.pe_values(pe, *self.head(self.k.B, 0, h - 2))
        pe.wait_ge(self.q_read.sem, self.q_read.value(self.k.B + 1, 2))
        for j in range(6):
            self.pe_tail(pe, self.k.B, 1, j)

    FRONT = [(j, True) for j in (4, 5, 6, 7)] + [(j, False) for j in range(8)]

    def vector(self, dve):
        st, late = Steps(dve, self.early_step), Steps(dve, self.late_step)
        self.kc_steps, self.cg_steps = Steps(dve, self.kc_step), Steps(dve, self.cg_step)
        self.gate_steps = Steps(dve, self.gate_step)
        self.shift_steps, self.tail_steps = Steps(dve, self.shift_step), Steps(dve, self.tail_step)
        for j, early in self.FRONT:
            self.dve_front(dve, st if early else late, 0, 0, j, early)
            if j == 7 and early:
                self.clear_probs(dve)
            if j == 2:
                self.k.vector_later(dve)
            if j == 4 and not early:
                self.k.clear_later(dve)
            if j == 2:
                self.dve_front(dve, late, 0, 0, 2.3, False)
            if j in (2, 3, 5) and not early:
                self.dve_front(dve, late, 0, 0, j + 0.5, False)
        for h in range(4):
            self.dve_max(dve, 0, h)
        self.dve_front(dve, st, 1, 1, 4, True)
        self.dve_shift(dve, 0, 0, 0)
        self.dve_shifted(dve, 0, 0)
        for j, early in self.FRONT[1:4]:
            self.dve_front(dve, st, 1, 1, j, True)
        self.dve_gates(dve, 0, 0)
        dve.wait_ge(self.k.x_loaded[1], 16)
        dve.wait_ge(self.k.consts_ready, 3)
        dve.wait_ge(self.k.cleared, 3)
        with dve.Fori(0, self.k.B // 2) as i:
            for par in range(2):
                b = i * 2 + par
                for h in range(self.H):
                    u, j = h // 4, h % 4
                    nb, npar, nu = (b, par, 1) if u == 0 else (b + 1, 1 - par, 0)
                    if h == 5:
                        self.dve_front(dve, late, b + 1, 1 - par, 5, False)
                    if h == 6 and par == 0:
                        self.k.split_expert(dve, i)
                    if h == 6:
                        self.dve_front(dve, late, b + 1, 1 - par, 5.5, False)
                        self.dve_tail(dve, b, 1 - par, 6)
                    for x in ((), (0, 1), (2, 3), ())[j]:
                        self.dve_max(dve, nb, 4 * nu + x)
                    if j == 2:
                        self.dve_shift(dve, nb, npar, nu)
                    if j == 3:
                        self.dve_shifted(dve, nb, nu)
                    if h == 3:
                        self.dve_front(dve, late, b + 1, 1 - par, 2.3, False)
                        self.dve_front(dve, late, b + 1, 1 - par, 2.5, False)
                        self.dve_tail(dve, b, 1 - par, 2)
                    if h == 7:
                        self.dve_front(dve, st, b + 2, par, h, True)
                    if h != 5:
                        self.dve_front(dve, late, b + 1, 1 - par, h, False)
                    if h == 7:
                        self.dve_gates(dve, b + 1, 1 - par)
                    if h == 0:
                        self.dve_tail(dve, b, 1 - par, 0)
                    if h == 3:
                        self.dve_front(dve, late, b + 1, 1 - par, 3.5, False)
                        self.dve_tail(dve, b, 1 - par, 2.2)
                        self.dve_tail(dve, b, 1 - par, 2.5)
                    if h < 7:
                        self.dve_front(dve, st, b + 2, par, h, True)
        for j in (0, 2, 2.2, 2.5, 6):
            self.dve_tail(dve, self.k.B, 1, j)

    def scalar(self, act):
        for j, early in self.FRONT:
            self.act_front(act, 0, 0, j, early, first=True)
        for j, early in self.FRONT[:4]:
            self.act_front(act, 1, 1, j, early)
        act.wait_ge(self.k.consts_ready, 3)
        act.wait_ge(self.k.cleared, 2)
        with act.Fori(0, self.k.B // 2) as i:
            for par in range(2):
                b = i * 2 + par
                for h in range(self.H):
                    self.act_exp(act, b, h)
                    self.act_front(act, b + 1, 1 - par, h, False)
                    if h == 1:
                        self.act_project(act, b, par)
                    self.act_tail(act, b, 1 - par, h)
                    self.act_front(act, b + 2, par, h, True)
                    self.act_output(act, *self.head(b, par, h - 2))
        for h in range(2):
            self.act_output(act, *self.head(self.k.B, 0, h - 2))
        for j in range(5):
            self.act_tail(act, self.k.B, 1, j)

    def gpsimd(self, pool):
        pool.memset(self.O[:, :], 1.0)
        self.pool_rstd(pool, 0)
        self.k.self_pool_windows(pool)
        self.pool_query_norms(pool, 0)
        self.pool_rope(pool, 0)
        self.pool_key_norms(pool, 0)
        self.k.self_pool_select(pool)
        self.pool_rstd(pool, 1)
        pool.wait_ge(self.k.cleared, 2)
        with pool.Fori(0, self.k.B // 2) as i:
            for par in range(2):
                b = i * 2 + par
                for h in range(self.H):
                    self.split(pool, b, h)
                    if h == 0:
                        self.pool_query_norms(pool, b + 1)
                        self.pool_rope(pool, b + 1)
                        self.pool_key_norms(pool, b + 1)
                    if h == 2:
                        self.pool_tail(pool, b, 1 - par)
                    if h == 4:
                        self.pool_rstd(pool, b + 2)
        self.k.cross_masks(pool)
        self.k.experts_consts(pool)
        self.pool_tail(pool, self.k.B, 1)


class SelfWeights:

    def self_alloc(self):
        sb, sem = self.sb, self.sem
        H, D = SelfAttention.H, SelfAttention.D
        NB = self.S // SelfAttention.CR
        self.wqc_raw = sb("wqc_raw", [P, 32], F32)
        self.wqup_raw = sb("wqup_raw", [32, H * D], F32)
        self.wkv_raw = sb("wkv_raw", [P, 2, D], F32)
        self.wog_raw = sb("wog_raw", [P, 4, D], F32)
        self.wout_raw = sb("wout_raw", [D, 2, P], F32)
        self.wqcT = sb("wqcT", [32, P], F32)
        self.wogT = sb("wogT", [D, 4, P], F32)
        self.wgate_raw = sb("wgate_raw", [P, 3], F32)
        self.gq_col = sb("gq_col", [P, 1], F32)
        self.gq_row = sb("gq_row", [P, D], F32)
        self.gk_row = sb("gk_row", [P, D], F32)
        self.gqk_sb = sb("gqk_sb", [P, D], F32)
        self.wg_sb = sb("wg_sb", [P, 3], F32)
        self.bgate_sb = sb("bgate_sb", [P, 3], F32)
        self.sink2 = sb("sink2", [P, 2 * H], F32)
        self.rope_sb = sb("rope_sb", [P, self.S // P, 64], F32)
        self.WQ_hi = sb("WQ_hi", [P, H * D], F16)
        self.WQ_lo = sb("WQ_lo", [P, H * D], F16)
        self.aKV_hi = sb("aKV_hi", [P, 2 * D], F16)
        self.aKV_lo = sb("aKV_lo", [P, 2 * D], F16)
        self.Weff = sb("Weff", [P, 4, P], F32)
        self.maskq_a = sb("maskq_a", [P, 512], BF16)
        self.maskk_a = sb("maskk_a", [P, 512], BF16)
        self.maskc = sb("maskc", [P, 2, NB], F32)
        self.headmask = sb("headmask", [P, 4, H, NB], F32)
        self.blockmean = sb("blockmean", [P, 2, NB], F16)
        self.select = sb("select", [4 * H, 2 * H, P], F16)
        self.zero16 = sb("zero16", [P, P], F16)
        self.self_loaded = sem("self_loaded")
        self.self_small = sem("self_small_loaded")
        self.self_T_ps = sem("self_T_ps")
        self.self_T = sem("self_T")
        self.self_ps = sem("self_ps")
        self.self_ready = sem("self_ready")

    SELF_LOADS, SELF_SMALL = 6, 10

    def self_sync(self, sp):
        ap, D = self.ap, SelfAttention.D
        load = lambda dst, src, s: sp.dma_start(dst, src).then_inc(s, 16)
        load(self.wqc_raw[:, :], ap["L0_attn_w_qc"], self.self_loaded)
        load(self.wog_raw[:, :, :], ap["L0_attn_w_out_group"].rearrange("g (c p) i -> p (g c) i", p=P),
             self.self_loaded)
        load(self.wqup_raw[:, :], ap["L0_attn_w_qup"], self.self_loaded)
        load(self.wout_raw[:, :, :], ap["L0_attn_w_out"].rearrange("(g i) d -> i g d", i=D), self.self_loaded)
        load(self.wkv_raw[:, 0, :], ap["L0_attn_w_k"], self.self_loaded)
        load(self.wkv_raw[:, 1, :], ap["L0_attn_w_v"], self.self_loaded)

    def self_sync_small(self, sp):
        ap, D = self.ap, SelfAttention.D
        load = lambda dst, src: sp.dma_start(dst, src).then_inc(self.self_small, 16)
        row = lambda name: ap[name].rearrange("(a d) -> a d", a=1)
        for half in range(2):
            rows = slice(half * D, (half + 1) * D)
            load(self.wgate_raw[rows, :], ap["L0_attn_w_gate"])
            load(self.gq_col[rows, :], ap["L0_attn_g_qnorm"].rearrange("(d a) -> d a", a=1))
            h = SelfAttention.H
            load(self.sink2[:, half * h:(half + 1) * h], row("L0_attn_sink_logit").broadcast_to([P, h]))
        load(self.gq_row[:, :], row("L0_attn_g_qnorm").broadcast_to([P, D]))
        load(self.gk_row[:, :], row("L0_attn_g_knorm").broadcast_to([P, D]))
        load(self.bgate_sb[:, :], row("L0_attn_b_gate").broadcast_to([P, 3]))
        load(self.rope_sb[:, :, :], ap["rope"].rearrange("(s p) d -> p s d", p=P))

    def keep(self, pool, t, base, mult, pattern, fill=NEG):
        return pool.affine_select(out=t, in_=t, compare_op=ALU.is_ge, fill=fill, base=base, pattern=pattern,
                                  channel_multiplier=mult)

    def self_pool_blocks(self, pool):
        H, CR = SelfAttention.H, SelfAttention.CR
        NB = self.S // CR
        step, keep, hm = self.pool_st.done, self.keep, self.headmask
        pool.memset(self.maskc[:, :, :], 0.0)
        pool.memset(hm[:, :, :, :], 1.0)
        pool.memset(self.zero16[:, :], 0.0)
        step(pool.memset(self.blockmean[:, :, :], 1.0 / CR))
        keep(pool, self.maskc[:, :, :], 1 - CR, 1, [[P, 2], [-CR, NB]])
        step(keep(pool, self.blockmean[:, :, :], 0, 1, [[P, 2], [-CR, NB]], 0.0))
        step(keep(pool, self.blockmean[:, :, :], CR - 1, -1, [[-P, 2], [CR, NB]], 0.0))
        for half in range(2):
            for sign in (-1, 1):
                step(keep(pool, hm[half * 64:(half + 1) * 64, :, :, :].rearrange("p c h n -> p (c h n)"), sign * half,
                          0, [[2 * sign, 4], [-sign, H], [0, NB]], 0.0))
        pool.sem_inc(self.consts_ready, 1)

    def self_pool_windows(self, pool):
        step, q, k = self.pool_st.done, self.maskq_a, self.maskk_a
        keep = lambda *a: self.keep(pool, *a)
        pool.memset(q[:, :], 0.0)
        step(pool.memset(k[:, :], 0.0))
        keep(q[:, 0:128], 0, 1, [[-1, 128]])
        keep(q[:, 256:320], -64, 1, [[-1, 64]])
        keep(q[:, 320:512], 64, 1, [[-1, 192]])
        keep(k[:, 0:128], 0, -1, [[1, 128]])
        keep(k[:, 128:256], 64, -1, [[0, 2], [1, 64]])
        keep(k[:, 256:448], 0, -1, [[1, 192]])
        step(keep(k[:, 448:512], 0, -1, [[1, 64]]))
        keep(q[:, 0:128], 63, -1, [[1, 128]])
        keep(k[:, 0:128], 63, 1, [[-1, 128]])
        step(keep(k[:, 128:256], -1, 1, [[0, 2], [-1, 64]]))
        for half in range(2):
            rows = slice(half * 64, (half + 1) * 64)
            step(keep(q[rows, 128:256], 64, 1, [[-1, 128]]))
            step(keep(q[rows, 128:256], -1, -1, [[1, 128]]))
        pool.sem_inc(self.consts_ready, 1)

    def self_pool_select(self, pool):
        t, H, step = self.select[:, :, :], SelfAttention.H, self.pool_st.done
        step(pool.memset(t, 1.0))
        step(self.keep(pool, t, 0, 1, [[-2, 2 * H], [0, P]], 0.0))
        self.keep(pool, t, 1, -1, [[2, 2 * H], [0, P]], 0.0).then_inc(self.consts_ready, 1)

    def self_tensor(self, pe):
        ps, D = self.ps, SelfAttention.D
        pe.wait_ge(self.self_loaded, 16 * self.SELF_LOADS)
        pe.transpose(ps[0:32, 2, 0:P], self.wqc_raw[:, :], self.identF[:, :])
        for c in range(4):
            last = pe.transpose(ps[0:D, 1, c * P:(c + 1) * P], self.wog_raw[:, c, :], self.identF[:, :])
        last.then_inc(self.self_T_ps, 1)
        pe.wait_ge(self.self_T, 2)
        pe.matmul(ps[:, 0, :], self.wqcT[:, :], self.wqup_raw[:, :], start=True, stop=True)
        for c in range(4):
            last = pe.matmul(ps[:, 3, c * P:(c + 1) * P], self.wogT[:, c, :], self.wout_raw[:, c // 2, :],
                             start=(c == 0), stop=(c == 3), skip_group_check=True)
        last.then_inc(self.self_ps, 1)

    def self_scalar(self, act):
        act.wait_ge(self.self_T_ps, 1)
        act.copy(self.wogT[:, :, :].rearrange("p c d -> p (c d)"), self.ps[0:64, 1, :]).then_inc(self.self_T, 1)

    def self_vector(self, dve):
        ps, st = self.ps, self.self_dst
        H, NB = SelfAttention.H, self.S // SelfAttention.CR
        dve.wait_ge(self.self_loaded, 16 * self.SELF_LOADS)
        raw = self.wkv_raw[:, :, :].rearrange("p a d -> p (a d)")
        st.done(dve.tensor_scalar(self.aKV_hi[:, :], raw, WS, None, ALU.mult))
        dve.scalar_tensor_tensor(self.aKV_lo[:, :], raw, WS, self.aKV_hi[:, :], ALU.mult, ALU.subtract)
        dve.wait_ge(self.self_T_ps, 1)
        dve.tensor_copy(self.wqcT[:, :], ps[0:32, 2, 0:P]).then_inc(self.self_T, 1)
        dve.wait_ge(self.self_small, 16 * self.SELF_SMALL)
        dve.scalar_tensor_tensor(self.gqk_sb[:, :], self.gq_row[:, :], 0.125, self.gk_row[:, :], ALU.mult, ALU.mult)
        for par in range(2):
            dve.tensor_scalar(self.selfatt.nm[:, par, SelfAttention.SINK, :, :].rearrange("p s h -> p (s h)"),
                              self.sink2[:, :], -1.0, None, ALU.mult)
        st.done(dve.tensor_scalar(self.wg_sb[:, :], self.wgate_raw[:, :], self.gq_col[:, 0:1], None, ALU.mult))
        kcg = self.selfatt.kcg
        st.done(dve.tensor_copy(kcg[:, 0, NB:], self.wg_sb[:, :]))
        dve.tensor_tensor(kcg[:, 1, NB:], self.wg_sb[:, :], kcg[:, 0, NB:], ALU.subtract)
        dve.wait_ge(self.self_ps, 1)
        st.done(dve.tensor_scalar(self.WQ_hi[:, :], ps[:, 0, :], WS, None, ALU.mult))
        dve.tensor_copy(self.Weff[:, :, :].rearrange("p c d -> p (c d)"), ps[:, 3, :])
        dve.scalar_tensor_tensor(self.WQ_lo[:, :], ps[:, 0, :], WS, self.WQ_hi[:, :], ALU.mult, ALU.subtract)\
            .then_inc(self.self_ready, 1)


class Layer(SelfWeights):

    EPS = 1e-5

    def __init__(self, nc, ctx, ap):
        self.nc, self.ctx, self.ap = nc, ctx, ap
        self.scope = ctx
        self.B, self.S, _ = ap["x"].shape
        self.tiles = self.B * self.S // P
        self.tile0 = Experts.T
        self.after = 4
        self.W1, self.W2 = ap["L0_ffn_W1"], ap["L0_ffn_W2"]
        self.E = self.W1.shape[0]
        C = self.W1.shape[2] // P
        self.C = C
        self.ps = ctx.enter_context(nc.psum_tensor("ps", [P, 8, 512], F32))
        sb = self.sb
        self.x_all = sb("x_all", [P, self.tile0 + self.tiles + self.after, P], F32)
        self.x_v = ap["x"].rearrange("b (s p) d -> p (b s) d", p=P)
        self.out_v = ap["out"].rearrange("b (s p) d -> p (b s) d", p=P)
        self.ffn_raw = sb("ffn_raw", [P, 2, C * P], F32)
        self.W1hi = sb("W1hi", [P, self.E, C * P], F16)
        self.W1lo = sb("W1lo", [P, self.E, C * P], F16)
        self.W2hi = sb("W2hi", [P, self.E, C, P], F16)
        self.W2lo = sb("W2lo", [P, self.E, C, P], F16)
        self.b1_raw = sb("b1_raw", [self.E * C, P], F32)
        self.b1_sb = sb("b1_sb", [P, self.E * C], F32)
        self.Wg_sb = sb("Wg_sb", [P, self.E], F32)
        self.bg_sb = sb("bg_sb", [P, self.E], F32)
        self.b2_raw = sb("b2_raw", [32, P], F32)
        self.b2_rest = sb("b2_rest", [32, P], F32)
        self.b2parts = sb("b2parts", [32, 3, P], BF16)
        self.identF = sb("identF", [P, P], F32)
        self.identB = sb("identB", [P, P], BF16)
        self.ident16 = sb("ident16", [P, P], F16)
        self.pick = sb("pick", [32, self.E, P], BF16)
        self.gp = sb("f_gp", [P, self.C * P // P, 32], BF16)
        self.iota8 = sb("iota8", [P, 8], F32)
        self.minus_half = sb("minus_half", [P, 64], F32)
        self.spare = sb("spare", [P, 2], F32)
        self.euler = sb("euler", [P, 64], F32)
        sem = self.sem
        self.pool_step = Count(sem("pool_setup_steps"), 0)
        self.dve_step = Count(sem("dve_setup_steps"), 0)
        self.consts_ready = sem("consts_ready")
        self.cleared = sem("cleared")
        self.x_loaded = [sem(f"x_loaded{i}") for i in range(2)]
        self.ffn_loaded = sem("ffn_loaded")
        self.small_loaded = sem("small_loaded")
        self.b1_loaded = sem("b1_loaded")
        self.ffn_split = Count(sem("ffn_split"), 1, 1)
        self.split_step = Count(sem("ffn_split_steps"), 1)
        self.b2_split = sem("b2_split")
        self.b2_zero = sem("b2_zero")
        self.b1T_ready = sem("b1T_ready")
        self.b1_ready = sem("b1_ready")
        B, H = self.B, P
        self.ctx_all = sb("ctx_all", [ap["ctx_1024"].shape[1], B + 2, P], F32)
        self.xw_raw = sb("xw_raw", [P, 3, P], F32)
        self.xw_hi = sb("xw_hi", [P, 3, P], F16)
        self.xw_lo = sb("xw_lo", [P, 3, P], F16)
        self.Wq_hi, self.Wq_lo = self.xw_hi[:, 0, :], self.xw_lo[:, 0, :]
        self.Wkv_hi, self.Wkv_lo = (w[:, 1:3, :].rearrange("p a d -> p (a d)") for w in (self.xw_hi, self.xw_lo))
        self.Wout_sb = sb("Wout_sb", [P, P], F32)
        self.bout_sb = sb("bout_sb", [P, P], F32)
        self.one_row = sb("one_row", [1, P], F32)
        self.maskq_x = sb("maskq_x", [P, P], BF16)
        self.maskk_x = sb("maskk_x", [P, 64 + P], BF16)
        self.x_weights_loaded = sem("x_weights_loaded")
        self.ctx_loaded = sem("ctx_loaded")
        self.x_split = sem("x_split")
        self.x_used = sem("x_phase_done")
        self.cross = Cross(self)
        with ExitStack() as self.scope:
            self.self_alloc()
            self.selfatt = SelfAttention(self)
        with ExitStack() as self.scope:
            self.cross.alloc()
        self.scope = ctx
        self.experts = Experts(self)

    def sb(self, name, shape, dt):
        return self.scope.enter_context(self.nc.sbuf_tensor(name, shape, dt))

    def sem(self, name):
        return self.ctx.enter_context(self.nc.semaphore(name))

    SMALL = 5

    def sync_setup(self, sp):
        ap, first = self.ap, 4
        t0 = self.tile0
        self.self_sync(sp)
        sp.dma_start(self.x_all[:, t0:t0 + first, :], self.x_v[:, 0:first, :]).then_inc(self.x_loaded[0], 16)
        self.self_sync_small(sp)
        sp.dma_start(self.b1_raw[:, :], ap["L0_ffn_b1"].rearrange("e (c p) -> (e c) p", p=P))\
            .then_inc(self.b1_loaded, 16)
        sp.dma_start(self.x_all[:, t0 + first:t0 + self.tiles, :], self.x_v[:, first:self.tiles, :])\
            .then_inc(self.x_loaded[1], 16)
        sp.dma_start(self.Wg_sb[:, :], ap["L0_ffn_Wg"]).then_inc(self.small_loaded, 16)
        sp.dma_start(self.bg_sb[:, :], ap["L0_ffn_bg"].rearrange("(a e) -> a e", a=1).broadcast_to([P, self.E]))\
            .then_inc(self.small_loaded, 16)
        sp.dma_start(self.xw_raw[:, 0, :], ap["L0_xattn_Wq"]).then_inc(self.x_weights_loaded, 16)
        sp.dma_start(self.xw_raw[:, 1:3, :].rearrange("p a d -> p (a d)"), ap["L0_xattn_Wkv"])\
            .then_inc(self.x_weights_loaded, 16)
        sp.dma_start(self.Wout_sb[:, :], ap["L0_xattn_Wout"]).then_inc(self.x_weights_loaded, 16)
        sp.dma_start(self.bout_sb[:, :], ap["L0_xattn_bout"].rearrange("(a d) -> a d", a=1).broadcast_to([P, P]))\
            .then_inc(self.x_weights_loaded, 16)
        sp.dma_start(self.ctx_all[:, 0:self.B, :], ap["ctx_1024"].rearrange("b m d -> m b d"))\
            .then_inc(self.ctx_loaded, 16)
        sp.wait_ge(self.b2_zero, 1)
        for m in range(3):
            sp.dma_start(self.b2_raw[m * self.E:(m + 1) * self.E, :], ap["L0_ffn_b2"])\
                .then_inc(self.small_loaded, 16)
        self.sync_experts(sp)

    def sync_experts(self, sp):
        with sp.Fori(0, self.E) as e:
            sp.wait_ge(self.ffn_split.sem, self.ffn_split.value(e, 0))
            sp.dma_start(self.ffn_raw[:, 0, :], self.W1[e]).then_inc(self.ffn_loaded, 16)
            sp.dma_start(self.ffn_raw[:, 1, :].rearrange("p (c d) -> p c d", d=P),
                         self.W2[e].rearrange("(c p) d -> p c d", p=P)).then_inc(self.ffn_loaded, 16)

    def split_expert(self, dve, e):
        dve.wait_ge(self.ffn_loaded, e * 32 + 32)
        st = Steps(dve, self.split_step)
        st.start(e)
        W2hi, W2lo = (w[:, e, :, :].rearrange("p c d -> p (c d)") for w in (self.W2hi, self.W2lo))
        dve.tensor_scalar(self.W1hi[:, e, :], self.ffn_raw[:, 0, :], WS, None, ALU.mult)
        st.done(dve.tensor_scalar(W2hi, self.ffn_raw[:, 1, :], WS, None, ALU.mult))
        dve.scalar_tensor_tensor(self.W1lo[:, e, :], self.ffn_raw[:, 0, :], WS, self.W1hi[:, e, :],
                                 ALU.mult, ALU.subtract)
        dve.scalar_tensor_tensor(W2lo, self.ffn_raw[:, 1, :], WS, W2hi, ALU.mult, ALU.subtract)\
            .then_inc(self.ffn_split.sem, 1)

    def gpsimd_setup(self, pool):
        st = self.pool_st = Steps(pool, self.pool_step)
        pool.memset(self.b2_raw[:, :], 0.0).then_inc(self.b2_zero, 1)
        st.done(pool.memset(self.identF[:, :], 0.0))
        st.done(pool.affine_select(out=self.identF[:, :], in_=self.identF[:, :], compare_op=ALU.not_equal, fill=1.0,
                                   base=0, pattern=[[-1, P]], channel_multiplier=1))
        pool.tensor_copy(self.ident16[:, :], self.identF[:, :])
        pool.tensor_copy(self.identB[:, :], self.identF[:, :]).then_inc(self.consts_ready, 1)
        pool.memset(self.minus_half[:, :], -0.5)
        pool.memset(self.spare[:, :], 0.0)
        pool.memset(self.one_row[:, :], 1.0)
        self.self_pool_blocks(pool)
        self.selfatt.credits(pool)
        pool.sem_inc(self.ffn_split.sem, self.ffn_split.credit)
        self.cross.credits(pool)
        self.experts.credits(pool)
        pool.wait_ge(self.cleared, 1)

    def cross_masks(self, pool):
        st = self.pool_st
        pool.memset(self.maskq_x[:, :], 0.0)
        st.done(pool.memset(self.maskk_x[:, :], 0.0))
        pool.affine_select(out=self.maskq_x[:, :], in_=self.maskq_x[:, :], compare_op=ALU.is_ge, fill=NEG,
                           base=0, pattern=[[-1, P]], channel_multiplier=1)
        pool.affine_select(out=self.maskk_x[:, 0:64], in_=self.maskk_x[:, 0:64], compare_op=ALU.is_ge, fill=NEG,
                           base=64, pattern=[[1, 64]], channel_multiplier=-1)
        pool.affine_select(out=self.maskk_x[:, 64:], in_=self.maskk_x[:, 64:], compare_op=ALU.is_ge, fill=NEG,
                           base=0, pattern=[[1, P]], channel_multiplier=-1).then_inc(self.consts_ready, 1)

    def experts_consts(self, pool):
        st = self.pool_st
        pool.memset(self.euler[:, :], 2.718281828459045)
        pool.iota(self.iota8[:, :], pattern=[[1, 8]], base=0, channel_multiplier=0,
                  allow_small_or_imprecise_dtypes=True)
        st.done(pool.memset(self.pick[:, :, :], 0.0))
        for m in range(3):
            st.done(pool.affine_select(out=self.pick[:, :, :], in_=self.pick[:, :, :], compare_op=ALU.not_equal,
                                       fill=1.0 / WS, base=-m * self.E, pattern=[[-1, self.E], [0, P]],
                                       channel_multiplier=1))
        pool.sem_inc(self.consts_ready, 1)

    def vector_setup(self, dve):
        st = self.self_dst = Steps(dve, self.dve_step)
        self.selfatt.clear(dve)
        dve.memset(self.gp[:, :, :], 0.0).then_inc(self.cleared, 1)
        self.self_vector(dve)
        dve.wait_ge(self.b1T_ready, 1)
        dve.tensor_copy(self.b1_sb[:, :], self.ps[:, 7, 0:self.E * self.C]).then_inc(self.b1_ready, 1)
        dve.wait_ge(self.x_loaded[0], 16)
        dve.wait_ge(self.consts_ready, 2)

    def clear_later(self, dve):
        st = self.self_dst
        self.cross.clear(dve)
        dve.memset(self.x_all[:, 0:self.tile0, :], 0.0)
        st.done(dve.memset(self.x_all[:, self.tile0 + self.tiles:, :], 0.0))
        self.cross.ones(dve)
        dve.memset(self.ctx_all[:, self.B:, :], 0.0).then_inc(self.cleared, 1)

    def vector_later(self, dve):
        st = self.self_dst
        dve.wait_ge(self.x_weights_loaded, 16 * 4)
        st.done(dve.tensor_scalar(self.xw_hi[:, :, :], self.xw_raw[:, :, :], WS, None, ALU.mult))
        dve.scalar_tensor_tensor(self.xw_lo[:, :, :], self.xw_raw[:, :, :], WS, self.xw_hi[:, :, :],
                                 ALU.mult, ALU.subtract).then_inc(self.x_split, 1)
        dve.wait_ge(self.ctx_loaded, 16)
        dve.wait_ge(self.small_loaded, 16 * self.SMALL)
        st.done(dve.tensor_copy(self.b2parts[:, 0, :], self.b2_raw[:, :]))
        st.done(dve.tensor_tensor(self.b2_rest[:, :], self.b2_raw[:, :], self.b2parts[:, 0, :], ALU.subtract))
        st.done(dve.tensor_copy(self.b2parts[:, 1, :], self.b2_rest[:, :]))
        dve.tensor_tensor(self.b2parts[:, 2, :], self.b2_rest[:, :], self.b2parts[:, 1, :], ALU.subtract)\
            .then_inc(self.b2_split, 1)

    def tensor_setup(self, pe):
        pe.wait_ge(self.consts_ready, 1)
        self.self_tensor(pe)
        pe.wait_ge(self.b1_loaded, 16)
        n = self.E * self.C
        pe.transpose(self.ps[:, 7, 0:n], self.b1_raw[:, :], self.identF[0:n, 0:n]).then_inc(self.b1T_ready, 1)
        pe.wait_ge(self.self_ready, 1)
        pe.wait_ge(self.cleared, 1)
        pe.wait_ge(self.b1_ready, 1)
        pe.wait_ge(self.consts_ready, 2)

    def tensor_later(self, pe):
        pe.wait_ge(self.x_weights_loaded, 16 * 4)
        pe.wait_ge(self.x_split, 1)
        pe.wait_ge(self.b2_split, 1)
        pe.wait_ge(self.cleared, 3)

    def scalar_setup(self, act):
        self.self_scalar(act)
        act.wait_ge(self.b1_ready, 1)
        act.wait_ge(self.cleared, 1)

    def build(self):
        block = self.ctx.enter_context(self.nc.Block())

        @block.sync
        def _(sp):
            self.sync_setup(sp)
            self.experts.sync(sp)

        @block.gpsimd
        def _(pool):
            self.gpsimd_setup(pool)
            self.selfatt.gpsimd(pool)
            pool.wait_ge(self.selfatt.x_done.sem, self.selfatt.x_done.value(self.B, 1))
            pool.wait_ge(self.cleared, 3)
            self.cross.gpsimd(pool)
            pool.wait_ge(self.cross.x_done.sem, self.cross.x_done.value(self.B, 1))
            self.experts.gpsimd(pool)

        @block.vector
        def _(dve):
            self.vector_setup(dve)
            self.selfatt.vector(dve)
            dve.wait_ge(self.selfatt.x_done.sem, self.selfatt.x_done.value(self.B, 1))
            dve.wait_ge(self.x_loaded[1], 16)
            dve.wait_ge(self.cleared, 3)
            self.cross.vector(dve)
            dve.wait_ge(self.cross.x_done.sem, self.cross.x_done.value(self.B, 1))
            dve.wait_ge(self.consts_ready, 6)
            self.experts.vector(dve)

        @block.scalar
        def _(act):
            self.scalar_setup(act)
            self.selfatt.scalar(act)
            act.wait_ge(self.cleared, 3)
            self.cross.scalar(act)
            self.experts.scalar(act)

        @block.tensor
        def _(pe):
            self.tensor_setup(pe)
            self.selfatt.tensor(pe)
            self.tensor_later(pe)
            self.cross.tensor(pe)
            pe.wait_ge(self.consts_ready, 6)
            pe.wait_ge(self.ffn_split.sem, self.ffn_split.value(self.E, 0))
            self.experts.tensor(pe)


def decoder_layer(nc, ap):
    with ExitStack() as ctx:
        Layer(nc, ctx, ap).build()


_OUT = ((16, 256, 128), 'float32')


def rope_table(positions, half, theta=10000.0):
    import numpy as np
    inv = np.float32(1.0) / np.float32(theta) ** (np.arange(half, dtype=np.float32) * np.float32(2.0)
                                                  / np.float32(2 * half))
    ang = np.arange(positions, dtype=np.float32)[:, None] * inv[None, :]
    cos, sin = np.cos(ang), np.sin(ang)
    return np.concatenate([cos, cos, -sin, sin], axis=1)


def kernel(**inputs):
    import numpy as _np
    import concourse.bacc as _bacc
    from concourse import mybir as _mybir
    from concourse.bass_utils import run_bass_kernel_spmd as _run

    nc = _bacc.Bacc("TRN2", target_bir_lowering=False, num_devices=1)
    arrays, ap = {}, {}
    inputs["rope"] = rope_table(inputs["x"].shape[1], 16)
    for name, value in inputs.items():
        a = _np.ascontiguousarray(value)
        arrays[f"in_{name}_dram"] = a
        ap[name] = nc.dram_tensor(f"in_{name}_dram", a.shape, _mybir.dt.from_np(a.dtype), kind="ExternalInput").ap()
    ap["out"] = nc.dram_tensor("out_dram", _OUT[0], _mybir.dt.from_np(_np.dtype(_OUT[1])), kind="ExternalOutput").ap()
    decoder_layer(nc, ap)
    r = _run(nc, [arrays], core_ids=[0])
    return r.results[0]["out_dram"]
```
